# Optimizing a Trainium2 kernel written in Bass

```python
import numpy as np
import jax
import jax.numpy as jnp

def _softmax(x, axis=-1):
    return jax.nn.softmax(x, axis=axis)

def _gelu(x):
    return jax.nn.gelu(x, approximate=True)

def _silu(x):
    return jax.nn.silu(x)

def _sigmoid(x):
    return jax.nn.sigmoid(x)

def _layernorm(x, axis=-1, eps=1e-05):
    m = jnp.mean(x, axis=axis, keepdims=True)
    v = jnp.var(x, axis=axis, keepdims=True)
    return (x - m) / jnp.sqrt(v + eps)

def _scatter_add(tgt, idx, src, axis=0):
    return tgt.at[idx].add(src)

def _segment_sum(src, seg, n):
    return jax.ops.segment_sum(src, seg, n)
kernel_name = 'mk_decoder_postln_d2_seqx_r8_12b9f2'

def setup_inputs(seed: int=0):
    np.random.seed(seed)
    _w = jnp.asarray

    def _rec_inputs():
        import jax
        import jax.numpy as jnp
        _rk = jax.random.key(seed)
        x = -0.0002928 + 1 * jax.random.normal(jax.random.fold_in(_rk, 1), (16, 256, 128), jnp.float32)
        _lenS = 256 - jax.random.randint(jax.random.fold_in(_rk, 7), (16,), 0, max(1, 256 // 4) + 1, jnp.int32)
        _lenS2 = 1601 - jax.random.randint(jax.random.fold_in(_rk, 8), (16,), 0, max(1, 1601 // 4) + 1, jnp.int32)
        _ctx_1024P = jax.random.normal(jax.random.fold_in(_rk, 11), (16, 16, 128), jnp.float32)
        _ctx_1024c = jax.random.dirichlet(jax.random.fold_in(_rk, 511), 0.3 * jnp.ones((16,), jnp.float32), (16, 1601))
        _ctx_1024t = jnp.einsum('bsk,bkd->bsd', _ctx_1024c, _ctx_1024P)
        _ctx_1024t = _ctx_1024t * jax.lax.rsqrt(jnp.mean(jnp.square(_ctx_1024t)) + 1e-12) * 0.953939
        ctx_1024 = -1.39393e-06 + 0.999914 * (_ctx_1024t + 0.3 * jax.random.normal(jax.random.fold_in(_rk, 611), (16, 1601, 128), jnp.float32))
        _validS = jnp.arange(256)[None, :] < _lenS[:, None]
        _validS2 = jnp.arange(1601)[None, :] < _lenS2[:, None]
        _causal = jnp.tril(jnp.ones((256, 256), dtype=bool))
        mask_BxS2_bf0 = jnp.logical_not(jnp.ones((16, 1601), dtype=bool))
        return (x, ctx_1024, mask_BxS2_bf0)
    x, ctx_1024, mask_BxS2_bf0 = _rec_inputs()

    def _L0_attn_setup():
        import jax, jax.numpy as jnp
        import numpy as np
        import math
        D_MODEL = 128
        N_HEADS = 16
        HEAD_DIM = D_MODEL // N_HEADS

        def rotary_embedding(dim, seq_len):
            inv_freq = 1.0 / 10000.0 ** (jnp.arange(0, dim, 2, dtype=jnp.float32) / dim)
            t = jnp.arange(seq_len, dtype=jnp.float32)
            freqs = t[:, None] * inv_freq[None, :]
            return jnp.concatenate((freqs, freqs), axis=-1)

        def apply_rope(x, rope):
            x1 = x[..., ::2]
            x2 = x[..., 1::2]
            ang = rope[..., ::2]
            c, s = (jnp.cos(ang), jnp.sin(ang))
            o1 = x1 * c - x2 * s
            o2 = x1 * s + x2 * c
            return jnp.stack((o1, o2), axis=-1).reshape(x.shape)
        key = jax.random.key(seed)
        ks = jax.random.split(key, 9)
        d = D_MODEL
        sc = 1.0 / math.sqrt(d)
        return {'x': jax.random.normal(ks[0], (2, 256, d), dtype=jnp.float32), 'Wq': jax.random.normal(ks[1], (d, d), dtype=jnp.float32) * sc, 'bq': jax.random.normal(ks[2], (d,), dtype=jnp.float32) * 0.02, 'Wk': jax.random.normal(ks[3], (d, d), dtype=jnp.float32) * sc, 'bk': jax.random.normal(ks[4], (d,), dtype=jnp.float32) * 0.02, 'Wv': jax.random.normal(ks[5], (d, d), dtype=jnp.float32) * sc, 'bv': jax.random.normal(ks[6], (d,), dtype=jnp.float32) * 0.02, 'Wo': jax.random.normal(ks[7], (d, d), dtype=jnp.float32) * sc, 'bo': jax.random.normal(ks[8], (d,), dtype=jnp.float32) * 0.02}
    _L0_attn_all = _L0_attn_setup()
    _L0_attn_in = {k: v for k, v in _L0_attn_all.items() if k in ('Wq', 'bq', 'Wk', 'bk', 'Wv', 'bv', 'Wo', 'bo')}
    del _L0_attn_all

    def _L0_xattn_setup():
        import jax, jax.numpy as jnp
        import numpy as np
        HEADS = 16
        DIM_HEAD = 64
        QUERY_DIM = 128
        CTX_DIM = 128
        INNER = HEADS * DIM_HEAD
        key = jax.random.key(seed)
        ks = jax.random.split(key, 7)
        B, N, M = (2, 256, 256)
        s = 0.02
        return {'x': jax.random.normal(ks[0], (B, N, QUERY_DIM), dtype=jnp.float32), 'context': jax.random.normal(ks[1], (B, M, CTX_DIM), dtype=jnp.float32), 'Wq': jax.random.normal(ks[2], (QUERY_DIM, INNER), dtype=jnp.float32) * s, 'Wk': jax.random.normal(ks[3], (CTX_DIM, INNER), dtype=jnp.float32) * s, 'Wv': jax.random.normal(ks[4], (CTX_DIM, INNER), dtype=jnp.float32) * s, 'Wo': jax.random.normal(ks[5], (INNER, QUERY_DIM), dtype=jnp.float32) * s, 'bo': jnp.zeros((QUERY_DIM,), dtype=jnp.float32)}
    _L0_xattn_all = _L0_xattn_setup()
    _L0_xattn_in = {k: v for k, v in _L0_xattn_all.items() if k in ('Wq', 'Wk', 'Wv', 'Wo', 'bo')}
    del _L0_xattn_all

    def _L0_ffn_setup():
        import jax, jax.numpy as jnp
        import numpy as np
        R = 64
        key = jax.random.key(seed)
        k1, k2, k3 = jax.random.split(key, 3)
        B, S, D_IN, D_OUT = (8, 512, 128, 128)
        x = jax.random.normal(k1, (B, S, D_IN), dtype=jnp.float32)
        weight = jax.random.normal(k2, (D_OUT, D_IN), dtype=jnp.float32) * (1.0 / np.sqrt(D_IN))
        disha = jax.random.normal(k3, (R, D_OUT), dtype=jnp.float32) * 0.01
        return {'x': x, 'weight': weight, 'disha': disha}
    _L0_ffn_all = _L0_ffn_setup()
    _L0_ffn_in = {k: v for k, v in _L0_ffn_all.items() if k in ('weight', 'disha')}
    del _L0_ffn_all

    def _L1_attn_setup():
        import jax, jax.numpy as jnp
        import numpy as np
        EMB = 128
        HEADS = 16
        HEAD_DIM = EMB // HEADS
        B, S = (2, 256)
        key = jax.random.key(seed)
        k1, k2, k3 = jax.random.split(key, 3)
        scale = 0.02
        return {'x': jax.random.normal(k1, (B, S, EMB), dtype=jnp.float32), 'W_qkv': jax.random.normal(k2, (3 * EMB, EMB), dtype=jnp.float32) * scale, 'b_qkv': jnp.zeros((3 * EMB,), dtype=jnp.float32), 'W_out': jax.random.normal(k3, (EMB, EMB), dtype=jnp.float32) * scale, 'b_out': jnp.zeros((EMB,), dtype=jnp.float32)}
    _L1_attn_all = _L1_attn_setup()
    _L1_attn_in = {k: v for k, v in _L1_attn_all.items() if k in ('W_qkv', 'b_qkv', 'W_out', 'b_out')}
    del _L1_attn_all

    def _L1_xattn_setup():
        import jax, jax.numpy as jnp
        import numpy as np
        HEAD = 16
        D_MODEL = 128
        D_HEAD = D_MODEL // HEAD
        key = jax.random.key(seed)
        ks = jax.random.split(key, 9)
        B, NQ, NK = (4, 256, 256)
        s = 1.0 / np.sqrt(D_MODEL)
        return {'queries': jax.random.normal(ks[0], (B, NQ, D_MODEL), jnp.float32), 'keys': jax.random.normal(ks[1], (B, NK, D_MODEL), jnp.float32), 'values': jax.random.normal(ks[2], (B, NK, D_MODEL), jnp.float32), 'attention_mask': jnp.zeros((B, NK), dtype=bool), 'Wq': jax.random.normal(ks[3], (D_MODEL, D_MODEL), jnp.float32) * s, 'bq': jax.random.normal(ks[4], (D_MODEL,), jnp.float32) * s, 'Wk': jax.random.normal(ks[5], (D_MODEL, D_MODEL), jnp.float32) * s, 'bk': jax.random.normal(ks[6], (D_MODEL,), jnp.float32) * s, 'Wv': jax.random.normal(ks[7], (D_MODEL, D_MODEL), jnp.float32) * s, 'bv': jax.random.normal(ks[8], (D_MODEL,), jnp.float32) * s}
    _L1_xattn_all = _L1_xattn_setup()
    _L1_xattn_in = {k: v for k, v in _L1_xattn_all.items() if k in ('Wq', 'bq', 'Wk', 'bk', 'Wv', 'bv')}
    del _L1_xattn_all

    def _L1_ffn_setup():
        import jax, jax.numpy as jnp
        import numpy as np
        B, S, D = (4, 256, 128)
        E, F = (8, 512)
        key = jax.random.key(seed)
        ks = jax.random.split(key, 5)
        x = jax.random.normal(ks[0], (B, S, D), dtype=jnp.float32)
        switch_w = jax.random.normal(ks[1], (D, E), dtype=jnp.float32) * D ** (-0.5)
        switch_b = jnp.zeros((E,), dtype=jnp.float32)
        w1 = jax.random.normal(ks[2], (E, D, F), dtype=jnp.float32) * D ** (-0.5)
        b1 = jnp.zeros((E, F), dtype=jnp.float32)
        w2 = jax.random.normal(ks[3], (E, F, D), dtype=jnp.float32) * F ** (-0.5)
        b2 = jnp.zeros((E, D), dtype=jnp.float32)
        return {'x': x, 'switch_w': switch_w, 'switch_b': switch_b, 'w1': w1, 'b1': b1, 'w2': w2, 'b2': b2}
    _L1_ffn_all = _L1_ffn_setup()
    _L1_ffn_in = {k: v for k, v in _L1_ffn_all.items() if k in ('switch_w', 'switch_b', 'w1', 'b1', 'w2', 'b2')}
    del _L1_ffn_all
    return {'x': x, 'ctx_1024': ctx_1024, 'mask_BxS2_bf0': mask_BxS2_bf0, 'L0_attn_Wq': _L0_attn_in['Wq'], 'L0_attn_bq': _L0_attn_in['bq'], 'L0_attn_Wk': _L0_attn_in['Wk'], 'L0_attn_bk': _L0_attn_in['bk'], 'L0_attn_Wv': _L0_attn_in['Wv'], 'L0_attn_bv': _L0_attn_in['bv'], 'L0_attn_Wo': _L0_attn_in['Wo'], 'L0_attn_bo': _L0_attn_in['bo'], 'L0_xattn_Wq': _L0_xattn_in['Wq'], 'L0_xattn_Wk': _L0_xattn_in['Wk'], 'L0_xattn_Wv': _L0_xattn_in['Wv'], 'L0_xattn_Wo': _L0_xattn_in['Wo'], 'L0_xattn_bo': _L0_xattn_in['bo'], 'L0_ffn_weight': _L0_ffn_in['weight'], 'L0_ffn_disha': _L0_ffn_in['disha'], 'L1_attn_W_qkv': _L1_attn_in['W_qkv'], 'L1_attn_b_qkv': _L1_attn_in['b_qkv'], 'L1_attn_W_out': _L1_attn_in['W_out'], 'L1_attn_b_out': _L1_attn_in['b_out'], 'L1_xattn_Wq': _L1_xattn_in['Wq'], 'L1_xattn_bq': _L1_xattn_in['bq'], 'L1_xattn_Wk': _L1_xattn_in['Wk'], 'L1_xattn_bk': _L1_xattn_in['bk'], 'L1_xattn_Wv': _L1_xattn_in['Wv'], 'L1_xattn_bv': _L1_xattn_in['bv'], 'L1_ffn_switch_w': _L1_ffn_in['switch_w'], 'L1_ffn_switch_b': _L1_ffn_in['switch_b'], 'L1_ffn_w1': _L1_ffn_in['w1'], 'L1_ffn_b1': _L1_ffn_in['b1'], 'L1_ffn_w2': _L1_ffn_in['w2'], 'L1_ffn_b2': _L1_ffn_in['b2']}

def reference(x, ctx_1024, mask_BxS2_bf0, L0_attn_Wq, L0_attn_bq, L0_attn_Wk, L0_attn_bk, L0_attn_Wv, L0_attn_bv, L0_attn_Wo, L0_attn_bo, L0_xattn_Wq, L0_xattn_Wk, L0_xattn_Wv, L0_xattn_Wo, L0_xattn_bo, L0_ffn_weight, L0_ffn_disha, L1_attn_W_qkv, L1_attn_b_qkv, L1_attn_W_out, L1_attn_b_out, L1_xattn_Wq, L1_xattn_bq, L1_xattn_Wk, L1_xattn_bk, L1_xattn_Wv, L1_xattn_bv, L1_ffn_switch_w, L1_ffn_switch_b, L1_ffn_w1, L1_ffn_b1, L1_ffn_w2, L1_ffn_b2):
    import jax
    import jax.numpy as jnp

    def _L0_attn_ref(x, Wq, bq, Wk, bk, Wv, bv, Wo, bo):
        import jax, jax.numpy as jnp
        import numpy as np
        import math
        D_MODEL = 128
        N_HEADS = 16
        HEAD_DIM = D_MODEL // N_HEADS

        def rotary_embedding(dim, seq_len):
            inv_freq = 1.0 / 10000.0 ** (jnp.arange(0, dim, 2, dtype=jnp.float32) / dim)
            t = jnp.arange(seq_len, dtype=jnp.float32)
            freqs = t[:, None] * inv_freq[None, :]
            return jnp.concatenate((freqs, freqs), axis=-1)

        def apply_rope(x, rope):
            x1 = x[..., ::2]
            x2 = x[..., 1::2]
            ang = rope[..., ::2]
            c, s = (jnp.cos(ang), jnp.sin(ang))
            o1 = x1 * c - x2 * s
            o2 = x1 * s + x2 * c
            return jnp.stack((o1, o2), axis=-1).reshape(x.shape)
        B, S, d = x.shape
        H, Dh = (N_HEADS, HEAD_DIM)
        q = (x @ Wq + bq).reshape(B, S, H, Dh).transpose(0, 2, 1, 3)
        k = (x @ Wk + bk).reshape(B, S, H, Dh).transpose(0, 2, 1, 3)
        v = (x @ Wv + bv).reshape(B, S, H, Dh).transpose(0, 2, 1, 3)
        rope = rotary_embedding(Dh, S)
        q = apply_rope(q, rope)
        k = apply_rope(k, rope)
        scores = jnp.einsum('bhqd,bhkd->bhqk', q, k) / math.sqrt(Dh)
        attn = jax.nn.softmax(scores, axis=-1)
        out = jnp.einsum('bhqk,bhkd->bhqd', attn, v)
        out = out.transpose(0, 2, 1, 3).reshape(B, S, d)
        return out @ Wo + bo

    def _L0_xattn_ref(x, context, Wq, Wk, Wv, Wo, bo):
        import jax, jax.numpy as jnp
        import numpy as np
        HEADS = 16
        DIM_HEAD = 64
        QUERY_DIM = 128
        CTX_DIM = 128
        INNER = HEADS * DIM_HEAD
        B, N, _ = x.shape
        M = context.shape[1]
        scale = DIM_HEAD ** (-0.5)
        q = (x @ Wq).reshape(B, N, HEADS, DIM_HEAD).transpose(0, 2, 1, 3)
        k = (context @ Wk).reshape(B, M, HEADS, DIM_HEAD).transpose(0, 2, 1, 3)
        v = (context @ Wv).reshape(B, M, HEADS, DIM_HEAD).transpose(0, 2, 1, 3)
        sim = jnp.einsum('bhid,bhjd->bhij', q, k) * scale
        attn = jax.nn.softmax(sim, axis=-1)
        out = jnp.einsum('bhij,bhjd->bhid', attn, v)
        out = out.transpose(0, 2, 1, 3).reshape(B, N, INNER)
        return out @ Wo + bo

    def _L0_ffn_ref(x, weight, disha):
        import jax, jax.numpy as jnp
        import numpy as np
        R = 64
        result = jnp.einsum('bsd,od->bso', x, weight)
        r = disha.shape[0]
        pooled = x.reshape(*x.shape[:-1], x.shape[-1] // r, r).sum(axis=-2)
        return result + pooled @ disha

    def _L1_attn_ref(x, W_qkv, b_qkv, W_out, b_out):
        import jax, jax.numpy as jnp
        import numpy as np
        EMB = 128
        HEADS = 16
        HEAD_DIM = EMB // HEADS
        B, S = (2, 256)
        b = x.shape[0]
        qkv = jnp.einsum('bse,fe->bsf', x, W_qkv) + b_qkv
        qkv = qkv.reshape(b, HEADS, -1, 3 * HEAD_DIM)
        q, k, v = jnp.split(qkv, 3, axis=-1)
        score = jnp.einsum('bhqd,bhkd->bhqk', q, k) / np.sqrt(HEAD_DIM).astype(np.float32)
        weights = jax.nn.softmax(score, axis=-1)
        context = jnp.einsum('bhqk,bhkd->bhqd', weights, v)
        context = jnp.transpose(context, (0, 2, 1, 3)).reshape(b, -1, EMB)
        out = jnp.einsum('bse,fe->bsf', context, W_out) + b_out
        return out

    def _L1_xattn_ref(queries, keys, values, attention_mask, Wq, bq, Wk, bk, Wv, bv):
        import jax, jax.numpy as jnp
        import numpy as np
        HEAD = 16
        D_MODEL = 128
        D_HEAD = D_MODEL // HEAD
        b_s, nq, _ = queries.shape
        nk = keys.shape[1]
        q = (queries @ Wq.T + bq).reshape(b_s, nq, HEAD, D_HEAD)
        k = (keys @ Wk.T + bk).reshape(b_s, nk, HEAD, D_HEAD)
        v = (values @ Wv.T + bv).reshape(b_s, nk, HEAD, D_HEAD)
        att = jnp.einsum('bqhd,bkhd->bhqk', q, k) / np.sqrt(D_HEAD).astype(jnp.float32)
        att = jax.nn.softmax(att, axis=-1)
        out = jnp.einsum('bhqk,bkhd->bqhd', att, v)
        return out.reshape(b_s, nq, D_MODEL)

    def _L1_ffn_ref(x, switch_w, switch_b, w1, b1, w2, b2):
        import jax, jax.numpy as jnp
        import numpy as np
        B, S, D = (4, 256, 128)
        E, F = (8, 512)
        b, s, d = x.shape
        t = x.reshape(-1, d)
        logits = t @ switch_w + switch_b
        route_prob = jax.nn.softmax(logits, axis=-1)
        route_prob_max = jnp.max(route_prob, axis=-1)
        routes = jnp.argmax(route_prob, axis=-1)
        out = jnp.zeros_like(t)
        n_experts = w1.shape[0]
        for e in range(n_experts):
            h = jax.nn.gelu(t @ w1[e] + b1[e])
            y = h @ w2[e] + b2[e]
            mask = (routes == e)[:, None]
            out = jnp.where(mask, y, out)
        out = out * route_prob_max[:, None]
        return out.reshape(b, s, d)
    x = _layernorm(x + _L0_attn_ref(x, L0_attn_Wq, L0_attn_bq, L0_attn_Wk, L0_attn_bk, L0_attn_Wv, L0_attn_bv, L0_attn_Wo, L0_attn_bo), axis=-1)
    x = _layernorm(x + _L0_xattn_ref(x, ctx_1024, L0_xattn_Wq, L0_xattn_Wk, L0_xattn_Wv, L0_xattn_Wo, L0_xattn_bo), axis=-1)
    x = _layernorm(x + _L0_ffn_ref(x, L0_ffn_weight, L0_ffn_disha), axis=-1)
    x = _layernorm(x + _L1_attn_ref(x, L1_attn_W_qkv, L1_attn_b_qkv, L1_attn_W_out, L1_attn_b_out), axis=-1)
    x = _layernorm(x + _L1_xattn_ref(x, ctx_1024, ctx_1024, mask_BxS2_bf0, L1_xattn_Wq, L1_xattn_bq, L1_xattn_Wk, L1_xattn_bk, L1_xattn_Wv, L1_xattn_bv), axis=-1)
    x = _layernorm(x + _L1_ffn_ref(x, L1_ffn_switch_w, L1_ffn_switch_b, L1_ffn_w1, L1_ffn_b1, L1_ffn_w2, L1_ffn_b2), axis=-1)
    return x

_drawn_inputs = setup_inputs


def setup_inputs(seed=0):
    import zlib

    import numpy as np

    out = dict(_drawn_inputs(seed))
    spreads = {'L0_xattn_bo': (0.0, 0.1),
     'L1_attn_b_qkv': (0.0, 0.39),
     'L1_attn_b_out': (0.0, 0.1),
     'L1_ffn_switch_b': (0.0, 0.1),
     'L1_ffn_b1': (0.0, 0.312),
     'L1_ffn_b2': (0.0, 0.1)}
    factors = {'L0_attn_bq': 7.551,
     'L0_attn_bk': 7.842,
     'L0_xattn_Wq': 8.0,
     'L0_xattn_Wk': 8.0,
     'L1_attn_W_qkv': 5.332,
     'L1_attn_W_out': 3.596,
     'L1_xattn_bk': 8.0}
    for name, (base, spread) in spreads.items():
        noise = np.random.default_rng([zlib.crc32(name.encode()), seed]).standard_normal(out[name].shape)
        drawn = base * np.exp(spread * noise) if base else spread * noise
        out[name] = jnp.asarray(drawn.astype(out[name].dtype))
    for name, factor in factors.items():
        out[name] = (out[name] * factor).astype(out[name].dtype)
    return out
```

```python
from contextlib import ExitStack

import numpy as np

import concourse.bass as bass
from concourse import mybir

F32 = mybir.dt.float32
F16 = mybir.dt.float16
ALU = mybir.AluOpType
ACT = mybir.ActivationFunctionType
AX = mybir.AxisListType

NB, S, D, NKC = 16, 256, 128, 1601
QT = S // 128
H, DH, NG, HG = 16, 8, 4, 4
SLOT = 32
M_ROW = 24
EPS = 1e-5
BANK = 512


def due(value):
    return not isinstance(value, int) or value > 0


class UseOrder:

    def __init__(self, prologue, first, body, last, post):
        self.lists = prologue, first, body, last, post

    def no(self, b, use):
        prologue, first, body, last, post = self.lists
        if isinstance(b, int):
            if b == -1:
                return prologue.index(use)
            if b == 0:
                return len(prologue) + first.index(use)
            if b == NB - 1:
                return len(prologue) + len(first) + (NB - 2) * len(body) + last.index(use)
            if b == NB:
                return len(prologue) + len(first) + (NB - 2) * len(body) + len(last) + post.index(use)
        return b * len(body) + (len(prologue) + len(first) - len(body) + body.index(use))


def over_batches(eng, body):
    body(0, 0, 0, True, False)
    body(1, 0, 1, False, False)
    with eng.Fori(1, NB // 2 - 1) as i:
        for par in range(2):
            body(i * 2 + par, i, par, False, False)
    body(NB - 2, NB // 2 - 1, 0, False, False)
    body(NB - 1, NB // 2 - 1, 1, False, True)


def spread(others, chunks):
    out, n, m = [], len(others), len(chunks)
    for i in range(max(n, 1)):
        out += others[i:i + 1]
        out += chunks[i * m // max(n, 1):(i + 1) * m // max(n, 1)]
    return out


def tokens(x, b):
    return x[bass.ds(b, 1)].rearrange("o (t p) d -> p (o t) d", p=128)


def layer_norm_stats(nc, dve, y, stats, mv, ve):
    for t in range(QT):
        nc.vector.bn_stats(stats[:, t, :], y[:, t, :])
    dve.drain()
    for t in range(QT):
        nc.vector.bn_aggr(mv[:, t, :], stats[:, t, :])
    dve.drain()
    return nc.vector.tensor_scalar(ve[:], mv[:, :, 1], EPS, None, ALU.add)


def attention8(nc, kind, x_src, x_dst, w, ps, ident, ident16, minus_half, ctx=None):
    psA, psB, psO, psM = ps
    cross, rope, chunked = kind == "cross", kind == "rope", kind == "chunked"
    NK = NKC if cross else S
    KT = -(-NK // 128)
    kn = [min(128, NK - 128 * k) for k in range(KT)]
    SCALE = float(DH) ** -0.5
    cuts = [NK * c // 4 for c in range(5)]
    CA = HG * QT * 4 if cross else HG
    kcuts = list(range(0, NK, BANK)) + [NK]

    if cross:
        set_x, set_g = [("X",)] + [("C", i) for i in range(4)], [[("Q", g)] + [("K", g, c) for c in range(4)] for g in range(NG)]
        v_uses = [("V", i) for i in range(4)]
        setups = [set_x + set_g[0], set_g[1], v_uses[:2] + set_g[2], v_uses[2:] + set_g[3]]
    elif rope:
        setups = [[("X",), ("Q", 0), ("K", 0)], [("Q", 1), ("K", 1)], [("V",), ("Q", 2), ("K", 2)], [("Q", 3), ("K", 3)]]
    else:
        setups = [[("X",), ("Q", 0), ("Q", 1), ("K", 0), ("K", 1)], [("V", 0), ("V", 1)], [("T", 0), ("T", 1)], []]
    ends = [[], [("EL",)], [], [("EN",)]] if cross else [[], [("EO",)], [("EW",)], [("EN",)]]
    NO_BANK = ("EL", "EN", "A")

    def units(g, first, last):
        u = [] if first else list(ends[g])
        u += [] if first and g == 0 else [("FG", g)]
        u += [] if last and g == 3 else [("MT", g)]
        u += [] if last else setups[g]
        return spread(u, [] if last and g >= 2 else [("A", g, c) for c in range(CA)])

    def bank_uses(us):
        return [u for u in us if u[0] not in NO_BANK]

    def of_body(first, last):
        return bank_uses([u for g in range(NG) for u in units(g, first, last)])

    prologue = [u for s in setups for u in s]
    post = [("FG", 0)] + [u for e in ends for u in e]
    order = UseOrder(prologue + [("MT", 3)], of_body(True, False), of_body(False, False), of_body(False, True), bank_uses(post))
    ready_use = {g: (("K", g, 3) if cross else ("K", g) if rope else ("K", 1)) for g in range(NG)}
    v_use = ("V", 3) if cross else ("V",) if rope else ("T", 1)

    def share(us, kt):
        n = len(us)
        return us[n * kt // KT:n * (kt + 1) // KT]

    with ExitStack() as c:
        def sb(name, shape, dt=F32):
            return c.enter_context(nc.sbuf_tensor(f"{kind}_{name}", shape, dt))

        def sem(name):
            return c.enter_context(nc.semaphore(f"{kind}_{name}"))

        def loaded(name, src):
            t = sb(name, list(src.shape))
            loads.append((t, src))
            return t

        loads = []
        if rope:
            wq, wk, wqs, wks = (loaded(n, w[n]) for n in ("wq", "wk", "wqs", "wks"))
            bq, bk, bqs, bks = (loaded(n, w[n]) for n in ("bq", "bk", "bqs", "bks"))
            cos, sin = loaded("cos", w["cos"]), loaded("sin", w["sin"])
        else:
            wq, wk, bq, bk = (loaded(n, w[n]) for n in ("wq", "wk", "bq", "bk"))
        wv, bv = loaded("wv", w["wv"]), loaded("bv", w["bv"])
        lo = loaded("lo", w["lo"])
        if not cross:
            wo, bo = loaded("wo", w["wo"]), loaded("bo", w["bo"])

        x_in = sb("x_in", [128, 2, QT, 128])
        x_res = sb("x_res", [128, 2, QT, 128])
        x_out = sb("x_out", [128, 2, QT, 128])
        xT = sb("xT", [128, S])
        KO = sb("KO", [128, 2, NG, NK], F16)
        QZ = sb("QZ", [128, 2, H, S], F16)
        VA = sb("VA", [128, 2, KT, H, SLOT])
        P = sb("P", [128, 4, HG, S])
        MX = sb("MX", [128, QT, 128], F16)
        mfull = sb("mfull", [128, QT, HG])
        mpart = sb("mpart", [128, QT, HG, 4])
        hi = sb("hi", [128, BANK], F16)
        oT = sb("oT", [128, S])
        O = sb("O", [128, QT, 128])
        rsum = sb("rsum", [128, QT, HG])
        y = sb("y", [128, QT, 128])
        stats = sb("stats", [128, QT, 6])
        mv = sb("mv", [128, QT, 2])
        ve = sb("ve", [128, QT])
        rstd = sb("rstd", [128, QT])
        if not cross:
            OT = sb("OT", [128, S])
        if rope:
            rot = sb("rot", [128, 3, S])
        if cross:
            ctx_in = sb("ctx_in", [128, 2, KT, 128])
            cT = sb("cT", [128, NK])
            lob = sb("lob", [128, NG])
        if chunked:
            xs = sb("xs", [128, BANK])
            VT = sb("VT", [128, NG, S])

        w_ld, init = sem("weights_loaded"), sem("initialised")
        x_ld = [sem(f"x_loaded{i}") for i in range(2)]
        xr_ld = [sem(f"residual_loaded{i}") for i in range(2)]
        c_ld = [sem(f"context_loaded{i}") for i in range(2)]
        st_done = [sem(f"stored{i}") for i in range(2)]
        m_full, m_free = sem("bank_full"), sem("bank_free")
        s_full, s_free = sem("scores_full"), sem("scores_maxed")
        t_full, e_done, pv_done = sem("scoresT_full"), sem("exp_done"), sem("pv_done")
        op_ready = sem("operand_ready")
        mx_ready, hi_ready, ot_ready = sem("max_ready"), sem("high_ready"), sem("oT_ready")
        xr_used, ve_ready, rstd_ready, y_ready = sem("residual_used"), sem("var_ready"), sem("rstd_ready"), sem("out_ready")

        with nc.Block() as block:
            @block.sync
            def _(sp):
                for t, src in loads:
                    sp.dma_start(t[:], src).then_inc(w_ld, 16)
                sp.wait_ge(w_ld, 16 * len(loads))

            @block.vector
            def _(dve):
                nc.vector.memset(QZ[:], 0.0)
                nc.vector.memset(MX[:], 0.0)
                nc.vector.memset(VA[:], 0.0)
                dve.drain()
                nc.vector.memset(VA[:, :, :, :, DH:DH + 1], 1.0)
                if cross:
                    dve.wait_ge(w_ld, 16 * len(loads))
                    nc.vector.tensor_scalar(lob[:], bk[:], lo[:, 0:1], None, ALU.mult)

        with nc.Block() as block:
            @block.sync
            def _(sp):
                def load(b, par):
                    sp.dma_start(x_in[:, par], tokens(x_src, b)).then_inc(x_ld[par], 16)

                def load_ctx(b, par):
                    src = ctx[bass.ds(b, 1)]
                    full = (KT - 1) * 128
                    sp.dma_start(ctx_in[:, par, 0:KT - 1, :],
                                 src[:, 0:full].rearrange("o (k p) d -> p (o k) d", p=128)).then_inc(c_ld[par], 16)
                    sp.dma_start(ctx_in[0:kn[-1], par, KT - 1, :],
                                 src[:, full:NK].rearrange("o p d -> p (o d)")).then_inc(c_ld[par], 16)

                def load_res(b, par):
                    sp.dma_start(x_res[:, par], tokens(x_src, b)).then_inc(xr_ld[par], 16)

                for b in range(2):
                    load(b, b)
                    if cross:
                        load_ctx(b, b)
                    load_res(b, b)

                def store(b, par):
                    sp.wait_ge(y_ready, b + 1)
                    sp.dma_start(tokens(x_dst, b), x_out[:, par]).then_inc(st_done[par], 16)

                def body(b, it, par, first, last):
                    if not (isinstance(b, int) and b >= NB - 2):
                        setup_b = b - 1
                        sp.wait_ge(m_free, order.no(setup_b, ("C", 3) if cross else ("X",)) + 1)
                        load(b + 2, par)
                        if cross:
                            load_ctx(b + 2, par)
                    if not first:
                        store(b - 1, 1 - par)
                        if not last:
                            if due(b):
                                sp.wait_ge(xr_used, b)
                            load_res(b + 1, 1 - par)

                over_batches(sp, body)
                store(NB - 1, 1)
                sp.wait_ge(st_done[0], 16 * NB // 2)
                sp.wait_ge(st_done[1], 16 * NB // 2)

            @block.tensor
            def _(pe):
                def begin(b, u):
                    if due(order.no(b, u)):
                        pe.wait_ge(m_free, order.no(b, u))

                def setup(b, bs, its, par, u):
                    begin(b, u)
                    if u[0] == "X":
                        pe.wait_ge(x_ld[par], its * 16 + 16)
                        for t in range(QT):
                            last = nc.tensor.transpose(psM[:, t * 128:t * 128 + 128], x_in[:, par, t, :], ident[:])
                    elif u[0] == "C":
                        if u[1] == 0:
                            pe.wait_ge(c_ld[par], its * 32 + 32)
                        for i, k in enumerate(range(4 * u[1], min(4 * u[1] + 4, KT))):
                            last = nc.tensor.transpose(psM[:, i * 128:i * 128 + kn[k]], ctx_in[0:kn[k], par, k, :],
                                                       ident[0:kn[k], 0:kn[k]])
                    elif rope and u[0] in "QK":
                        for i, m in enumerate((wq, wqs) if u[0] == "Q" else (wk, wks)):
                            last = nc.tensor.matmul(psM[:, i * S:i * S + S], m[:, u[1] * 128:u[1] * 128 + 128], xT[:],
                                                    start=True, stop=True, skip_group_check=True)
                    elif rope and u[0] == "V":
                        for t in range(QT):
                            last = nc.tensor.matmul(psM[:, t * 128:t * 128 + 128], xT[:, t * 128:t * 128 + 128], wv[:],
                                                    start=True, stop=True, skip_group_check=True)
                    elif chunked and u[0] in "QKV":
                        m = {"Q": wq, "K": wk, "V": wv}[u[0]]
                        for i in range(8):
                            for j in range(HG):
                                last = nc.tensor.matmul(psM[j * SLOT:(j + 1) * SLOT, i * 64:i * 64 + 64],
                                                        m[:, (8 * u[1] + i) * SLOT:(8 * u[1] + i + 1) * SLOT],
                                                        xT[:, j * 64:j * 64 + 64], start=True, stop=True, skip_group_check=True)
                    elif u[0] == "T":
                        pe.wait_ge(op_ready, bs * 6 + 6)
                        for g in range(NG):
                            last = nc.tensor.transpose(psM[:, g * 128:g * 128 + 128], VT[:, g, u[1] * 128:u[1] * 128 + 128], ident[:])
                    elif u[0] == "Q":
                        last = nc.tensor.matmul(psM[:, 0:S], wq[:, u[1] * 128:u[1] * 128 + 128], xT[:],
                                                start=True, stop=True, skip_group_check=True)
                    elif u[0] == "K":
                        a, z = kcuts[u[2]], kcuts[u[2] + 1]
                        last = nc.tensor.matmul(psM[:, 0:z - a], wk[:, u[1] * 128:u[1] * 128 + 128], cT[:, a:z],
                                                start=True, stop=True, skip_group_check=True)
                    elif u[0] == "V":
                        for i, k in enumerate(range(4 * u[1], min(4 * u[1] + 4, KT))):
                            last = nc.tensor.matmul(psM[0:kn[k], i * 128:i * 128 + 128], cT[:, k * 128:k * 128 + kn[k]], wv[:],
                                                    start=True, stop=True, skip_group_check=True)
                    last.then_inc(m_full, 1)

                def scores(G, g, par, ch, setup_at):
                    n = G * CA + ch
                    if ch == 0 and chunked:
                        pe.wait_ge(op_ready, (setup_at + 1) * 6 + 4)
                    elif ch == 0:
                        pe.wait_ge(m_free, order.no(setup_at, ready_use[g]) + 1)
                    if due(n - 1):
                        pe.wait_ge(s_free, n - 1)
                    out = psA[:, ch % 2]
                    if cross:
                        j, t, k = ch // 8, ch // 4 % 2, ch % 4
                        a, z = cuts[k], cuts[k + 1]
                        last = nc.tensor.matmul(out[:, 0:z - a], QZ[:, par, 4 * g + j, t * 128:t * 128 + 128], KO[:, par, g, a:z],
                                                start=True, stop=True, skip_group_check=True)
                    else:
                        for t in range(QT):
                            last = nc.tensor.matmul(out[:, t * S:t * S + S], QZ[:, par, 4 * g + ch, t * 128:t * 128 + 128],
                                                    KO[:, par, g, :], start=True, stop=True, skip_group_check=True)
                    last.then_inc(s_full, 1)

                def max_rows(b, G, u):
                    pe.wait_ge(mx_ready, G + 1)
                    begin(b, u)
                    for t in range(QT):
                        last = nc.tensor.transpose(psM[:, t * 64:t * 64 + 64].bitcast(F16), MX[:, t, :], ident16[:])
                    last.then_inc(m_full, 1)

                def scoresT(b, G, g, par, kt):
                    n = G * KT + kt
                    if kt == 0:
                        pe.wait_ge(m_free, order.no(b if g else b - 1, ("MT", (g - 1) % 4)) + 1)
                    if due(n - 1):
                        pe.wait_ge(e_done, n - 1)
                    out = psB[0:kn[kt], (g * KT + kt) % 2]
                    for i in range(2):
                        last = nc.tensor.matmul(out[:, i * BANK:(i + 1) * BANK], KO[:, par, g, kt * 128:kt * 128 + kn[kt]],
                                                QZ[:, par, 4 * g + 2 * i:4 * g + 2 * i + 2, :],
                                                start=True, stop=True, skip_group_check=True)
                    last.then_inc(t_full, 1)

                def weigh(b, G, g, par, kt):
                    n = G * KT + kt
                    if kt == 0:
                        if due(G):
                            pe.wait_ge(ot_ready, G)
                        if g == 0:
                            pe.wait_ge(m_free, order.no(b - 1, v_use) + 1)
                    pe.wait_ge(e_done, n + 1)
                    for j in range(HG):
                        last = nc.tensor.matmul(psO[j * SLOT:(j + 1) * SLOT, 0:S],
                                                VA[0:kn[kt], par, kt, 4 * g + j, :], P[0:kn[kt], (g * KT + kt) % 4, j, :],
                                                start=(kt == 0), stop=(kt == KT - 1), skip_group_check=True)
                    last.then_inc(pv_done, 1)

                def end(b, be, G, u):
                    if u[0] == "FG":
                        pe.wait_ge(ot_ready, G + 1)
                        begin(b, u)
                        for t in range(QT):
                            last = nc.tensor.transpose(psM[:, t * 128:t * 128 + 128], oT[:, t * 128:t * 128 + 128], ident[:])
                        last.then_inc(m_full, 1)
                    elif u[0] == "EO":
                        begin(b, u)
                        for t in range(QT):
                            last = nc.tensor.transpose(psM[:, t * 128:t * 128 + 128], O[:, t, :], ident[:])
                        last.then_inc(m_full, 1)
                    elif u[0] == "EW":
                        begin(b, u)
                        for t in range(QT):
                            last = nc.tensor.matmul(psM[:, t * 128:t * 128 + 128], OT[:, t * 128:t * 128 + 128], wo[:],
                                                    start=True, stop=True, skip_group_check=True)
                        last.then_inc(m_full, 1)

                def unit(b, it, par, u, g):
                    if u[0] == "A":
                        far = g >= 2
                        scores(b * 4 + g + 2, (g + 2) % 4, 1 - par if far else par, u[2], b if far else b - 1)
                    elif u[0] == "MT":
                        max_rows(b, b * 4 + g + 1, u)
                    elif u[0] in ("FG", "EO", "EW"):
                        end(b, b - 1, b * 4 + g - 1, u)
                    elif u[0] not in NO_BANK:
                        setup(b, b + 1, it + par, 1 - par, u)

                for u in prologue:
                    setup(-1, 0, 0, 0, u)
                for ch in range(CA):
                    scores(0, 0, 0, ch, -1)
                max_rows(-1, 0, ("MT", 3))
                for ch in range(CA):
                    scores(1, 1, 0, ch, -1)

                def body(b, it, par, first, last):
                    for g in range(NG):
                        us = units(g, first, last)
                        for kt in range(KT):
                            scoresT(b, b * 4 + g, g, par, kt)
                            if kt:
                                weigh(b, b * 4 + g, g, par, kt - 1)
                            for u in share(us, kt):
                                unit(b, it, par, u, g)
                        weigh(b, b * 4 + g, g, par, KT - 1)

                over_batches(pe, body)
                for u in post:
                    end(NB, NB - 1, NB * 4 - 1, u)

            @block.scalar
            def _(act):
                def take(b, u):
                    act.wait_ge(m_full, order.no(b, u) + 1)

                def exps(G, g, kt):
                    n = G * KT + kt
                    act.wait_ge(t_full, n + 1)
                    if due(n - 3):
                        act.wait_ge(pv_done, n - 3)
                    r = (g * KT + kt)
                    nc.scalar.activation(P[0:kn[kt], r % 4, :, :].rearrange("p j q -> p (j q)"), psB[0:kn[kt], r % 2],
                                         ACT.Exp, scale=SCALE).then_inc(e_done, 1)

                def copy_out(b, G, g):
                    if due(G * KT):
                        act.wait_ge(pv_done, G * KT)
                    if not (isinstance(b, int) and b == 0 and g == 1):
                        act.wait_ge(m_full, order.no(b if g else b - 1, ("FG", (g - 1) % 4)) + 1)
                    nc.scalar.activation(oT[:], psO[:, 0:S], ACT.Copy).then_inc(ot_ready, 1)

                def unit(b, be, G, u):
                    if u[0] == "X":
                        take(b, u)
                        if chunked:
                            nc.scalar.activation(xT[:].rearrange("d (j g t) -> d g j t", j=HG, g=NG),
                                                 psM[:, 0:S].rearrange("d (g j t) -> d g j t", j=HG, g=NG),
                                                 ACT.Copy).then_inc(m_free, 1)
                        else:
                            nc.scalar.activation(xT[:], psM[:, 0:S], ACT.Copy).then_inc(m_free, 1)
                    elif u[0] == "C":
                        take(b, u)
                        a, z = kcuts[u[1]], kcuts[u[1] + 1]
                        nc.scalar.activation(cT[:, a:z], psM[:, 0:z - a], ACT.Copy).then_inc(m_free, 1)
                    elif u[0] == "K" and cross:
                        take(b, u)
                        a, z = kcuts[u[2]], kcuts[u[2] + 1]
                        nc.scalar.activation(hi[:, 0:z - a], psM[:, 0:z - a], ACT.Identity, scale=lo[:, 0:1],
                                             bias=lob[:, u[1]:u[1] + 1]).then_inc(hi_ready, 1)
                    elif u[0] == "T":
                        take(b, u)
                        nc.scalar.activation(VA[:, parity[0], u[1]].rearrange("k h s -> k (h s)"), psM[:, :],
                                             ACT.Copy).then_inc(m_free, 1)
                    elif u[0] == "EO":
                        take(b, u)
                        nc.scalar.activation(OT[:], psM[:, 0:S], ACT.Copy).then_inc(m_free, 1)

                parity = [0]
                for u in prologue:
                    unit(-1, 0, 0, u)

                def body(b, it, par, first, last):
                    parity[0] = 1 - par
                    for g in range(NG):
                        us = units(g, first, last)
                        for kt in range(KT):
                            exps(b * 4 + g, g, kt)
                            if kt == 0 and not (first and g == 0):
                                copy_out(b, b * 4 + g, g)
                            for u in share(us, kt):
                                unit(b, b - 1, b * 4 + g - 1, u)

                over_batches(act, body)
                copy_out(NB, NB * 4, 0)
                for u in post:
                    unit(NB, NB - 1, NB * 4 - 1, u)

            @block.gpsimd
            def _(pool):
                def body(b, it, par, first, last):
                    pool.wait_ge(ve_ready, b + 1)
                    nc.gpsimd.tensor_tensor(rstd[:], ve[:], minus_half[:, 0:QT], ALU.pow).then_inc(rstd_ready, 1)
                over_batches(pool, body)

            @block.vector
            def _(dve):
                def take(b, u):
                    dve.wait_ge(m_full, order.no(b, u) + 1)

                def setup(b, par, u):
                    if u[0] == "Q" and not chunked or u[0] == "K" and rope:
                        take(b, u)
                        g, isk = u[1], u[0] == "K"
                        if rope:
                            bias, biass = (bk, bks) if isk else (bq, bqs)
                            nc.vector.scalar_tensor_tensor(out=rot[:, 0], in0=psM[:, 0:S], scalar=bias[:, g:g + 1], in1=cos[:],
                                                           op0=ALU.add, op1=ALU.mult)
                            nc.vector.scalar_tensor_tensor(out=rot[:, 1], in0=psM[:, S:2 * S], scalar=biass[:, g:g + 1],
                                                           in1=sin[:], op0=ALU.add, op1=ALU.mult)
                            dve.drain()
                            nc.vector.tensor_tensor(rot[:, 2], rot[:, 0], rot[:, 1], ALU.add)
                            dve.drain()
                            col = 0 if isk else 1
                            nc.vector.tensor_scalar(hi[:, 0:S], rot[:, 2], lo[:, col:col + 1], None, ALU.mult)
                            dve.drain()
                            if isk:
                                nc.vector.tensor_tensor(KO[:, par, g, :], rot[:, 2], hi[:, 0:S], ALU.subtract).then_inc(m_free, 1)
                            else:
                                for j in range(HG):
                                    r = slice(j * SLOT, (j + 1) * SLOT)
                                    last = nc.vector.tensor_tensor(QZ[r, par, 4 * g + j, :], rot[r, 2], hi[r, 0:S], ALU.subtract)
                                dve.drain().then_inc(m_free, 1)
                        else:
                            nc.vector.tensor_scalar(hi2[:, 0:S], psM[:, 0:S], bq[:, g:g + 1], lo[:, 1:2], ALU.add, ALU.mult)
                            dve.drain()
                            for j in range(HG):
                                r = slice(j * SLOT, (j + 1) * SLOT)
                                nc.vector.scalar_tensor_tensor(out=QZ[r, par, 4 * g + j, :], in0=psM[r, 0:S],
                                                               scalar=bq[r, g:g + 1], in1=hi2[r, 0:S],
                                                               op0=ALU.add, op1=ALU.subtract)
                            dve.drain().then_inc(m_free, 1)
                    elif u[0] == "K" and cross:
                        take(b, u)
                        dve.wait_ge(hi_ready, hi_no(b, u) + 1)
                        a, z = kcuts[u[2]], kcuts[u[2] + 1]
                        nc.vector.scalar_tensor_tensor(out=KO[:, par, u[1], a:z], in0=psM[:, 0:z - a],
                                                       scalar=bk[:, u[1]:u[1] + 1], in1=hi[:, 0:z - a],
                                                       op0=ALU.add, op1=ALU.subtract).then_inc(m_free, 1)
                    elif u[0] in "QKV" and chunked:
                        take(b, u)
                        bias = {"Q": bq, "K": bk, "V": bv}[u[0]]
                        cs = slice(8 * u[1], 8 * u[1] + 8)
                        cgt = "r (c g t) -> r c g t"
                        vals = psM[:, :].rearrange("r (c q) -> r c q", c=8)
                        b_ = bias[:, cs].unsqueeze(2).to_broadcast([128, 8, 64])
                        nc.vector.tensor_tensor(xs[:].rearrange("r (c q) -> r c q", c=8), vals, b_, ALU.add)
                        dve.drain().then_inc(m_free, 1)
                        if u[0] != "V":
                            col = 0 if u[0] == "K" else 1
                            nc.vector.tensor_scalar(hi[:], xs[:], lo[:, col:col + 1], None, ALU.mult)
                            dve.drain()
                        x_ = xs[:].rearrange(cgt, c=8, g=NG)
                        h_ = hi[:].rearrange(cgt, c=8, g=NG)
                        if u[0] == "V":
                            nc.vector.tensor_copy(VT[:].rearrange("r g (t c) -> r c g t", c=16)[:, cs], x_)
                        elif u[0] == "K":
                            nc.vector.tensor_tensor(KO[:, par].rearrange("r g (t c) -> r c g t", c=16)[:, cs], x_, h_, ALU.subtract)
                        else:
                            for j in range(HG):
                                r = slice(j * SLOT, (j + 1) * SLOT)
                                nc.vector.tensor_tensor(
                                    QZ[r, par].rearrange("r (g j) (t c) -> r c g j t", j=HG, c=16)[:, cs, :, j, :],
                                    x_[r], h_[r], ALU.subtract)
                        dve.drain().then_inc(op_ready, 1)
                    elif u[0] == "V" and not chunked:
                        take(b, u)
                        if rope:
                            nc.vector.tensor_tensor(VA[:, par].rearrange("k t h s -> k (t h) s")[:, :, 0:DH],
                                                    psM[:, 0:QT * 128].rearrange("k (a s) -> k a s", s=DH),
                                                    bv[:].rearrange("k (a s) -> k a s", s=DH), ALU.add).then_inc(m_free, 1)
                        else:
                            ks = range(4 * u[1], min(4 * u[1] + 4, KT))
                            n, r = len(ks), kn[ks[-1]]
                            nc.vector.tensor_tensor(
                                VA[0:r, par, ks[0]:ks[-1] + 1].rearrange("k t h s -> k (t h) s")[:, :, 0:DH],
                                psM[0:r, 0:n * 128].rearrange("k (a s) -> k a s", s=DH),
                                bv[0:r, 0:n * 128].rearrange("k (a s) -> k a s", s=DH), ALU.add).then_inc(m_free, 1)

                def hi_no(b, u):
                    at = [x for x in prologue if x[0] == "K"].index(u)
                    return (b + 1) * 16 + at

                def maxima(G, ch):
                    n = G * CA + ch
                    if ch == 0:
                        if due(G):
                            dve.wait_ge(mx_ready, G)
                    dve.wait_ge(s_full, n + 1)
                    if cross:
                        j, t, k = ch // 8, ch // 4 % 2, ch % 4
                        nc.vector.tensor_reduce(mpart[:, t, j, k:k + 1], psA[:, ch % 2, 0:cuts[k + 1] - cuts[k]],
                                                AX.X, ALU.max).then_inc(s_free, 1)
                    else:
                        nc.vector.tensor_reduce(mfull[:, :, ch], psA[:, ch % 2].rearrange("p (t k) -> p t k", t=QT),
                                                AX.X, ALU.max).then_inc(s_free, 1)
                    if ch == CA - 1:
                        if cross:
                            dve.drain()
                            nc.vector.tensor_reduce(mfull[:], mpart[:], AX.X, ALU.max)
                        cols = MX[:].rearrange("p t (j s) -> p t j s", s=SLOT)
                        dve.drain()
                        nc.vector.tensor_scalar(cols[:, :, :, M_ROW], mfull[:], -1.0, None, ALU.mult)
                        dve.drain()
                        nc.vector.scalar_tensor_tensor(out=cols[:, :, :, M_ROW + 1], in0=mfull[:], scalar=-1.0,
                                                       in1=cols[:, :, :, M_ROW], op0=ALU.mult,
                                                       op1=ALU.subtract).then_inc(mx_ready, 1)

                def add_max(b, g, par, u):
                    take(b, u)
                    for j in range(HG):
                        r = slice(j * SLOT, (j + 1) * SLOT)
                        nc.vector.tensor_tensor(QZ[r, par, 4 * g + j, :], psM[r, 0:S // 2].bitcast(F16),
                                                QZ[r, par, 4 * g + j, :], ALU.add)
                    dve.drain().then_inc(m_free, 1)

                def end(b, be, G, gg, it, par, u):
                    if u[0] == "FG":
                        take(b, u)
                        rows = psM[:, 0:S].rearrange("p (t j s) -> p t j s", t=QT, j=HG)
                        nc.vector.reciprocal(rsum[:], rows[:, :, :, DH])
                        dve.drain()
                        for t in range(QT):
                            last = nc.vector.tensor_tensor(
                                O[:, t, gg * 32:gg * 32 + 32].rearrange("p (j d) -> p j d", j=HG), rows[:, t, :, 0:DH],
                                rsum[:, t, :].unsqueeze(2).to_broadcast([128, HG, DH]), ALU.mult)
                        dve.drain().then_inc(m_free, 1)
                    elif u[0] in ("EW", "EL"):
                        dve.wait_ge(xr_ld[par], it * 16 + 16)
                        if u[0] == "EW":
                            take(b, u)
                            nc.vector.tensor_tensor(y[:], psM[:, 0:S].rearrange("p (t d) -> p t d", t=QT), bo[:], ALU.add)
                            dve.drain().then_inc(m_free, 1)
                            nc.vector.tensor_tensor(y[:], y[:], x_res[:, par], ALU.add)
                        else:
                            nc.vector.tensor_tensor(y[:], O[:], x_res[:, par], ALU.add)
                        dve.drain().then_inc(xr_used, 1)
                        layer_norm_stats(nc, dve, y, stats, mv, ve).then_inc(ve_ready, 1)
                    elif u[0] == "EN":
                        dve.wait_ge(rstd_ready, be + 1)
                        if due(it * 16):
                            dve.wait_ge(st_done[par], it * 16)
                        for t in range(QT):
                            nc.vector.tensor_scalar(x_out[:, par, t, :], y[:, t, :], mv[:, t, 0:1], rstd[:, t:t + 1],
                                                    ALU.subtract, ALU.mult)
                        dve.drain().then_inc(y_ready, 1)

                hi2 = sb("hi2", [128, S], F16) if cross else None
                for u in prologue:
                    setup(-1, 0, u)
                for ch in range(CA):
                    maxima(0, ch)
                add_max(-1, 0, 0, ("MT", 3))
                for ch in range(CA):
                    maxima(1, ch)

                def body(b, it, par, first, last):
                    for g in range(NG):
                        for u in units(g, first, last):
                            if u[0] == "A":
                                maxima(b * 4 + g + 2, u[2])
                            elif u[0] == "MT":
                                add_max(b, (g + 1) % 4, 1 - par if g == 3 else par, u)
                            elif u[0] in ("FG", "EW", "EL", "EN"):
                                end(b, b - 1, b * 4 + g - 1, (g - 1) % 4, it - 1 + par, 1 - par, u)
                            elif u[0] != "EO":
                                setup(b, 1 - par, u)

                over_batches(dve, body)
                for u in post:
                    end(NB, NB - 1, NB * 4 - 1, 3, NB // 2 - 1, 1, u)


def cross64(nc, x_src, x_dst, w, ps, ident, ident16, minus_half, ctx):
    psA, psB, psO, psM = ps
    NK, DQ, NP, HB = NKC, 64, 8, 2
    KT = -(-NK // 128)
    kn = [min(128, NK - 128 * k) for k in range(KT)]
    NC = -(-KT // 2)
    SCALE = float(DQ) ** -0.5
    cuts = [NK * c // 4 for c in range(5)]
    CA = HB * QT * 4
    kcuts = list(range(0, NK, BANK)) + [NK]
    VS = [[0, 4, 7, 10, 13], [0, 5, 9, 13]]

    xc = [("X",)] + [("C", i) for i in range(4)]
    kq = [[("Q", p)] + [("K", p, c) for c in range(4)] for p in range(NP)]
    v1 = [[("V", 1, k) for k in range(VS[0][i], VS[0][i + 1])] for i in range(4)]
    v0 = [[("V", 0, k) for k in range(VS[1][i], VS[1][i + 1])] for i in range(3)]
    ends = [[], [("EW",)], [], [("EN",)], [("FT",)], [("FW",)], [], [("FN",)]]
    NO_BANK = ("EN", "FN", "A", "C2")

    def units(p, first, last):
        u = [] if last and p == 7 else [("MT", p), ("C2", p)]
        u += [] if first else ends[p]
        if p < 4:
            u += v1[p]
        elif p >= 5 and not last:
            u += (xc if p == 5 else []) + v0[p - 5]
        if not (last and p >= 5):
            u += kq[(p + 3) % 8]
        if not (first and p == 0):
            u.insert(len(u) * 2 // 3, ("FG", p))
        return spread(u, [] if last and p >= 6 else [("A", p, c) for c in range(CA)])

    def bank_uses(us):
        return [u for u in us if u[0] not in NO_BANK]

    def of_body(first, last):
        return bank_uses([u for p in range(NP) for u in units(p, first, last)])

    prologue = xc + kq[0] + kq[1] + kq[2] + v0[0] + v0[1] + v0[2]
    post = [("FG", 0)] + [u for e in ends for u in e]
    order = UseOrder(prologue + [("MT", 7)], of_body(True, False), of_body(False, False), of_body(False, True), bank_uses(post))

    def over(eng, body):
        body(0, True, False)
        with eng.Fori(1, NB - 1) as b:
            body(b, False, False)
        body(NB - 1, False, True)

    def share(us, c):
        n = len(us)
        return us[n * c // NC:n * (c + 1) // NC]

    def tiles(c):
        return range(2 * c, min(2 * c + 2, KT))

    with ExitStack() as cx:
        def sb(name, shape, dt=F32):
            return cx.enter_context(nc.sbuf_tensor(f"wide_{name}", shape, dt))

        def sem(name):
            return cx.enter_context(nc.semaphore(f"wide_{name}"))

        def loaded(name, src):
            t = sb(name, list(src.shape))
            loads.append((t, src))
            return t

        loads = []
        wq, wk, wv, wo, bo, wf, dd = (loaded(n, w[n]) for n in ("wq", "wk", "wv", "wo", "bo", "wf", "dd"))
        x_in = sb("x_in", [128, QT, 128])
        x_res = sb("x_res", [128, QT, 128])
        x_out = sb("x_out", [128, QT, 128])
        x1 = sb("x1", [128, QT, 128])
        x1T = sb("x1T", [128, S])
        xT = sb("xT", [128, S])
        ctx_in = sb("ctx_in", [128, KT, 128])
        cT = sb("cT", [128, NK])
        V = sb("V", [128, KT, H * DQ])
        K1 = sb("K1", [128, 4, HB, NK], F16)
        K2 = sb("K2", [128, 2, HB, NK], F16)
        Q1 = sb("Q1", [128, 4, HB, S], F16)
        Q2 = sb("Q2", [128, 4, HB, S], F16)
        qh = sb("qh", [128, S], F16)
        P = sb("P", [128, 4, 2, HB, S])
        acc = sb("acc", [128, 2, HB * S])
        MX = sb("MX", [128, QT, 128], F16)
        mpart = sb("mpart", [128, QT, HB, 4])
        mfull = sb("mfull", [128, QT, HB])
        ones = sb("ones", [128, DQ])
        oT = sb("oT", [128, S])
        rsum = sb("rsum", [128, S])
        ON = sb("ON", [128, NP, S])
        y = sb("y", [128, QT, 128])
        stats = sb("stats", [128, QT, 6])
        mv = sb("mv", [128, QT, 2])
        ve = sb("ve", [128, QT])
        rstd = sb("rstd", [128, QT])

        w_ld, started = sem("weights_loaded"), sem("started")
        x_ld, xr_ld, c_ld, st_done = sem("x_loaded"), sem("residual_loaded"), sem("context_loaded"), sem("stored")
        m_full, m_free = sem("bank_full"), sem("bank_free")
        s_full, s_free = sem("scores_full"), sem("scores_maxed")
        t_full, e_done, pv_done = sem("scoresT_full"), sem("exp_done"), sem("pv_done")
        p_summed, acc_ready = sem("p_summed"), sem("sums_ready")
        mx_ready, hi_ready, ot_ready, k2_ready = sem("max_ready"), sem("high_ready"), sem("oT_ready"), sem("k2_ready")
        x1_ready = sem("x1_ready")
        xr_used, ve_ready, rstd_ready, y_ready = sem("residual_used"), sem("var_ready"), sem("rstd_ready"), sem("out_ready")

        with nc.Block() as block:
            @block.sync
            def _(sp):
                for t, src in loads:
                    sp.dma_start(t[:], src).then_inc(w_ld, 16)
                sp.wait_ge(w_ld, 16 * len(loads))

            @block.vector
            def _(dve):
                nc.vector.memset(Q2[:], 0.0)
                nc.vector.memset(MX[:], 0.0)
                nc.vector.memset(ones[:], 1.0)
                nc.vector.memset(K2[:], 0.0)
                dve.drain()
                nc.vector.memset(K2[DQ:DQ + 2, :, 0, :], 1.0)
                nc.vector.memset(K2[0:2, :, 1, :], 1.0)
                dve.drain().then_inc(started, 1)

        with nc.Block() as block:
            @block.sync
            def _(sp):
                def load(b):
                    sp.dma_start(x_in[:], tokens(x_src, b)).then_inc(x_ld, 16)
                    src = ctx[bass.ds(b, 1)]
                    full = (KT - 1) * 128
                    sp.dma_start(ctx_in[:, 0:KT - 1, :],
                                 src[:, 0:full].rearrange("o (k p) d -> p (o k) d", p=128)).then_inc(c_ld, 16)
                    sp.dma_start(ctx_in[0:kn[-1], KT - 1, :],
                                 src[:, full:NK].rearrange("o p d -> p (o d)")).then_inc(c_ld, 16)

                def load_res(b):
                    sp.dma_start(x_res[:], tokens(x_src, b)).then_inc(xr_ld, 16)

                def store(b):
                    sp.wait_ge(y_ready, b + 1)
                    sp.dma_start(tokens(x_dst, b), x_out[:]).then_inc(st_done, 16)

                load(0)
                load_res(0)

                def body(b, first, last):
                    if not last:
                        sp.wait_ge(m_free, order.no(b - 1, ("C", 3)) + 1)
                        load(b + 1)
                    if not first:
                        if due(b):
                            sp.wait_ge(xr_used, b)
                        load_res(b)
                        store(b - 1)

                over(sp, body)
                store(NB - 1)
                sp.wait_ge(st_done, 16 * NB)

            @block.tensor
            def _(pe):
                def begin(b, u):
                    if due(order.no(b, u)):
                        pe.wait_ge(m_free, order.no(b, u))

                def setup(b, bs, u):
                    begin(b, u)
                    if u[0] == "X":
                        pe.wait_ge(x_ld, bs * 16 + 16)
                        for t in range(QT):
                            last = nc.tensor.transpose(psM[:, t * 128:t * 128 + 128], x_in[:, t, :], ident[:])
                    elif u[0] == "C":
                        if u[1] == 0:
                            pe.wait_ge(c_ld, bs * 32 + 32)
                        for i, k in enumerate(range(4 * u[1], min(4 * u[1] + 4, KT))):
                            last = nc.tensor.transpose(psM[:, i * 128:i * 128 + kn[k]], ctx_in[0:kn[k], k, :],
                                                       ident[0:kn[k], 0:kn[k]])
                    elif u[0] == "Q":
                        last = nc.tensor.matmul(psM[:, 0:S], wq[:, u[1] * 128:u[1] * 128 + 128], xT[:],
                                                start=True, stop=True, skip_group_check=True)
                    elif u[0] == "K":
                        a, z = kcuts[u[2]], kcuts[u[2] + 1]
                        last = nc.tensor.matmul(psM[:, 0:z - a], wk[:, u[1] * 128:u[1] * 128 + 128], cT[:, a:z],
                                                start=True, stop=True, skip_group_check=True)
                    elif u[0] == "V":
                        k = u[2]
                        last = nc.tensor.matmul(psM[0:kn[k], :], cT[:, k * 128:k * 128 + kn[k]], wv[:, u[1] * 512:u[1] * 512 + 512],
                                                start=True, stop=True, skip_group_check=True)
                    last.then_inc(m_full, 1)

                def scores(G, p, ch, at, use):
                    n = G * CA + ch
                    if ch == 0:
                        pe.wait_ge(m_free, order.no(at, use) + 1)
                    if due(n - 1):
                        pe.wait_ge(s_free, n - 1)
                    i, t, k = ch // 8, ch // 4 % 2, ch % 4
                    a, z = cuts[k], cuts[k + 1]
                    nc.tensor.matmul(psA[:, ch % 2, 0:z - a], Q1[:, p % 4, i, t * 128:t * 128 + 128], K1[:, p % 4, i, a:z],
                                     start=True, stop=True, skip_group_check=True).then_inc(s_full, 1)

                def max_rows(b, G, u):
                    pe.wait_ge(mx_ready, G + 1)
                    begin(b, u)
                    for t in range(QT):
                        last = nc.tensor.transpose(psM[:, t * 64:t * 64 + 64].bitcast(F16), MX[:, t, :], ident16[:])
                    last.then_inc(m_full, 1)

                def scoresT(b, G, p, c):
                    n = G * NC + c
                    if c == 0:
                        pe.wait_ge(m_free, order.no(b if p else b - 1, ("MT", (p - 1) % 8)) + 1)
                        pe.wait_ge(k2_ready, G + 1)
                    if due(n - 1):
                        pe.wait_ge(e_done, n - 1)
                    for e, k in enumerate(tiles(c)):
                        ks = slice(k * 128, k * 128 + kn[k])
                        for i in range(HB):
                            out = psB[0:kn[k], (p * NC + c) % 2, e * BANK + i * S:e * BANK + i * S + S]
                            nc.tensor.matmul(out, K1[:, p % 4, i, ks], Q1[:, p % 4, i, :], start=True, stop=False, skip_group_check=True)
                            last = nc.tensor.matmul(out, K2[:, p % 2, i, ks], Q2[:, p % 4, i, :], start=False, stop=True,
                                                    skip_group_check=True)
                    last.then_inc(t_full, 1)

                def weigh(b, G, p, c):
                    n = G * NC + c
                    if c == 0:
                        if due(G):
                            pe.wait_ge(ot_ready, G)
                        if p in (0, 4):
                            pe.wait_ge(m_free, order.no(b if p else b - 1, ("V", p // 4, KT - 1)) + 1)
                    pe.wait_ge(e_done, n + 1)
                    pe.wait_ge(started, 1)
                    for e, k in enumerate(tiles(c)):
                        for i in range(HB):
                            last = nc.tensor.matmul(psO[i * DQ:(i + 1) * DQ, 0:S], V[0:kn[k], k, (2 * p + i) * DQ:(2 * p + i + 1) * DQ],
                                                    P[0:kn[k], (p * NC + c) % 4, e, i, :], start=(k == 0), stop=(k == KT - 1),
                                                    skip_group_check=True)
                    last.then_inc(pv_done, 1)

                def end(b, G, u):
                    if u[0] == "FG":
                        pe.wait_ge(acc_ready, G + 1)
                        begin(b, u)
                        pe.wait_ge(started, 1)
                        for i in range(HB):
                            last = nc.tensor.matmul(psM[i * DQ:(i + 1) * DQ, 0:S], ones[:], acc[:, (u[1] - 1) % 2, i * S:i * S + S],
                                                    start=True, stop=True, skip_group_check=True)
                        last.then_inc(m_full, 1)
                    elif u[0] == "EW":
                        begin(b, u)
                        for t in range(QT):
                            for p in range(NP):
                                last = nc.tensor.matmul(psM[:, t * 128:t * 128 + 128], ON[:, p, t * 128:t * 128 + 128], wo[:, p, :],
                                                        start=(p == 0), stop=(p == NP - 1), skip_group_check=True)
                        last.then_inc(m_full, 1)
                    elif u[0] == "FT":
                        if due(b):
                            pe.wait_ge(x1_ready, b)
                        begin(b, u)
                        for t in range(QT):
                            last = nc.tensor.transpose(psM[:, t * 128:t * 128 + 128], x1[:, t, :], ident[:])
                        last.then_inc(m_full, 1)
                    elif u[0] == "FW":
                        begin(b, u)
                        for t in range(QT):
                            for m in (wf, dd):
                                last = nc.tensor.matmul(psM[:, t * 128:t * 128 + 128], x1T[:, t * 128:t * 128 + 128], m[:],
                                                        start=(m is wf), stop=(m is dd), skip_group_check=True)
                        last.then_inc(m_full, 1)

                def unit(b, p, u):
                    if u[0] == "A":
                        q = (p + 2) % 8
                        at = b if p else b - 1
                        scores(b * 8 + p + 2, q, u[2], at, ("K", q, 3))
                    elif u[0] == "MT":
                        max_rows(b, b * 8 + p + 1, u)
                    elif u[0] in ("FG", "EW", "FT", "FW"):
                        end(b, b * 8 + p - 1, u)
                    elif u[0] not in NO_BANK:
                        setup(b, b + 1 if u[0] in "XC" else 0, u)

                for u in prologue:
                    setup(-1, 0, u)
                for ch in range(CA):
                    scores(0, 0, ch, -1, ("K", 0, 3))
                max_rows(-1, 0, ("MT", 7))
                for ch in range(CA):
                    scores(1, 1, ch, -1, ("K", 1, 3))

                def body(b, first, last):
                    for p in range(NP):
                        us = units(p, first, last)
                        for c in range(NC):
                            scoresT(b, b * 8 + p, p, c)
                            if c:
                                weigh(b, b * 8 + p, p, c - 1)
                            for u in share(us, c):
                                unit(b, p, u)
                        weigh(b, b * 8 + p, p, NC - 1)

                over(pe, body)
                for u in post:
                    end(NB, NB * 8 - 1, u)

            @block.scalar
            def _(act):
                def take(b, u):
                    act.wait_ge(m_full, order.no(b, u) + 1)

                def exps(G, p, c):
                    n = G * NC + c
                    act.wait_ge(t_full, n + 1)
                    if due(n - 3):
                        act.wait_ge(pv_done, n - 3)
                    if due(n - 3):
                        act.wait_ge(p_summed, n - 3)
                    r, ks = p * NC + c, tiles(c)
                    rows, e = kn[ks[0]], len(ks)
                    nc.scalar.activation(P[0:rows, r % 4, 0:e].rearrange("k e i q -> k (e i q)"), psB[0:rows, r % 2, 0:e * BANK],
                                         ACT.Exp, scale=SCALE).then_inc(e_done, 1)

                def copy_out(b, G, p):
                    if due(G * NC):
                        act.wait_ge(pv_done, G * NC)
                    if not (isinstance(b, int) and b == 0 and p == 1):
                        act.wait_ge(m_free, order.no(b if p else b - 1, ("FG", (p - 1) % 8)) + 1)
                    nc.scalar.activation(oT[:], psO[:, 0:S], ACT.Copy).then_inc(ot_ready, 1)

                def unit(b, u):
                    if u[0] == "X":
                        take(b, u)
                        nc.scalar.activation(xT[:], psM[:, 0:S], ACT.Copy).then_inc(m_free, 1)
                    elif u[0] == "FT":
                        take(b, u)
                        nc.scalar.activation(x1T[:], psM[:, 0:S], ACT.Copy).then_inc(m_free, 1)
                    elif u[0] == "C":
                        take(b, u)
                        a, z = kcuts[u[1]], kcuts[u[1] + 1]
                        nc.scalar.activation(cT[:, a:z], psM[:, 0:z - a], ACT.Copy).then_inc(m_free, 1)
                    elif u[0] == "K":
                        take(b, u)
                        a, z = kcuts[u[2]], kcuts[u[2] + 1]
                        for i in range(HB):
                            r = slice(i * DQ, (i + 1) * DQ)
                            last = nc.scalar.activation(K1[r, u[1] % 4, i, a:z], psM[r, 0:z - a], ACT.Copy)
                        act.drain().then_inc(hi_ready, 1)
                    elif u[0] == "V":
                        take(b, u)
                        k = u[2]
                        nc.scalar.activation(V[0:kn[k], k, u[1] * 512:u[1] * 512 + 512], psM[0:kn[k], :], ACT.Copy).then_inc(m_free, 1)

                for u in prologue:
                    unit(-1, u)

                def body(b, first, last):
                    for p in range(NP):
                        us = units(p, first, last)
                        for c in range(NC):
                            exps(b * 8 + p, p, c)
                            if c == 0 and not (first and p == 0):
                                copy_out(b, b * 8 + p, p)
                            for u in share(us, c):
                                unit(b, u)

                over(act, body)
                copy_out(NB, NB * 8, 0)
                for u in post:
                    unit(NB, u)

            @block.gpsimd
            def _(pool):
                def sums(b, G, p, c):
                    n = G * NC + c
                    pool.wait_ge(e_done, n + 1)
                    out = acc[:, p % 2, :]
                    r = (p * NC + c) % 4

                    def tile(e):
                        return P[:, r, e].rearrange("k i q -> k (i q)")
                    if c == 0:
                        if not (isinstance(b, int) and b == 0 and p < 2):
                            use = ("FG", (p - 1) % 8)
                            pool.wait_ge(m_full, order.no(b if p >= 1 else b - 1, use) + 1)
                        last = nc.gpsimd.tensor_tensor(out, tile(0), tile(1), ALU.add)
                    else:
                        for e, k in enumerate(tiles(c)):
                            if e:
                                pool.drain()
                            last = nc.gpsimd.tensor_tensor(out[0:kn[k]], out[0:kn[k]], tile(e)[0:kn[k]], ALU.add)
                    pool.drain().then_inc(p_summed, 1)
                    if c == NC - 1:
                        pool.drain().then_inc(acc_ready, 1)

                def root(n):
                    if due(n):
                        pool.wait_ge(ve_ready, n)
                    nc.gpsimd.tensor_tensor(rstd[:], ve[:], minus_half[:, 0:QT], ALU.pow).then_inc(rstd_ready, 1)

                def body(b, first, last):
                    for p in range(NP):
                        if not first and p == 2:
                            root(b * 2 - 1)
                        if not first and p == 6:
                            root(b * 2)
                        for c in range(NC):
                            sums(b, b * 8 + p, p, c)

                over(pool, body)
                root(NB * 2 - 1)
                root(NB * 2)

            @block.vector
            def _(dve):
                def take(b, u):
                    dve.wait_ge(m_full, order.no(b, u) + 1)

                def hi_no(bs, u):
                    return bs * 32 + u[1] * 4 + u[2] + 1

                def setup(b, bs, u):
                    if u[0] == "Q":
                        take(b, u)
                        p = u[1]
                        nc.vector.tensor_copy(qh[:], psM[:, 0:S])
                        dve.drain()
                        for i in range(HB):
                            r, o = slice(i * DQ, (i + 1) * DQ), slice((1 - i) * DQ, (2 - i) * DQ)
                            nc.vector.tensor_tensor(Q2[r, p % 4, i, :], psM[r, 0:S], qh[r, :], ALU.subtract)
                            nc.vector.tensor_copy(Q1[r, p % 4, i, :], qh[r, :])
                            nc.vector.tensor_copy(Q1[o, p % 4, i, :], qh[r, :])
                        dve.drain().then_inc(m_free, 1)
                    elif u[0] == "K":
                        take(b, u)
                        if due(hi_no(bs, u)):
                            dve.wait_ge(hi_ready, hi_no(bs, u))
                        a, z = kcuts[u[2]], kcuts[u[2] + 1]
                        for i in range(HB):
                            r, o = slice(i * DQ, (i + 1) * DQ), slice((1 - i) * DQ, (2 - i) * DQ)
                            nc.vector.tensor_tensor(K1[o, u[1] % 4, i, a:z], psM[r, 0:z - a], K1[r, u[1] % 4, i, a:z], ALU.subtract)
                        dve.drain().then_inc(m_free, 1)

                def copy_high(G, p):
                    if due((G - 1) * NC):
                        dve.wait_ge(t_full, (G - 1) * NC)
                    for i in range(HB):
                        r = slice(i * DQ, (i + 1) * DQ)
                        nc.vector.tensor_copy(K2[r, p % 2, i, :], K1[r, p % 4, i, :])
                    dve.drain().then_inc(k2_ready, 1)

                def maxima(G, ch):
                    n = G * CA + ch
                    if ch == 0:
                        if due(G):
                            dve.wait_ge(mx_ready, G)
                    dve.wait_ge(s_full, n + 1)
                    i, t, k = ch // 8, ch // 4 % 2, ch % 4
                    nc.vector.tensor_reduce(mpart[:, t, 1 - i, k:k + 1], psA[:, ch % 2, 0:cuts[k + 1] - cuts[k]],
                                            AX.X, ALU.max).then_inc(s_free, 1)
                    if ch == CA - 1:
                        dve.drain()
                        nc.vector.tensor_reduce(mfull[:], mpart[:], AX.X, ALU.max)
                        cols = MX[:].rearrange("p t (i s) -> p t i s", s=DQ)
                        dve.drain()
                        nc.vector.tensor_scalar(cols[:, :, :, 0], mfull[:], -1.0, None, ALU.mult)
                        dve.drain()
                        nc.vector.scalar_tensor_tensor(out=cols[:, :, :, 1], in0=mfull[:], scalar=-1.0, in1=cols[:, :, :, 0],
                                                       op0=ALU.mult, op1=ALU.subtract).then_inc(mx_ready, 1)

                def add_max(b, p, u):
                    take(b, u)
                    for i in range(HB):
                        o = slice((1 - i) * DQ, (2 - i) * DQ)
                        nc.vector.tensor_copy(Q2[o, p % 4, i, :], psM[o, 0:S // 2].bitcast(F16))
                    dve.drain().then_inc(m_free, 1)

                def end(b, be, G, gp, u):
                    if u[0] == "FG":
                        dve.wait_ge(ot_ready, G + 1)
                        take(b, u)
                        nc.vector.reciprocal(rsum[:], psM[:, 0:S])
                        dve.drain()
                        nc.vector.tensor_tensor(ON[:, gp, :], oT[:], rsum[:], ALU.mult)
                        dve.drain().then_inc(m_free, 1)
                    elif u[0] == "EW":
                        dve.wait_ge(xr_ld, be * 16 + 16)
                        take(b, u)
                        nc.vector.tensor_tensor(y[:], psM[:, 0:S].rearrange("p (t d) -> p t d", t=QT), bo[:], ALU.add)
                        dve.drain().then_inc(m_free, 1)
                        nc.vector.tensor_tensor(y[:], y[:], x_res[:], ALU.add)
                        dve.drain().then_inc(xr_used, 1)
                        layer_norm_stats(nc, dve, y, stats, mv, ve).then_inc(ve_ready, 1)
                    elif u[0] == "FW":
                        take(b, u)
                        nc.vector.tensor_tensor(y[:], psM[:, 0:S].rearrange("p (t d) -> p t d", t=QT), x1[:], ALU.add)
                        dve.drain().then_inc(m_free, 1)
                        layer_norm_stats(nc, dve, y, stats, mv, ve).then_inc(ve_ready, 1)
                    elif u[0] in ("EN", "FN"):
                        out = x1 if u[0] == "EN" else x_out
                        dve.wait_ge(rstd_ready, be * 2 + (1 if u[0] == "EN" else 2))
                        if u[0] == "FN":
                            if due(be * 16):
                                dve.wait_ge(st_done, be * 16)
                        for t in range(QT):
                            nc.vector.tensor_scalar(out[:, t, :], y[:, t, :], mv[:, t, 0:1], rstd[:, t:t + 1],
                                                    ALU.subtract, ALU.mult)
                        dve.drain().then_inc(x1_ready if u[0] == "EN" else y_ready, 1)

                for u in prologue:
                    setup(-1, 0, u)
                for ch in range(CA):
                    maxima(0, ch)
                add_max(-1, 0, ("MT", 7))
                copy_high(0, 0)
                for ch in range(CA):
                    maxima(1, ch)

                def body(b, first, last):
                    for p in range(NP):
                        for u in units(p, first, last):
                            if u[0] == "A":
                                maxima(b * 8 + p + 2, u[2])
                            elif u[0] == "MT":
                                add_max(b, (p + 1) % 8, u)
                            elif u[0] == "C2":
                                copy_high(b * 8 + p + 1, (p + 1) % 8)
                            elif u[0] in ("FG", "EW", "EN", "FW", "FN"):
                                end(b, b - 1, b * 8 + p - 1, (p - 1) % 8, u)
                            else:
                                setup(b, b + 1 if p >= 5 else b, u)

                over(dve, body)
                for u in post:
                    end(NB, NB - 1, NB * 8 - 1, 7, u)


def experts(nc, x_src, x_dst, w, ps, ident, minus_half):
    psA, psB, psO, psM = ps
    E, F = 8, 512
    FT, TQ = F // 128, 4
    NQ = NB * S // (TQ * 128)
    TT = TQ * 128
    xs = x_src.rearrange("b s d -> (b s) d").rearrange("(q t p) d -> q p t d", t=TQ, p=128)
    xd = x_dst.rearrange("b s d -> (b s) d").rearrange("(q t p) d -> q p t d", t=TQ, p=128)

    def quad(x, q):
        return x[bass.ds(q, 1)].rearrange("o p t d -> p (o t) d")

    with ExitStack() as cx:
        def sb(name, shape, dt=F32):
            return cx.enter_context(nc.sbuf_tensor(f"moe_{name}", shape, dt))

        def sem(name):
            return cx.enter_context(nc.semaphore(f"moe_{name}"))

        def loaded(name, src):
            t = sb(name, list(src.shape))
            loads.append((t, src))
            return t

        loads = []
        sw, sbias, rank, pick, w1, b1, w2, b2 = (loaded(n, w[n]) for n in ("sw", "sb", "rank", "pick", "w1", "b1", "w2", "b2"))
        x_in = sb("x_in", [128, 2, TQ, 128])
        x_out = sb("x_out", [128, 2, TQ, 128])
        xT = sb("xT", [128, 2, TT])
        NT = NQ * TQ
        lg = sb("logits", [128, NT, E])
        ex = sb("exps", [128, NT, E])
        sel = sb("selected", [128, NT, E])
        gates = sb("gates", [128, NT, E])
        top = sb("top", [128, NT])
        den = sb("den", [128, NT])
        gq = sb("gq", [128, TQ, E])
        gT = sb("gT", [E, TT])
        gB = sb("gB", [128, 2, TT])
        hT = sb("hT", [128, 2, FT, TT])
        tmp = sb("tmp", [128, TT])
        accT = sb("accT", [128, TT])
        accS = sb("accS", [128, TT])
        y = sb("y", [128, TQ, 128])
        stats = sb("stats", [128, TQ, 6])
        mv = sb("mv", [128, TQ, 2])
        ve = sb("ve", [128, TQ])
        rstd = sb("rstd", [128, TQ])

        w_ld, r_ld = sem("weights_loaded"), sem("router_x_loaded")
        x_ld = [sem(f"x_loaded{i}") for i in range(2)]
        st_done = [sem(f"stored{i}") for i in range(2)]
        r_full, r_T, r_lg, r_free = sem("router_T_full"), sem("router_T_copied"), sem("router_logits_full"), sem("router_logits_read")
        d_ready, ex_ready = sem("shifted_ready"), sem("exps_ready")
        m_full, m_free, gq_ready = sem("bank_full"), sem("bank_free"), sem("gates_ready")
        h_full, h_done, y_full, y_used = sem("hidden_full"), sem("hidden_done"), sem("y_full"), sem("y_used")
        g_full, g_done, acc_ready = sem("gate_rows_full"), sem("gate_rows_done"), sem("sum_ready")
        x_used, ve_ready, rstd_ready, out_ready = sem("x_used"), sem("var_ready"), sem("rstd_ready"), sem("out_ready")

        with nc.Block() as block:
            @block.sync
            def _(sp):
                for t, src in loads:
                    sp.dma_start(t[:], src).then_inc(w_ld, 16)
                sp.wait_ge(w_ld, 16 * len(loads))

        with nc.Block() as block:
            @block.sync
            def _(sp):
                def load(q):
                    sp.dma_start(x_in[:, 0], quad(xs, q)).then_inc(r_ld, 16)
                load(0)
                with sp.Fori(1, NQ) as q:
                    if due(q):
                        sp.wait_ge(r_full, q)
                    load(q)

            @block.tensor
            def _(pe):
                def body(q):
                    pe.wait_ge(r_ld, q * 16 + 16)
                    if due(q):
                        pe.wait_ge(r_T, q)
                    for t in range(TQ):
                        last = nc.tensor.transpose(psM[:, t * 128:t * 128 + 128], x_in[:, 0, t, :], ident[:])
                    last.then_inc(r_full, 1)
                    pe.wait_ge(r_T, q + 1)
                    if due(q):
                        pe.wait_ge(r_free, q)
                    for t in range(TQ):
                        last = nc.tensor.matmul(psO[:, t * E:t * E + E], xT[:, 0, t * 128:t * 128 + 128], sw[:],
                                                start=True, stop=True, skip_group_check=True)
                    last.then_inc(r_lg, 1)
                body(0)
                with pe.Fori(1, NQ) as q:
                    body(q)

            @block.scalar
            def _(act):
                def body(q):
                    act.wait_ge(r_full, q + 1)
                    if due(q):
                        act.wait_ge(r_lg, q)
                    nc.scalar.activation(xT[:, 0], psM[:], ACT.Copy).then_inc(r_T, 1)
                body(0)
                with act.Fori(1, NQ) as q:
                    body(q)
                act.wait_ge(d_ready, 1)
                nc.scalar.activation(ex[:], ex[:], ACT.Exp).then_inc(ex_ready, 1)

            @block.vector
            def _(dve):
                def body(q):
                    dve.wait_ge(r_lg, q + 1)
                    nc.vector.tensor_tensor(lg[:, bass.ds(q * TQ, TQ), :], psO[:, 0:TQ * E].rearrange("p (t e) -> p t e", e=E),
                                            sbias[:], ALU.add).then_inc(r_free, 1)
                body(0)
                with dve.Fori(1, NQ) as q:
                    body(q)

                def wide(v):
                    return v[:].unsqueeze(2).to_broadcast([128, NT, E])
                dve.wait_ge(r_free, NQ)
                nc.vector.tensor_reduce(top[:], lg[:], AX.X, ALU.max)
                dve.drain()
                nc.vector.tensor_tensor(ex[:], lg[:], wide(top), ALU.subtract)
                nc.vector.tensor_tensor(sel[:], lg[:], wide(top), ALU.is_ge)
                dve.drain().then_inc(d_ready, 1)
                nc.vector.tensor_tensor(sel[:], sel[:], rank[:], ALU.mult)
                dve.drain()
                nc.vector.tensor_reduce(top[:], sel[:], AX.X, ALU.max)
                dve.drain()
                nc.vector.tensor_tensor(sel[:], sel[:], wide(top), ALU.is_equal)
                dve.wait_ge(ex_ready, 1)
                nc.vector.tensor_reduce(den[:], ex[:], AX.X, ALU.add)
                dve.drain()
                nc.vector.reciprocal(den[:], den[:])
                dve.drain()
                nc.vector.tensor_tensor(gates[:], sel[:], wide(den), ALU.mult)

        prologue = ["X", "GT"]
        body_uses = ["EO", "X", "GT"]

        def no(q, use):
            if isinstance(q, int):
                if q == -1:
                    return prologue.index(use)
                if q == 0:
                    return 2 + ["X", "GT"].index(use)
                if q == NQ - 1 or q == NQ:
                    return 4 + 3 * (NQ - 2) + (q - NQ + 1)
            return q * 3 + (1 + body_uses.index(use))

        def over(eng, body):
            body(0, 0, 0, True, False)
            body(1, 0, 1, False, False)
            with eng.Fori(1, NQ // 2 - 1) as i:
                for par in range(2):
                    body(i * 2 + par, i, par, False, False)
            body(NQ - 2, NQ // 2 - 1, 0, False, False)
            body(NQ - 1, NQ // 2 - 1, 1, False, True)

        with nc.Block() as block:
            @block.sync
            def _(sp):
                def load(q, par):
                    sp.dma_start(x_in[:, par], quad(xs, q)).then_inc(x_ld[par], 16)

                def store(q, par):
                    sp.wait_ge(out_ready, q + 1)
                    sp.dma_start(quad(xd, q), x_out[:, par]).then_inc(st_done[par], 16)
                load(0, 0)
                load(1, 1)

                def body(q, i, par, first, last):
                    if not first:
                        if not last:
                            if due(q):
                                sp.wait_ge(x_used, q)
                            load(q + 1, 1 - par)
                        store(q - 1, 1 - par)
                over(sp, body)
                store(NQ - 1, 1)
                sp.wait_ge(st_done[0], 16 * NQ // 2)
                sp.wait_ge(st_done[1], 16 * NQ // 2)

            @block.tensor
            def _(pe):
                def turn_x(q, par, its):
                    pe.wait_ge(x_ld[par], its * 16 + 16)
                    if due(no(q, "X")):
                        pe.wait_ge(m_free, no(q, "X"))
                    for t in range(TQ):
                        last = nc.tensor.transpose(psM[:, t * 128:t * 128 + 128], x_in[:, par, t, :], ident[:])
                    last.then_inc(m_full, 1)

                def turn_gates(q):
                    pe.wait_ge(gq_ready, q + 2)
                    if due(no(q, "GT")):
                        pe.wait_ge(m_free, no(q, "GT"))
                    for t in range(TQ):
                        last = nc.tensor.transpose(psM[0:E, t * 128:t * 128 + 128], gq[:, t, :], ident[:])
                    last.then_inc(m_full, 1)

                def turn_back(q):
                    if due(q):
                        pe.wait_ge(acc_ready, q)
                    if due(no(q, "EO")):
                        pe.wait_ge(m_free, no(q, "EO"))
                    for t in range(TQ):
                        last = nc.tensor.transpose(psM[:, t * 128:t * 128 + 128], accS[:, t * 128:t * 128 + 128], ident[:])
                    last.then_inc(m_full, 1)

                def hidden(q, par, e):
                    n = q * E + e
                    if e == 0:
                        pe.wait_ge(m_free, no(q - 1, "GT") + 1)
                    for f in range(FT):
                        if due(n * FT + f - 3):
                            pe.wait_ge(h_done, n * FT + f - 3)
                        nc.tensor.matmul(psB[:, f // 2, f % 2 * BANK:(f % 2 + 1) * BANK], w1[:, e, f * 128:f * 128 + 128], xT[:, par],
                                         start=True, stop=True, skip_group_check=True).then_inc(h_full, 1)
                    if due(n):
                        pe.wait_ge(g_done, n)
                    nc.tensor.matmul(psO[:], pick[:, e, :], gT[:], start=True, stop=True, skip_group_check=True).then_inc(g_full, 1)

                def out(n, e):
                    if due(n - 1):
                        pe.wait_ge(y_used, n - 1)
                    pe.wait_ge(h_done, n * FT + FT)
                    for f in range(FT):
                        last = nc.tensor.matmul(psA[:, e % 2], w2[:, e, f, :], hT[:, e % 2, f, :], start=(f == 0), stop=(f == FT - 1),
                                                skip_group_check=True)
                    last.then_inc(y_full, 1)

                turn_x(-1, 0, 0)
                turn_gates(-1)

                def body(q, i, par, first, last):
                    for e in range(E):
                        hidden(q, par, e)
                        if not (first and e == 0):
                            out(q * E + e - 1, (e - 1) % E)
                        if e == 2 and not first:
                            turn_back(q)
                        if e == 5 and not last:
                            turn_x(q, 1 - par, i + par)
                        if e == 7 and not last:
                            turn_gates(q)
                over(pe, body)
                out(NQ * E - 1, E - 1)
                turn_back(NQ)

            @block.scalar
            def _(act):
                def copy_x(q, par):
                    act.wait_ge(m_full, no(q, "X") + 1)
                    nc.scalar.activation(xT[:, par], psM[:], ACT.Copy).then_inc(m_free, 1)

                def copy_gates(q):
                    act.wait_ge(m_full, no(q, "GT") + 1)
                    if due((q + 1) * E):
                        act.wait_ge(g_full, (q + 1) * E)
                    nc.scalar.activation(gT[:], psM[0:E, :], ACT.Copy).then_inc(m_free, 1)

                copy_x(-1, 0)
                copy_gates(-1)

                def body(q, i, par, first, last):
                    for e in range(E):
                        n = q * E + e
                        for f in range(FT):
                            act.wait_ge(h_full, n * FT + f + 1)
                            if f == 0:
                                if due(n - 1):
                                    act.wait_ge(y_full, n - 1)
                            nc.scalar.activation(hT[:, e % 2, f, :], psB[:, f // 2, f % 2 * BANK:(f % 2 + 1) * BANK],
                                                 ACT.Gelu_apprx_tanh, bias=b1[:, e, f:f + 1]).then_inc(h_done, 1)
                        act.wait_ge(g_full, n + 1)
                        if due(n - 1):
                            act.wait_ge(y_used, n - 1)
                        nc.scalar.activation(gB[:, e % 2], psO[:], ACT.Copy).then_inc(g_done, 1)
                        if e == 5 and not last:
                            copy_x(q, 1 - par)
                        if e == 7 and not last:
                            copy_gates(q)
                over(act, body)

            @block.gpsimd
            def _(pool):
                def body(q, i, par, first, last):
                    pool.wait_ge(ve_ready, q + 1)
                    nc.gpsimd.tensor_tensor(rstd[:], ve[:], minus_half[:, 0:TQ], ALU.pow).then_inc(rstd_ready, 1)
                over(pool, body)

            @block.vector
            def _(dve):
                def take_gates(q):
                    if due(q + 1):
                        dve.wait_ge(m_full, no(q - 1, "GT") + 1)
                    nc.vector.tensor_copy(gq[:], gates[:, bass.ds((q + 1) * TQ, TQ), :]).then_inc(gq_ready, 1)

                def gate(n, e):
                    dve.wait_ge(g_done, n + 1)
                    dve.wait_ge(y_full, n + 1)
                    if e == 0:
                        nc.vector.scalar_tensor_tensor(out=accT[:], in0=psA[:, e % 2], scalar=b2[:, e:e + 1], in1=gB[:, e % 2],
                                                       op0=ALU.add, op1=ALU.mult)
                        dve.drain().then_inc(y_used, 1)
                    else:
                        nc.vector.scalar_tensor_tensor(out=tmp[:], in0=psA[:, e % 2], scalar=b2[:, e:e + 1], in1=gB[:, e % 2],
                                                       op0=ALU.add, op1=ALU.mult)
                        dve.drain().then_inc(y_used, 1)
                        nc.vector.tensor_tensor(accS[:] if e == E - 1 else accT[:], accT[:], tmp[:], ALU.add)
                        dve.drain()

                def finish(q, qe, par, its):
                    dve.wait_ge(m_full, no(q, "EO") + 1)
                    nc.vector.tensor_tensor(y[:], psM[:].rearrange("p (t d) -> p t d", t=TQ), x_in[:, par], ALU.add)
                    dve.drain().then_inc(m_free, 1)
                    for t in range(TQ):
                        nc.vector.bn_stats(stats[:, t, :], y[:, t, :])
                    dve.drain().then_inc(x_used, 1)
                    for t in range(TQ):
                        nc.vector.bn_aggr(mv[:, t, :], stats[:, t, :])
                    dve.drain()
                    nc.vector.tensor_scalar(ve[:], mv[:, :, 1], EPS, None, ALU.add).then_inc(ve_ready, 1)

                def normalise(qe, par, its):
                    dve.wait_ge(rstd_ready, qe + 1)
                    if due(its * 16):
                        dve.wait_ge(st_done[par], its * 16)
                    for t in range(TQ):
                        nc.vector.tensor_scalar(x_out[:, par, t, :], y[:, t, :], mv[:, t, 0:1], rstd[:, t:t + 1],
                                                ALU.subtract, ALU.mult)
                    dve.drain().then_inc(out_ready, 1)

                take_gates(-1)

                def body(q, i, par, first, last):
                    for e in range(E):
                        if not (first and e == 0):
                            gate(q * E + e - 1, (e - 1) % E)
                        if e == 0 and not first:
                            dve.drain().then_inc(acc_ready, 1)
                        if e == 2 and not first:
                            finish(q, q - 1, 1 - par, i - 1 + par)
                        if e == 4 and not first:
                            normalise(q - 1, 1 - par, i - 1 + par)
                        if e == 6 and not last:
                            take_gates(q)
                over(dve, body)
                gate(NQ * E - 1, E - 1)
                dve.drain().then_inc(acc_ready, 1)
                finish(NQ, NQ - 1, 1, NQ // 2 - 1)
                normalise(NQ - 1, 1, NQ // 2 - 1)


def decoder(nc, ins, out):
    with ExitStack() as c:
        def psum(name, shape):
            return c.enter_context(nc.psum_tensor(name, [128] + shape, F32))

        ps = psum("psA", [2, BANK]), psum("psB", [2, 2 * BANK]), psum("psO", [BANK]), psum("psM", [BANK])
        ident = c.enter_context(nc.sbuf_tensor("identity", [128, 128], F32))
        ident16 = c.enter_context(nc.sbuf_tensor("identity16", [128, 128], F16))
        minus_half = c.enter_context(nc.sbuf_tensor("minus_half", [128, 4], F32))
        const_ld = c.enter_context(nc.semaphore("constants_loaded"))
        between = [nc.dram_tensor(f"x_after_{n}", (NB, S, D), F32, kind="Internal").ap() for n in ("rope", "wide", "chunked", "cross")]

        def of(part):
            return {k[len(part) + 1:]: v for k, v in ins.items() if k.startswith(part + "_")}

        with nc.Block() as block:
            @block.sync
            def _(sp):
                sp.dma_start(ident[:], ins["ident"]).then_inc(const_ld, 16)
                sp.dma_start(ident16[:], ins["ident16"]).then_inc(const_ld, 16)
                sp.wait_ge(const_ld, 32)

            @block.gpsimd
            def _(pool):
                nc.gpsimd.memset(minus_half[:], -0.5)

        attention8(nc, "rope", ins["x"], between[0], of("rope"), ps, ident, ident16, minus_half)
        cross64(nc, between[0], between[1], of("wide"), ps, ident, ident16, minus_half, ins["ctx"])
        attention8(nc, "chunked", between[1], between[2], of("chunked"), ps, ident, ident16, minus_half)
        attention8(nc, "cross", between[2], between[3], of("cross"), ps, ident, ident16, minus_half, ctx=ins["ctx"])
        experts(nc, between[3], out, of("moe"), ps, ident, minus_half)


def head_columns(w, swap=False):
    w = np.asarray(w).reshape(D, H, DH)
    if swap:
        w = w.reshape(D, H, DH // 2, 2)[..., ::-1].reshape(D, H, DH)
    out = np.zeros((D, H, SLOT), np.float32)
    for s in range(3):
        out[:, :, DH * s:DH * s + DH] = w
    return out.reshape(D, H * SLOT)


def head_bias(b, shift_rows, swap=False):
    b = np.asarray(b).reshape(H, DH)
    if swap:
        b = b.reshape(H, DH // 2, 2)[..., ::-1].reshape(H, DH)
    out = np.zeros((H, SLOT), np.float32)
    for s in range(3):
        out[:, DH * s:DH * s + DH] = b
    out[:, M_ROW:M_ROW + 2] = shift_rows
    return np.ascontiguousarray(out.reshape(NG, HG * SLOT).T)


def low_rows():
    out = np.zeros((HG, SLOT, 2), np.float32)
    out[:, DH:2 * DH, 0] = 1
    out[:, 2 * DH:3 * DH, 1] = 1
    return out.reshape(128, 2)


def rope_tables():
    inv = (np.float32(1.0) / np.float32(10000.0) ** (np.arange(0, DH, 2, dtype=np.float32) / np.float32(DH))).astype(np.float32)
    freqs = np.arange(S, dtype=np.float32)[:, None] * inv[None, :]
    angle = np.concatenate([freqs, freqs], -1)[:, ::2]
    cos, sin = np.zeros((HG, SLOT, S), np.float32), np.zeros((HG, SLOT, S), np.float32)
    for s in range(3):
        for d in range(DH):
            cos[:, DH * s + d] = np.cos(angle[:, d // 2])
            sin[:, DH * s + d] = np.sin(angle[:, d // 2]) * (-1 if d % 2 == 0 else 1)
    cos[:, M_ROW:M_ROW + 2] = 1
    return cos.reshape(128, S), sin.reshape(128, S)


def chunk_columns(w, part):
    w = np.asarray(w).reshape(16, 3, DH, D)[:, part].transpose(2, 0, 1)
    out = np.zeros((D, 16, SLOT), np.float32)
    for s in range(3 if part < 2 else 1):
        out[:, :, DH * s:DH * s + DH] = w
    return out.reshape(D, 16 * SLOT)


def chunk_bias(b, part):
    b = np.asarray(b).reshape(16, 3, DH)[:, part].T
    out = np.zeros((HG, SLOT, 16), np.float32)
    for s in range(3 if part < 2 else 1):
        out[:, DH * s:DH * s + DH, :] = b
    if part == 1:
        out[:, M_ROW:M_ROW + 2] = 1
    if part == 2:
        out[:, DH] = 1
    return out.reshape(128, 16)


def on_rows(b, n):
    b = np.asarray(b).reshape(1, 1, -1)
    return np.ascontiguousarray(np.broadcast_to(b, (128, n, b.size)))


def flat_rows(b, n):
    return on_rows(b, n).reshape(128, -1)


def turned(w):
    return np.ascontiguousarray(np.asarray(w).T)


def laid_out(i):
    out = {"x": np.asarray(i["x"]), "ctx": np.asarray(i["ctx_1024"]),
           "ident": np.eye(128, dtype=np.float32), "ident16": np.eye(128, dtype=np.float16)}
    cos, sin = rope_tables()
    a = "L0_attn_"
    out |= {"rope_wq": head_columns(i[a + "Wq"]), "rope_wqs": head_columns(i[a + "Wq"], True),
            "rope_wk": head_columns(i[a + "Wk"]), "rope_wks": head_columns(i[a + "Wk"], True),
            "rope_bq": head_bias(i[a + "bq"], 0), "rope_bqs": head_bias(i[a + "bq"], 0, True),
            "rope_bk": head_bias(i[a + "bk"], 1), "rope_bks": head_bias(i[a + "bk"], 0, True),
            "rope_cos": cos, "rope_sin": sin, "rope_wv": np.asarray(i[a + "Wv"]), "rope_bv": flat_rows(i[a + "bv"], QT),
            "rope_lo": low_rows(), "rope_wo": np.asarray(i[a + "Wo"]), "rope_bo": on_rows(i[a + "bo"], QT)}
    a = "L0_xattn_"
    dd = np.asarray(i["L0_ffn_disha"])
    out |= {"wide_wq": np.asarray(i[a + "Wq"]), "wide_wk": np.asarray(i[a + "Wk"]), "wide_wv": np.asarray(i[a + "Wv"]),
            "wide_wo": np.ascontiguousarray(np.asarray(i[a + "Wo"]).reshape(8, 128, D).transpose(1, 0, 2)),
            "wide_bo": on_rows(i[a + "bo"], QT), "wide_wf": turned(i["L0_ffn_weight"]), "wide_dd": np.concatenate([dd, dd])}
    a = "L1_attn_"
    for n, name in enumerate("qkv"):
        out |= {f"chunked_w{name}": chunk_columns(i[a + "W_qkv"], n), f"chunked_b{name}": chunk_bias(i[a + "b_qkv"], n)}
    out |= {"chunked_lo": low_rows(), "chunked_wo": turned(i[a + "W_out"]), "chunked_bo": on_rows(i[a + "b_out"], QT)}
    a = "L1_xattn_"
    out |= {"cross_wq": head_columns(turned(i[a + "Wq"])), "cross_wk": head_columns(turned(i[a + "Wk"])),
            "cross_bq": head_bias(i[a + "bq"], 0), "cross_bk": head_bias(i[a + "bk"], 1),
            "cross_wv": turned(i[a + "Wv"]), "cross_bv": flat_rows(i[a + "bv"], 4), "cross_lo": low_rows()}
    a = "L1_ffn_"
    pick = np.zeros((8, 8, 128), np.float32)
    for e in range(8):
        pick[e, e] = 1
    out |= {"moe_sw": np.asarray(i[a + "switch_w"]), "moe_sb": on_rows(i[a + "switch_b"], 4),
            "moe_rank": on_rows(np.arange(8, 0, -1).astype(np.float32), NB * QT), "moe_pick": pick,
            "moe_w1": np.ascontiguousarray(np.asarray(i[a + "w1"]).transpose(1, 0, 2)),
            "moe_b1": np.ascontiguousarray(np.asarray(i[a + "b1"]).reshape(8, 4, 128).transpose(2, 0, 1)),
            "moe_w2": np.ascontiguousarray(np.asarray(i[a + "w2"]).reshape(8, 4, 128, D).transpose(2, 0, 1, 3)),
            "moe_b2": turned(i[a + "b2"])}
    return out


def kernel(**inputs):
    import concourse.bacc as bacc
    from concourse.bass_utils import run_bass_kernel_spmd

    nc = bacc.Bacc("TRN2", target_bir_lowering=False, num_devices=1)
    arrays = laid_out(inputs)
    ins = {k: nc.dram_tensor(f"in_{k}", v.shape, mybir.dt.from_np(v.dtype), kind="ExternalInput").ap() for k, v in arrays.items()}
    out = nc.dram_tensor("out", (NB, S, D), F32, kind="ExternalOutput").ap()
    decoder(nc, ins, out)
    r = run_bass_kernel_spmd(nc, [{f"in_{k}": v for k, v in arrays.items()}], core_ids=[0])
    return r.results[0]["out"]
```

```python
from contextlib import ExitStack

import numpy as np

import concourse.bass as bass
from concourse import mybir

F32 = mybir.dt.float32
F16 = mybir.dt.float16
ALU = mybir.AluOpType
ACT = mybir.ActivationFunctionType
AX = mybir.AxisListType

NB, S, D, NKC = 16, 256, 128, 1601
QT = S // 128
H, DH, NG, HG = 16, 8, 4, 4
SLOT = 32
M_ROW = 24
EPS = 1e-5
BANK = 512


def due(value):
    return not isinstance(value, int) or value > 0


class UseOrder:

    def __init__(self, banks, prologue, first, body, last, post):
        self.lists = prologue, first, body, last, post
        self.banks = {use: i % banks for i, use in enumerate(body)}

    def bank(self, use):
        return self.banks[use]

    def no(self, b, use):
        bank = self.banks[use]
        prologue, first, body, last, post = ([u for u in us if self.banks[u] == bank] for us in self.lists)
        if isinstance(b, int):
            if b == -1:
                return prologue.index(use)
            if b == 0:
                return len(prologue) + first.index(use)
            if b == NB - 1:
                return len(prologue) + len(first) + (NB - 2) * len(body) + last.index(use)
            if b == NB:
                return len(prologue) + len(first) + (NB - 2) * len(body) + len(last) + post.index(use)
        return b * len(body) + (len(prologue) + len(first) - len(body) + body.index(use))


def over_batches(eng, body):
    body(0, 0, 0, True, False)
    body(1, 0, 1, False, False)
    with eng.Fori(1, NB // 2 - 1) as i:
        for par in range(2):
            body(i * 2 + par, i, par, False, False)
    body(NB - 2, NB // 2 - 1, 0, False, False)
    body(NB - 1, NB // 2 - 1, 1, False, True)


def spread(others, chunks):
    out, n, m = [], len(others), len(chunks)
    for i in range(max(n, 1)):
        out += others[i:i + 1]
        out += chunks[i * m // max(n, 1):(i + 1) * m // max(n, 1)]
    return out


def mixed(a, b):
    at = [((i + 0.5) / len(us), u) for us in (a, b) for i, u in enumerate(us)]
    return [u for _, u in sorted(at, key=lambda x: x[0])]


def delayed(us):
    us = list(us)
    for i in range(len(us) - 1, 0, -1):
        if us[i][0] == "A" and us[i - 1][0] != "A":
            us[i - 1:i + 1] = us[i], us[i - 1]
    return us


def tokens(x, b):
    return x[bass.ds(b, 1)].rearrange("o (t p) d -> p (o t) d", p=128)


def layer_norm_stats(nc, dve, y, stats, mv, ve):
    for t in range(QT):
        nc.vector.bn_stats(stats[:, t, :], y[:, t, :])
    dve.drain()
    for t in range(QT):
        nc.vector.bn_aggr(mv[:, t, :], stats[:, t, :])
    dve.drain()
    return nc.vector.tensor_scalar(ve[:], mv[:, :, 1], EPS, None, ALU.add)


def attention8(nc, kind, x_src, x_dst, w, ident, ident16, minus_half, ctx=None):
    cross, rope, chunked = kind == "cross", kind == "rope", kind == "chunked"
    NK = NKC if cross else S
    KT = -(-NK // 128)
    kn = [min(128, NK - 128 * k) for k in range(KT)]
    STEPS = 2 * KT
    LAG = 2
    SCALE = float(DH) ** -0.5
    cuts = [NK * c // 4 for c in range(5)]
    CA = HG * QT * 4 if cross else HG
    kcuts = list(range(0, NK, BANK)) + [NK]
    AB, MB = (3, 2) if cross else (2, 3)
    back = [AB if i >= AB else CA - max(j for j in range(CA) if j % AB == i) + i for i in range(CA)]

    if cross:
        set_x, set_g = [("X",)] + [("C", i) for i in range(4)], [[("Q", g)] + [("K", g, c) for c in range(4)] for g in range(NG)]
        v_uses = [("V", i) for i in range(4)]
        setups = [set_x + set_g[0], set_g[1], v_uses[:2] + set_g[2], v_uses[2:] + set_g[3]]
    elif rope:
        setups = [[("X",), ("Q", 0), ("K", 0)], [("Q", 1), ("K", 1)], [("V",), ("Q", 2), ("K", 2)], [("Q", 3), ("K", 3)]]
    else:
        setups = [[("X",), ("Q", 0), ("Q", 1), ("K", 0), ("K", 1)], [("V", 0), ("V", 1)], [("T", 0), ("T", 1)], []]
    ends = [[], [("EL",)], [], [("EN",)]] if cross else [[], [("EO",)], [("EW",)], [("EN",)]]
    NO_BANK = ("EL", "EN", "A")

    def units(g, first, last):
        u = [] if first else list(ends[g])
        u += [] if last else setups[g]
        if not (last and g == 3):
            u.insert(1 if cross else 0, ("MT", g))
        if not (first and g == 0):
            u.insert(max((len(u) + 1) // 2, len(u) if last else 0), ("FG", g))
        return spread(u, [] if last and g >= 2 else [("A", g, c) for c in range(CA)])

    def bank_uses(us):
        return [u for u in us if u[0] not in NO_BANK]

    def of_body(first, last):
        return bank_uses([u for g in range(NG) for u in units(g, first, last)])

    prologue = [u for s in setups for u in s]
    post = [("FG", 0)] + [u for e in ends for u in e]
    order = UseOrder(MB, prologue + [("MT", 3)], of_body(True, False), of_body(False, False), of_body(False, True), bank_uses(post))
    ready_use = {g: (("K", g, 3) if cross else ("K", g) if rope else ("K", 1)) for g in range(NG)}
    v_use = ("V", 3) if cross else ("V",) if rope else ("T", 1)

    def share(us, s):
        n = len(us)
        return us[n * s // STEPS:n * (s + 1) // STEPS]

    with ExitStack() as c:
        def sb(name, shape, dt=F32):
            return c.enter_context(nc.sbuf_tensor(f"{kind}_{name}", shape, dt))

        def psum(name, shape):
            return c.enter_context(nc.psum_tensor(f"{kind}_{name}", [128] + shape, F32))

        def sem(name):
            return c.enter_context(nc.semaphore(f"{kind}_{name}"))

        def loaded(name, src):
            t = sb(name, list(src.shape))
            loads.append((t, src))
            return t

        loads = []
        if rope:
            wq, wk, wqs, wks = (loaded(n, w[n]) for n in ("wq", "wk", "wqs", "wks"))
            bq, bk, bqs, bks = (loaded(n, w[n]) for n in ("bq", "bk", "bqs", "bks"))
            cos, sin = loaded("cos", w["cos"]), loaded("sin", w["sin"])
        else:
            wq, wk, bq, bk = (loaded(n, w[n]) for n in ("wq", "wk", "bq", "bk"))
        wv, bv = loaded("wv", w["wv"]), loaded("bv", w["bv"])
        lo = loaded("lo", w["lo"])
        if not cross:
            wo, bo = loaded("wo", w["wo"]), loaded("bo", w["bo"])

        psA, psB = psum("scores", [AB, BANK]), psum("scoresT", [2, BANK])
        psO, psM = psum("weighed", [BANK]), psum("shared", [MB, BANK])
        x_in = sb("x_in", [128, 2, QT, 128])
        x_res = sb("x_res", [128, 2, QT, 128])
        x_out = sb("x_out", [128, 2, QT, 128])
        xT = sb("xT", [128, S])
        KO = sb("KO", [128, 2, NG, NK], F16)
        QZ = sb("QZ", [128, 2, H, S], F16)
        VA = sb("VA", [128, 2, KT, H, SLOT])
        P = sb("P", [128, 8, 2, S])
        MX = sb("MX", [128, QT, 128], F16)
        mfull = sb("mfull", [128, QT, HG])
        mpart = sb("mpart", [128, QT, HG, 4])
        hi = sb("hi", [128, 2, BANK] if cross else [128, BANK], F16)
        oT = sb("oT", [128, S])
        O = sb("O", [128, QT, 128])
        rsum = sb("rsum", [128, QT, HG])
        y = sb("y", [128, QT, 128])
        stats = sb("stats", [128, QT, 6])
        mv = sb("mv", [128, QT, 2])
        ve = sb("ve", [128, QT])
        rstd = sb("rstd", [128, QT])
        if not cross:
            OT = sb("OT", [128, S])
        if rope:
            rot = sb("rot", [128, 3, S])
        if cross:
            ctx_in = sb("ctx_in", [128, 2, KT, 128])
            cT = sb("cT", [128, NK])
            lob = sb("lob", [128, NG])
        if chunked:
            xs = sb("xs", [128, BANK])
            VT = sb("VT", [128, NG, S])

        w_ld, init = sem("weights_loaded"), sem("initialised")
        x_ld = [sem(f"x_loaded{i}") for i in range(2)]
        xr_ld = [sem(f"residual_loaded{i}") for i in range(2)]
        c_ld = [sem(f"context_loaded{i}") for i in range(2)]
        st_done = [sem(f"stored{i}") for i in range(2)]
        m_full, m_free = [sem(f"bank_full{i}") for i in range(MB)], [sem(f"bank_free{i}") for i in range(MB)]
        s_full, s_free = sem("scores_full"), sem("scores_maxed")
        t_full, e_done, pv_done = sem("scoresT_full"), sem("exp_done"), sem("pv_done")
        op_ready = sem("operand_ready")
        mx_ready, hi_ready, ot_ready = sem("max_ready"), sem("high_ready"), sem("oT_ready")
        xr_used, ve_ready, rstd_ready, y_ready = sem("residual_used"), sem("var_ready"), sem("rstd_ready"), sem("out_ready")

        def M(use):
            return psM[:, order.bank(use)]

        def full(use):
            return m_full[order.bank(use)]

        def free(use):
            return m_free[order.bank(use)]

        with nc.Block() as block:
            @block.sync
            def _(sp):
                for t, src in loads:
                    sp.dma_start(t[:], src).then_inc(w_ld, 16)
                sp.wait_ge(w_ld, 16 * len(loads))

            @block.vector
            def _(dve):
                nc.vector.memset(QZ[:], 0.0)
                nc.vector.memset(MX[:], 0.0)
                nc.vector.memset(VA[:], 0.0)
                dve.drain()
                nc.vector.memset(VA[:, :, :, :, DH:DH + 1], 1.0)
                if cross:
                    dve.wait_ge(w_ld, 16 * len(loads))
                    nc.vector.tensor_scalar(lob[:], bk[:], lo[:, 0:1], None, ALU.mult)

        with nc.Block() as block:
            @block.sync
            def _(sp):
                def load(b, par):
                    sp.dma_start(x_in[:, par], tokens(x_src, b)).then_inc(x_ld[par], 16)

                def load_ctx(b, par):
                    src = ctx[bass.ds(b, 1)]
                    full = (KT - 1) * 128
                    sp.dma_start(ctx_in[:, par, 0:KT - 1, :],
                                 src[:, 0:full].rearrange("o (k p) d -> p (o k) d", p=128)).then_inc(c_ld[par], 16)
                    sp.dma_start(ctx_in[0:kn[-1], par, KT - 1, :],
                                 src[:, full:NK].rearrange("o p d -> p (o d)")).then_inc(c_ld[par], 16)

                def load_res(b, par):
                    sp.dma_start(x_res[:, par], tokens(x_src, b)).then_inc(xr_ld[par], 16)

                for b in range(2):
                    load(b, b)
                    if cross:
                        load_ctx(b, b)
                    load_res(b, b)

                def store(b, par):
                    sp.wait_ge(y_ready, b + 1)
                    sp.dma_start(tokens(x_dst, b), x_out[:, par]).then_inc(st_done[par], 16)

                def body(b, it, par, first, last):
                    if not (isinstance(b, int) and b >= NB - 2):
                        setup_b = b - 1
                        sp.wait_ge(free(("C", 3) if cross else ("X",)), order.no(setup_b, ("C", 3) if cross else ("X",)) + 1)
                        load(b + 2, par)
                        if cross:
                            load_ctx(b + 2, par)
                    if not first:
                        store(b - 1, 1 - par)
                        if not last:
                            if due(b):
                                sp.wait_ge(xr_used, b)
                            load_res(b + 1, 1 - par)

                over_batches(sp, body)
                store(NB - 1, 1)
                sp.wait_ge(st_done[0], 16 * NB // 2)
                sp.wait_ge(st_done[1], 16 * NB // 2)

            @block.tensor
            def _(pe):
                def begin(b, u):
                    if due(order.no(b, u)):
                        pe.wait_ge(free(u), order.no(b, u))

                def setup(b, bs, its, par, u):
                    begin(b, u)
                    if u[0] in "QKV" and (u[0] == "Q" or not cross):
                        pe.wait_ge(free(("X",)), order.no(b, ("X",)) + 1)
                    if cross and u[0] in "KV":
                        pe.wait_ge(free(("C", u[-1])), order.no(b, ("C", u[-1])) + 1)
                    if u[0] == "X":
                        pe.wait_ge(x_ld[par], its * 16 + 16)
                        for t in range(QT):
                            last = nc.tensor.transpose(M(u)[:, t * 128:t * 128 + 128], x_in[:, par, t, :], ident[:])
                    elif u[0] == "C":
                        if u[1] == 0:
                            pe.wait_ge(c_ld[par], its * 32 + 32)
                        for i, k in enumerate(range(4 * u[1], min(4 * u[1] + 4, KT))):
                            last = nc.tensor.transpose(M(u)[:, i * 128:i * 128 + kn[k]], ctx_in[0:kn[k], par, k, :],
                                                       ident[0:kn[k], 0:kn[k]])
                    elif rope and u[0] in "QK":
                        for i, m in enumerate((wq, wqs) if u[0] == "Q" else (wk, wks)):
                            last = nc.tensor.matmul(M(u)[:, i * S:i * S + S], m[:, u[1] * 128:u[1] * 128 + 128], xT[:],
                                                    start=True, stop=True, skip_group_check=True)
                    elif rope and u[0] == "V":
                        for t in range(QT):
                            last = nc.tensor.matmul(M(u)[:, t * 128:t * 128 + 128], xT[:, t * 128:t * 128 + 128], wv[:],
                                                    start=True, stop=True, skip_group_check=True)
                    elif chunked and u[0] in "QKV":
                        m = {"Q": wq, "K": wk, "V": wv}[u[0]]
                        for i in range(8):
                            for j in range(HG):
                                last = nc.tensor.matmul(M(u)[j * SLOT:(j + 1) * SLOT, i * 64:i * 64 + 64],
                                                        m[:, (8 * u[1] + i) * SLOT:(8 * u[1] + i + 1) * SLOT],
                                                        xT[:, j * 64:j * 64 + 64], start=True, stop=True, skip_group_check=True)
                    elif u[0] == "T":
                        pe.wait_ge(op_ready, bs * 6 + 6)
                        for g in range(NG):
                            last = nc.tensor.transpose(M(u)[:, g * 128:g * 128 + 128], VT[:, g, u[1] * 128:u[1] * 128 + 128], ident[:])
                    elif u[0] == "Q":
                        last = nc.tensor.matmul(M(u)[:, 0:S], wq[:, u[1] * 128:u[1] * 128 + 128], xT[:],
                                                start=True, stop=True, skip_group_check=True)
                    elif u[0] == "K":
                        a, z = kcuts[u[2]], kcuts[u[2] + 1]
                        last = nc.tensor.matmul(M(u)[:, 0:z - a], wk[:, u[1] * 128:u[1] * 128 + 128], cT[:, a:z],
                                                start=True, stop=True, skip_group_check=True)
                    elif u[0] == "V":
                        for i, k in enumerate(range(4 * u[1], min(4 * u[1] + 4, KT))):
                            last = nc.tensor.matmul(M(u)[0:kn[k], i * 128:i * 128 + 128], cT[:, k * 128:k * 128 + kn[k]], wv[:],
                                                    start=True, stop=True, skip_group_check=True)
                    last.then_inc(full(u), 1)

                def scores(G, g, par, ch, setup_at):
                    n = G * CA + ch
                    if ch == 0 and chunked:
                        pe.wait_ge(op_ready, (setup_at + 1) * 6 + 4)
                    elif ch == 0:
                        pe.wait_ge(free(ready_use[g]), order.no(setup_at, ready_use[g]) + 1)
                    if due(n + 1 - back[ch]):
                        pe.wait_ge(s_free, n + 1 - back[ch])
                    out = psA[:, ch % AB]
                    if cross:
                        j, t, k = ch // 8, ch // 4 % 2, ch % 4
                        a, z = cuts[k], cuts[k + 1]
                        last = nc.tensor.matmul(out[:, 0:z - a], QZ[:, par, 4 * g + j, t * 128:t * 128 + 128], KO[:, par, g, a:z],
                                                start=True, stop=True, skip_group_check=True)
                    else:
                        for t in range(QT):
                            last = nc.tensor.matmul(out[:, t * S:t * S + S], QZ[:, par, 4 * g + ch, t * 128:t * 128 + 128],
                                                    KO[:, par, g, :], start=True, stop=True, skip_group_check=True)
                    last.then_inc(s_full, 1)

                def max_rows(b, G, u):
                    pe.wait_ge(mx_ready, G + 1)
                    begin(b, u)
                    for t in range(QT):
                        last = nc.tensor.transpose(M(u)[:, t * 64:t * 64 + 64].bitcast(F16), MX[:, t, :], ident16[:])
                    last.then_inc(full(u), 1)

                def scoresT(b, G, g, par, s):
                    n, kt, i = G * STEPS + s, s // 2, s % 2
                    if s == 0:
                        before = ("MT", (g - 1) % 4)
                        pe.wait_ge(free(before), order.no(b if g else b - 1, before) + 1)
                    if due(n - 1):
                        pe.wait_ge(e_done, n - 1)
                    nc.tensor.matmul(psB[0:kn[kt], i], KO[:, par, g, kt * 128:kt * 128 + kn[kt]],
                                     QZ[:, par, 4 * g + 2 * i:4 * g + 2 * i + 2, :],
                                     start=True, stop=True, skip_group_check=True).then_inc(t_full, 1)

                def weigh(b, G, g, par, s):
                    n, kt, i = G * STEPS + s, s // 2, s % 2
                    if s == 0:
                        if due(G):
                            pe.wait_ge(ot_ready, G)
                        if g == 0:
                            pe.wait_ge(free(v_use), order.no(b - 1, v_use) + 1)
                    pe.wait_ge(e_done, n + 1)
                    for j in (2 * i, 2 * i + 1):
                        last = nc.tensor.matmul(psO[j * SLOT:(j + 1) * SLOT, 0:S],
                                                VA[0:kn[kt], par, kt, 4 * g + j, :], P[0:kn[kt], (g * STEPS + s) % 8, j % 2, :],
                                                start=(kt == 0), stop=(kt == KT - 1), skip_group_check=True)
                    last.then_inc(pv_done, 1)

                def end(b, be, G, u):
                    if u[0] == "FG":
                        pe.wait_ge(ot_ready, G + 1)
                        begin(b, u)
                        for t in range(QT):
                            last = nc.tensor.transpose(M(u)[:, t * 128:t * 128 + 128], oT[:, t * 128:t * 128 + 128], ident[:])
                        last.then_inc(full(u), 1)
                    elif u[0] == "EO":
                        pe.wait_ge(free(("FG", 0)), order.no(b, ("FG", 0)) + 1)
                        begin(b, u)
                        for t in range(QT):
                            last = nc.tensor.transpose(M(u)[:, t * 128:t * 128 + 128], O[:, t, :], ident[:])
                        last.then_inc(full(u), 1)
                    elif u[0] == "EW":
                        pe.wait_ge(free(("EO",)), order.no(b, ("EO",)) + 1)
                        begin(b, u)
                        for t in range(QT):
                            last = nc.tensor.matmul(M(u)[:, t * 128:t * 128 + 128], OT[:, t * 128:t * 128 + 128], wo[:],
                                                    start=True, stop=True, skip_group_check=True)
                        last.then_inc(full(u), 1)

                def unit(b, it, par, u, g):
                    if u[0] == "A":
                        far = g >= 2
                        scores(b * 4 + g + 2, (g + 2) % 4, 1 - par if far else par, u[2], b if far else b - 1)
                    elif u[0] == "MT":
                        max_rows(b, b * 4 + g + 1, u)
                    elif u[0] in ("FG", "EO", "EW"):
                        end(b, b - 1, b * 4 + g - 1, u)
                    elif u[0] not in NO_BANK:
                        setup(b, b + 1, it + par, 1 - par, u)

                for u in prologue:
                    setup(-1, 0, 0, 0, u)
                for ch in range(CA):
                    scores(0, 0, 0, ch, -1)
                max_rows(-1, 0, ("MT", 3))
                for ch in range(CA):
                    scores(1, 1, 0, ch, -1)

                def body(b, it, par, first, last):
                    for g in range(NG):
                        us = units(g, first, last)
                        for s in range(STEPS):
                            scoresT(b, b * 4 + g, g, par, s)
                            if s >= LAG:
                                weigh(b, b * 4 + g, g, par, s - LAG)
                            elif g:
                                weigh(b, b * 4 + g - 1, g - 1, par, STEPS - LAG + s)
                            elif not first:
                                weigh(b - 1, b * 4 - 1, 3, 1 - par, STEPS - LAG + s)
                            for u in share(us, s):
                                unit(b, it, par, u, g)

                over_batches(pe, body)
                for s in range(STEPS - LAG, STEPS):
                    weigh(NB - 1, NB * 4 - 1, 3, 1, s)
                for u in post:
                    end(NB, NB - 1, NB * 4 - 1, u)

            @block.scalar
            def _(act):
                def take(b, u):
                    act.wait_ge(full(u), order.no(b, u) + 1)

                def exps(G, g, s):
                    n, kt = G * STEPS + s, s // 2
                    act.wait_ge(t_full, n + 1)
                    if due(n - 7):
                        act.wait_ge(pv_done, n - 7)
                    nc.scalar.activation(P[0:kn[kt], (g * STEPS + s) % 8].rearrange("p j q -> p (j q)"), psB[0:kn[kt], s % 2],
                                         ACT.Exp, scale=SCALE).then_inc(e_done, 1)

                def copy_out(b, G, g):
                    if due(G * STEPS):
                        act.wait_ge(pv_done, G * STEPS)
                    if not (isinstance(b, int) and b == 0 and g == 1):
                        act.wait_ge(full(("FG", (g - 1) % 4)), order.no(b if g else b - 1, ("FG", (g - 1) % 4)) + 1)
                    nc.scalar.activation(oT[:], psO[:, 0:S], ACT.Copy).then_inc(ot_ready, 1)

                def unit(b, be, G, u):
                    if u[0] == "X":
                        take(b, u)
                        if chunked:
                            nc.scalar.activation(xT[:].rearrange("d (j g t) -> d g j t", j=HG, g=NG),
                                                 M(u)[:, 0:S].rearrange("d (g j t) -> d g j t", j=HG, g=NG),
                                                 ACT.Copy).then_inc(free(u), 1)
                        else:
                            nc.scalar.activation(xT[:], M(u)[:, 0:S], ACT.Copy).then_inc(free(u), 1)
                    elif u[0] == "C":
                        take(b, u)
                        a, z = kcuts[u[1]], kcuts[u[1] + 1]
                        nc.scalar.activation(cT[:, a:z], M(u)[:, 0:z - a], ACT.Copy).then_inc(free(u), 1)
                    elif u[0] == "K" and cross:
                        take(b, u)
                        a, z = kcuts[u[2]], kcuts[u[2] + 1]
                        before = ("K", u[1], u[2] - 2) if u[2] >= 2 else ("K", (u[1] - 1) % 4, u[2] + 2)
                        if not (isinstance(b, int) and b == -1 and u[1] == 0 and u[2] < 2):
                            act.wait_ge(free(before), order.no(b - 1 if u[1] == 0 and u[2] < 2 else b, before) + 1)
                        nc.scalar.activation(hi[:, u[2] % 2, 0:z - a], M(u)[:, 0:z - a], ACT.Identity, scale=lo[:, 0:1],
                                             bias=lob[:, u[1]:u[1] + 1]).then_inc(hi_ready, 1)
                    elif u[0] == "T":
                        take(b, u)
                        nc.scalar.activation(VA[:, parity[0], u[1]].rearrange("k h s -> k (h s)"), M(u),
                                             ACT.Copy).then_inc(free(u), 1)
                    elif u[0] == "EO":
                        take(b, u)
                        nc.scalar.activation(OT[:], M(u)[:, 0:S], ACT.Copy).then_inc(free(u), 1)

                parity = [0]
                for u in prologue:
                    unit(-1, 0, 0, u)

                def body(b, it, par, first, last):
                    parity[0] = 1 - par
                    for g in range(NG):
                        us = units(g, first, last)
                        for s in range(STEPS):
                            exps(b * 4 + g, g, s)
                            if s == LAG - 1 and not (first and g == 0):
                                copy_out(b, b * 4 + g, g)
                            for u in share(us, s):
                                unit(b, b - 1, b * 4 + g - 1, u)

                over_batches(act, body)
                copy_out(NB, NB * 4, 0)
                for u in post:
                    unit(NB, NB - 1, NB * 4 - 1, u)

            @block.gpsimd
            def _(pool):
                def body(b, it, par, first, last):
                    pool.wait_ge(ve_ready, b + 1)
                    nc.gpsimd.tensor_tensor(rstd[:], ve[:], minus_half[:, 0:QT], ALU.pow).then_inc(rstd_ready, 1)
                over_batches(pool, body)

            @block.vector
            def _(dve):
                def take(b, u):
                    dve.wait_ge(full(u), order.no(b, u) + 1)

                def setup(b, par, u):
                    if u[0] == "Q" and not chunked or u[0] == "K" and rope:
                        take(b, u)
                        g, isk = u[1], u[0] == "K"
                        if rope:
                            bias, biass = (bk, bks) if isk else (bq, bqs)
                            nc.vector.scalar_tensor_tensor(out=rot[:, 0], in0=M(u)[:, 0:S], scalar=bias[:, g:g + 1], in1=cos[:],
                                                           op0=ALU.add, op1=ALU.mult)
                            nc.vector.scalar_tensor_tensor(out=rot[:, 1], in0=M(u)[:, S:2 * S], scalar=biass[:, g:g + 1],
                                                           in1=sin[:], op0=ALU.add, op1=ALU.mult)
                            dve.drain()
                            nc.vector.tensor_tensor(rot[:, 2], rot[:, 0], rot[:, 1], ALU.add)
                            dve.drain()
                            col = 0 if isk else 1
                            nc.vector.tensor_scalar(hi[:, 0:S], rot[:, 2], lo[:, col:col + 1], None, ALU.mult)
                            dve.drain()
                            if isk:
                                nc.vector.tensor_tensor(KO[:, par, g, :], rot[:, 2], hi[:, 0:S], ALU.subtract).then_inc(free(u), 1)
                            else:
                                for j in range(HG):
                                    r = slice(j * SLOT, (j + 1) * SLOT)
                                    last = nc.vector.tensor_tensor(QZ[r, par, 4 * g + j, :], rot[r, 2], hi[r, 0:S], ALU.subtract)
                                dve.drain().then_inc(free(u), 1)
                        else:
                            nc.vector.tensor_scalar(hi2[:, 0:S], M(u)[:, 0:S], bq[:, g:g + 1], lo[:, 1:2], ALU.add, ALU.mult)
                            dve.drain()
                            for j in range(HG):
                                r = slice(j * SLOT, (j + 1) * SLOT)
                                nc.vector.scalar_tensor_tensor(out=QZ[r, par, 4 * g + j, :], in0=M(u)[r, 0:S],
                                                               scalar=bq[r, g:g + 1], in1=hi2[r, 0:S],
                                                               op0=ALU.add, op1=ALU.subtract)
                            dve.drain().then_inc(free(u), 1)
                    elif u[0] == "K" and cross:
                        take(b, u)
                        dve.wait_ge(hi_ready, hi_no(b, u) + 1)
                        a, z = kcuts[u[2]], kcuts[u[2] + 1]
                        nc.vector.scalar_tensor_tensor(out=KO[:, par, u[1], a:z], in0=M(u)[:, 0:z - a],
                                                       scalar=bk[:, u[1]:u[1] + 1], in1=hi[:, u[2] % 2, 0:z - a],
                                                       op0=ALU.add, op1=ALU.subtract).then_inc(free(u), 1)
                    elif u[0] in "QKV" and chunked:
                        take(b, u)
                        bias = {"Q": bq, "K": bk, "V": bv}[u[0]]
                        cs = slice(8 * u[1], 8 * u[1] + 8)
                        cgt = "r (c g t) -> r c g t"
                        vals = M(u).rearrange("r (c q) -> r c q", c=8)
                        b_ = bias[:, cs].unsqueeze(2).to_broadcast([128, 8, 64])
                        nc.vector.tensor_tensor(xs[:].rearrange("r (c q) -> r c q", c=8), vals, b_, ALU.add)
                        dve.drain().then_inc(free(u), 1)
                        if u[0] != "V":
                            col = 0 if u[0] == "K" else 1
                            nc.vector.tensor_scalar(hi[:], xs[:], lo[:, col:col + 1], None, ALU.mult)
                            dve.drain()
                        x_ = xs[:].rearrange(cgt, c=8, g=NG)
                        h_ = hi[:].rearrange(cgt, c=8, g=NG)
                        if u[0] == "V":
                            nc.vector.tensor_copy(VT[:].rearrange("r g (t c) -> r c g t", c=16)[:, cs], x_)
                        elif u[0] == "K":
                            nc.vector.tensor_tensor(KO[:, par].rearrange("r g (t c) -> r c g t", c=16)[:, cs], x_, h_, ALU.subtract)
                        else:
                            for j in range(HG):
                                r = slice(j * SLOT, (j + 1) * SLOT)
                                nc.vector.tensor_tensor(
                                    QZ[r, par].rearrange("r (g j) (t c) -> r c g j t", j=HG, c=16)[:, cs, :, j, :],
                                    x_[r], h_[r], ALU.subtract)
                        dve.drain().then_inc(op_ready, 1)
                    elif u[0] == "V" and not chunked:
                        take(b, u)
                        if rope:
                            nc.vector.tensor_tensor(VA[:, par].rearrange("k t h s -> k (t h) s")[:, :, 0:DH],
                                                    M(u)[:, 0:QT * 128].rearrange("k (a s) -> k a s", s=DH),
                                                    bv[:].rearrange("k (a s) -> k a s", s=DH), ALU.add).then_inc(free(u), 1)
                        else:
                            ks = range(4 * u[1], min(4 * u[1] + 4, KT))
                            n, r = len(ks), kn[ks[-1]]
                            nc.vector.tensor_tensor(
                                VA[0:r, par, ks[0]:ks[-1] + 1].rearrange("k t h s -> k (t h) s")[:, :, 0:DH],
                                M(u)[0:r, 0:n * 128].rearrange("k (a s) -> k a s", s=DH),
                                bv[0:r, 0:n * 128].rearrange("k (a s) -> k a s", s=DH), ALU.add).then_inc(free(u), 1)

                def hi_no(b, u):
                    at = [x for x in prologue if x[0] == "K"].index(u)
                    return (b + 1) * 16 + at

                def maxima(G, ch):
                    n = G * CA + ch
                    if ch == 0:
                        if due(G):
                            dve.wait_ge(mx_ready, G)
                    dve.wait_ge(s_full, n + 1)
                    if cross:
                        j, t, k = ch // 8, ch // 4 % 2, ch % 4
                        nc.vector.tensor_reduce(mpart[:, t, j, k:k + 1], psA[:, ch % AB, 0:cuts[k + 1] - cuts[k]],
                                                AX.X, ALU.max).then_inc(s_free, 1)
                    else:
                        nc.vector.tensor_reduce(mfull[:, :, ch], psA[:, ch % AB].rearrange("p (t k) -> p t k", t=QT),
                                                AX.X, ALU.max).then_inc(s_free, 1)
                    if ch == CA - 1:
                        if cross:
                            dve.drain()
                            nc.vector.tensor_reduce(mfull[:], mpart[:], AX.X, ALU.max)
                        cols = MX[:].rearrange("p t (j s) -> p t j s", s=SLOT)
                        dve.drain()
                        nc.vector.tensor_scalar(cols[:, :, :, M_ROW], mfull[:], -1.0, None, ALU.mult)
                        dve.drain()
                        nc.vector.scalar_tensor_tensor(out=cols[:, :, :, M_ROW + 1], in0=mfull[:], scalar=-1.0,
                                                       in1=cols[:, :, :, M_ROW], op0=ALU.mult,
                                                       op1=ALU.subtract).then_inc(mx_ready, 1)

                def add_max(b, g, par, u):
                    take(b, u)
                    for j in range(HG):
                        r = slice(j * SLOT, (j + 1) * SLOT)
                        nc.vector.tensor_tensor(QZ[r, par, 4 * g + j, :], M(u)[r, 0:S // 2].bitcast(F16),
                                                QZ[r, par, 4 * g + j, :], ALU.add)
                    dve.drain().then_inc(free(u), 1)

                def end(b, be, G, gg, it, par, u):
                    if u[0] == "FG":
                        take(b, u)
                        rows = M(u)[:, 0:S].rearrange("p (t j s) -> p t j s", t=QT, j=HG)
                        nc.vector.reciprocal(rsum[:], rows[:, :, :, DH])
                        dve.drain()
                        for t in range(QT):
                            last = nc.vector.tensor_tensor(
                                O[:, t, gg * 32:gg * 32 + 32].rearrange("p (j d) -> p j d", j=HG), rows[:, t, :, 0:DH],
                                rsum[:, t, :].unsqueeze(2).to_broadcast([128, HG, DH]), ALU.mult)
                        dve.drain().then_inc(free(u), 1)
                    elif u[0] in ("EW", "EL"):
                        dve.wait_ge(xr_ld[par], it * 16 + 16)
                        if u[0] == "EW":
                            take(b, u)
                            nc.vector.tensor_tensor(y[:], M(u)[:, 0:S].rearrange("p (t d) -> p t d", t=QT), bo[:], ALU.add)
                            dve.drain().then_inc(free(u), 1)
                            nc.vector.tensor_tensor(y[:], y[:], x_res[:, par], ALU.add)
                        else:
                            nc.vector.tensor_tensor(y[:], O[:], x_res[:, par], ALU.add)
                        dve.drain().then_inc(xr_used, 1)
                        layer_norm_stats(nc, dve, y, stats, mv, ve).then_inc(ve_ready, 1)
                    elif u[0] == "EN":
                        dve.wait_ge(rstd_ready, be + 1)
                        if due(it * 16):
                            dve.wait_ge(st_done[par], it * 16)
                        for t in range(QT):
                            nc.vector.tensor_scalar(x_out[:, par, t, :], y[:, t, :], mv[:, t, 0:1], rstd[:, t:t + 1],
                                                    ALU.subtract, ALU.mult)
                        dve.drain().then_inc(y_ready, 1)

                hi2 = sb("hi2", [128, S], F16) if cross else None
                for u in prologue:
                    setup(-1, 0, u)
                for ch in range(CA):
                    maxima(0, ch)
                add_max(-1, 0, 0, ("MT", 3))
                for ch in range(CA):
                    maxima(1, ch)

                def body(b, it, par, first, last):
                    for g in range(NG):
                        for u in delayed(units(g, first, last)):
                            if u[0] == "A":
                                maxima(b * 4 + g + 2, u[2])
                            elif u[0] == "MT":
                                add_max(b, (g + 1) % 4, 1 - par if g == 3 else par, u)
                            elif u[0] in ("FG", "EW", "EL", "EN"):
                                end(b, b - 1, b * 4 + g - 1, (g - 1) % 4, it - 1 + par, 1 - par, u)
                            elif u[0] != "EO":
                                setup(b, 1 - par, u)

                over_batches(dve, body)
                for u in post:
                    end(NB, NB - 1, NB * 4 - 1, 3, NB // 2 - 1, 1, u)


def cross64(nc, x_src, x_dst, w, ident, ident16, minus_half, ctx):
    NK, DQ, NP, HB = NKC, 64, 8, 2
    KT = -(-NK // 128)
    kn = [min(128, NK - 128 * k) for k in range(KT)]
    LAG = 2
    SCALE = float(DQ) ** -0.5
    cuts = [NK * c // 4 for c in range(5)]
    CA = HB * QT * 4
    kcuts = list(range(0, NK, BANK)) + [NK]
    AB, MB = 2, 3
    back = [AB if i >= AB else CA - max(j for j in range(CA) if j % AB == i) + i for i in range(CA)]
    VS = [[0, 4, 7, 10, 13], [0, 5, 9, 13]]

    xc = [("X",)] + [("C", i) for i in range(4)]
    kq = [[("Q", p)] + [("K", p, c) for c in range(4)] for p in range(NP)]
    v1 = [[("V", 1, k) for k in range(VS[0][i], VS[0][i + 1])] for i in range(4)]
    v0 = [[("V", 0, k) for k in range(VS[1][i], VS[1][i + 1])] for i in range(3)]
    ends = [[], [("EW",)], [], [("EN",)], [("FT",)], [("FW",)], [], [("FN",)]]
    NO_BANK = ("EN", "FN", "A", "C2")

    def units(p, first, last):
        u = [] if first else list(ends[p])
        u += xc if p == 5 and not last else []
        values = v1[p] if p < 4 else v0[p - 5] if p >= 5 and not last else []
        u += mixed(values, [] if last and p >= 5 else kq[(p + 3) % 8])
        if not (first and p == 0):
            u.insert(len(u) * 2 // 3, ("FG", p))
        if not (last and p == 7):
            u[1:1] = [("MT", p), ("C2", p)]
        return spread(u, [] if last and p >= 6 else [("A", p, c) for c in range(CA)])

    def bank_uses(us):
        return [u for u in us if u[0] not in NO_BANK]

    def of_body(first, last):
        return bank_uses([u for p in range(NP) for u in units(p, first, last)])

    prologue = xc + kq[0] + kq[1] + kq[2] + v0[0] + v0[1] + v0[2]
    post = [("FG", 0)] + [u for e in ends for u in e]
    order = UseOrder(MB, prologue + [("MT", 7)], of_body(True, False), of_body(False, False), of_body(False, True), bank_uses(post))

    def over(eng, body):
        body(0, True, False)
        with eng.Fori(1, NB - 1) as b:
            body(b, False, False)
        body(NB - 1, False, True)

    def share(us, k):
        n = len(us)
        return us[n * k // KT:n * (k + 1) // KT]

    with ExitStack() as cx:
        def sb(name, shape, dt=F32):
            return cx.enter_context(nc.sbuf_tensor(f"wide_{name}", shape, dt))

        def psum(name, shape):
            return cx.enter_context(nc.psum_tensor(f"wide_{name}", [128] + shape, F32))

        def sem(name):
            return cx.enter_context(nc.semaphore(f"wide_{name}"))

        def loaded(name, src):
            t = sb(name, list(src.shape))
            loads.append((t, src))
            return t

        loads = []
        wq, wk, wv, wo, bo, wf, dd = (loaded(n, w[n]) for n in ("wq", "wk", "wv", "wo", "bo", "wf", "dd"))
        psA, psB = psum("scores", [AB, BANK]), psum("scoresT", [2, BANK])
        psO, psM = psum("weighed", [BANK]), psum("shared", [MB, BANK])
        x_in = sb("x_in", [128, QT, 128])
        x_res = sb("x_res", [128, QT, 128])
        x_out = sb("x_out", [128, QT, 128])
        x1 = sb("x1", [128, QT, 128])
        x1T = sb("x1T", [128, S])
        xT = sb("xT", [128, S])
        ctx_in = sb("ctx_in", [128, KT, 128])
        cT = sb("cT", [128, NK])
        V = sb("V", [128, KT, H * DQ])
        K1 = sb("K1", [128, 4, HB, NK], F16)
        K2 = sb("K2", [128, 2, HB, NK], F16)
        Q1 = sb("Q1", [128, 4, HB, S], F16)
        Q2 = sb("Q2", [128, 4, HB, S], F16)
        qh = sb("qh", [128, S], F16)
        P = sb("P", [128, 8, HB, S])
        acc = sb("acc", [128, 2, HB * S])
        MX = sb("MX", [128, QT, 128], F16)
        mpart = sb("mpart", [128, QT, HB, 4])
        mfull = sb("mfull", [128, QT, HB])
        ones = sb("ones", [128, DQ])
        oT = sb("oT", [128, S])
        rsum = sb("rsum", [128, S])
        ON = sb("ON", [128, NP, S])
        y = sb("y", [128, QT, 128])
        stats = sb("stats", [128, QT, 6])
        mv = sb("mv", [128, QT, 2])
        ve = sb("ve", [128, QT])
        rstd = sb("rstd", [128, QT])

        w_ld, started = sem("weights_loaded"), sem("started")
        x_ld, xr_ld, c_ld, st_done = sem("x_loaded"), sem("residual_loaded"), sem("context_loaded"), sem("stored")
        m_full, m_free = [sem(f"bank_full{i}") for i in range(MB)], [sem(f"bank_free{i}") for i in range(MB)]
        s_full, s_free = sem("scores_full"), sem("scores_maxed")
        t_full, e_done, pv_done = sem("scoresT_full"), sem("exp_done"), sem("pv_done")
        p_summed = sem("p_summed")
        mx_ready, hi_ready, ot_ready, k2_ready = sem("max_ready"), sem("high_ready"), sem("oT_ready"), sem("k2_ready")
        x1_ready = sem("x1_ready")
        xr_used, ve_ready, rstd_ready, y_ready = sem("residual_used"), sem("var_ready"), sem("rstd_ready"), sem("out_ready")

        def M(use):
            return psM[:, order.bank(use)]

        def full(use):
            return m_full[order.bank(use)]

        def free(use):
            return m_free[order.bank(use)]

        with nc.Block() as block:
            @block.sync
            def _(sp):
                for t, src in loads:
                    sp.dma_start(t[:], src).then_inc(w_ld, 16)
                sp.wait_ge(w_ld, 16 * len(loads))

            @block.vector
            def _(dve):
                nc.vector.memset(Q2[:], 0.0)
                nc.vector.memset(MX[:], 0.0)
                nc.vector.memset(ones[:], 1.0)
                nc.vector.memset(K2[:], 0.0)
                dve.drain()
                nc.vector.memset(K2[DQ:DQ + 2, :, 0, :], 1.0)
                nc.vector.memset(K2[0:2, :, 1, :], 1.0)
                dve.drain().then_inc(started, 1)

        with nc.Block() as block:
            @block.sync
            def _(sp):
                def load(b):
                    sp.dma_start(x_in[:], tokens(x_src, b)).then_inc(x_ld, 16)
                    src = ctx[bass.ds(b, 1)]
                    full = (KT - 1) * 128
                    sp.dma_start(ctx_in[:, 0:KT - 1, :],
                                 src[:, 0:full].rearrange("o (k p) d -> p (o k) d", p=128)).then_inc(c_ld, 16)
                    sp.dma_start(ctx_in[0:kn[-1], KT - 1, :],
                                 src[:, full:NK].rearrange("o p d -> p (o d)")).then_inc(c_ld, 16)

                def load_res(b):
                    sp.dma_start(x_res[:], tokens(x_src, b)).then_inc(xr_ld, 16)

                def store(b):
                    sp.wait_ge(y_ready, b + 1)
                    sp.dma_start(tokens(x_dst, b), x_out[:]).then_inc(st_done, 16)

                load(0)
                load_res(0)

                def body(b, first, last):
                    if not last:
                        sp.wait_ge(free(("C", 3)), order.no(b - 1, ("C", 3)) + 1)
                        load(b + 1)
                    if not first:
                        if due(b):
                            sp.wait_ge(xr_used, b)
                        load_res(b)
                        store(b - 1)

                over(sp, body)
                store(NB - 1)
                sp.wait_ge(st_done, 16 * NB)

            @block.tensor
            def _(pe):
                def begin(b, u):
                    if due(order.no(b, u)):
                        pe.wait_ge(free(u), order.no(b, u))

                def setup(b, bs, u):
                    begin(b, u)
                    if u[0] == "X":
                        pe.wait_ge(x_ld, bs * 16 + 16)
                        for t in range(QT):
                            last = nc.tensor.transpose(M(u)[:, t * 128:t * 128 + 128], x_in[:, t, :], ident[:])
                    elif u[0] == "C":
                        if u[1] == 0:
                            pe.wait_ge(c_ld, bs * 32 + 32)
                        for i, k in enumerate(range(4 * u[1], min(4 * u[1] + 4, KT))):
                            last = nc.tensor.transpose(M(u)[:, i * 128:i * 128 + kn[k]], ctx_in[0:kn[k], k, :],
                                                       ident[0:kn[k], 0:kn[k]])
                    elif u[0] == "Q":
                        if u[1] == 0:
                            pe.wait_ge(free(("X",)), order.no(b, ("X",)) + 1)
                        last = nc.tensor.matmul(M(u)[:, 0:S], wq[:, u[1] * 128:u[1] * 128 + 128], xT[:],
                                                start=True, stop=True, skip_group_check=True)
                    elif u[0] == "K":
                        a, z = kcuts[u[2]], kcuts[u[2] + 1]
                        if u[1] == 0:
                            pe.wait_ge(free(("C", u[2])), order.no(b, ("C", u[2])) + 1)
                        last = nc.tensor.matmul(M(u)[:, 0:z - a], wk[:, u[1] * 128:u[1] * 128 + 128], cT[:, a:z],
                                                start=True, stop=True, skip_group_check=True)
                    elif u[0] == "V":
                        k = u[2]
                        if u[1] == 0:
                            pe.wait_ge(free(("C", k // 4)), order.no(b, ("C", k // 4)) + 1)
                        last = nc.tensor.matmul(M(u)[0:kn[k], :], cT[:, k * 128:k * 128 + kn[k]], wv[:, u[1] * 512:u[1] * 512 + 512],
                                                start=True, stop=True, skip_group_check=True)
                    last.then_inc(full(u), 1)

                def scores(G, p, ch, at, use):
                    n = G * CA + ch
                    if ch == 0:
                        pe.wait_ge(free(use), order.no(at, use) + 1)
                    if due(n + 1 - back[ch]):
                        pe.wait_ge(s_free, n + 1 - back[ch])
                    i, t, k = ch // 8, ch // 4 % 2, ch % 4
                    a, z = cuts[k], cuts[k + 1]
                    nc.tensor.matmul(psA[:, ch % AB, 0:z - a], Q1[:, p % 4, i, t * 128:t * 128 + 128], K1[:, p % 4, i, a:z],
                                     start=True, stop=True, skip_group_check=True).then_inc(s_full, 1)

                def max_rows(b, G, u):
                    pe.wait_ge(mx_ready, G + 1)
                    begin(b, u)
                    for t in range(QT):
                        last = nc.tensor.transpose(M(u)[:, t * 64:t * 64 + 64].bitcast(F16), MX[:, t, :], ident16[:])
                    last.then_inc(full(u), 1)

                def scoresT(b, G, p, k):
                    n = G * KT + k
                    if k == 0:
                        pe.wait_ge(free(("MT", (p - 1) % 8)), order.no(b if p else b - 1, ("MT", (p - 1) % 8)) + 1)
                        pe.wait_ge(k2_ready, G + 1)
                    if due(n - 1):
                        pe.wait_ge(e_done, n - 1)
                    ks = slice(k * 128, k * 128 + kn[k])
                    for i in range(HB):
                        out = psB[0:kn[k], (p * KT + k) % 2, i * S:i * S + S]
                        nc.tensor.matmul(out, K1[:, p % 4, i, ks], Q1[:, p % 4, i, :], start=True, stop=False, skip_group_check=True)
                        last = nc.tensor.matmul(out, K2[:, p % 2, i, ks], Q2[:, p % 4, i, :], start=False, stop=True,
                                                skip_group_check=True)
                    last.then_inc(t_full, 1)

                def weigh(b, G, p, k):
                    if k == 0:
                        if due(G):
                            pe.wait_ge(ot_ready, G)
                        if p in (0, 4):
                            v_use = ("V", p // 4, KT - 1)
                            pe.wait_ge(free(v_use), order.no(b if p else b - 1, v_use) + 1)
                    pe.wait_ge(e_done, G * KT + k + 1)
                    pe.wait_ge(started, 1)
                    for i in range(HB):
                        last = nc.tensor.matmul(psO[i * DQ:(i + 1) * DQ, 0:S], V[0:kn[k], k, (2 * p + i) * DQ:(2 * p + i + 1) * DQ],
                                                P[0:kn[k], (p * KT + k) % 8, i, :], start=(k == 0), stop=(k == KT - 1),
                                                skip_group_check=True)
                    last.then_inc(pv_done, 1)

                def end(b, G, u):
                    if u[0] == "FG":
                        pe.wait_ge(p_summed, G * KT + KT)
                        begin(b, u)
                        pe.wait_ge(started, 1)
                        for i in range(HB):
                            last = nc.tensor.matmul(M(u)[i * DQ:(i + 1) * DQ, 0:S], ones[:], acc[:, (u[1] - 1) % 2, i * S:i * S + S],
                                                    start=True, stop=True, skip_group_check=True)
                        last.then_inc(full(u), 1)
                    elif u[0] == "EW":
                        pe.wait_ge(free(("FG", 0)), order.no(b, ("FG", 0)) + 1)
                        begin(b, u)
                        for t in range(QT):
                            for p in range(NP):
                                last = nc.tensor.matmul(M(u)[:, t * 128:t * 128 + 128], ON[:, p, t * 128:t * 128 + 128], wo[:, p, :],
                                                        start=(p == 0), stop=(p == NP - 1), skip_group_check=True)
                        last.then_inc(full(u), 1)
                    elif u[0] == "FT":
                        if due(b):
                            pe.wait_ge(x1_ready, b)
                        begin(b, u)
                        for t in range(QT):
                            last = nc.tensor.transpose(M(u)[:, t * 128:t * 128 + 128], x1[:, t, :], ident[:])
                        last.then_inc(full(u), 1)
                    elif u[0] == "FW":
                        pe.wait_ge(free(("FT",)), order.no(b, ("FT",)) + 1)
                        begin(b, u)
                        for t in range(QT):
                            for m in (wf, dd):
                                last = nc.tensor.matmul(M(u)[:, t * 128:t * 128 + 128], x1T[:, t * 128:t * 128 + 128], m[:],
                                                        start=(m is wf), stop=(m is dd), skip_group_check=True)
                        last.then_inc(full(u), 1)

                def unit(b, p, u):
                    if u[0] == "A":
                        q = (p + 2) % 8
                        at = b if p else b - 1
                        scores(b * 8 + p + 2, q, u[2], at, ("K", q, 3))
                    elif u[0] == "MT":
                        max_rows(b, b * 8 + p + 1, u)
                    elif u[0] in ("FG", "EW", "FT", "FW"):
                        end(b, b * 8 + p - 1, u)
                    elif u[0] not in NO_BANK:
                        setup(b, b + 1 if u[0] in "XC" else 0, u)

                for u in prologue:
                    setup(-1, 0, u)
                for ch in range(CA):
                    scores(0, 0, ch, -1, ("K", 0, 3))
                max_rows(-1, 0, ("MT", 7))
                for ch in range(CA):
                    scores(1, 1, ch, -1, ("K", 1, 3))

                def body(b, first, last):
                    for p in range(NP):
                        us = units(p, first, last)
                        for k in range(KT):
                            scoresT(b, b * 8 + p, p, k)
                            if k >= LAG:
                                weigh(b, b * 8 + p, p, k - LAG)
                            elif not (first and p == 0):
                                weigh(b if p else b - 1, b * 8 + p - 1, (p - 1) % 8, KT - LAG + k)
                            for u in share(us, k):
                                unit(b, p, u)

                over(pe, body)
                for k in range(KT - LAG, KT):
                    weigh(NB - 1, NB * 8 - 1, 7, k)
                for u in post:
                    end(NB, NB * 8 - 1, u)

            @block.scalar
            def _(act):
                def take(b, u):
                    act.wait_ge(full(u), order.no(b, u) + 1)

                def exps(G, p, k):
                    n = G * KT + k
                    act.wait_ge(t_full, n + 1)
                    if due(n - 7):
                        act.wait_ge(pv_done, n - 7)
                    if due(n - 7):
                        act.wait_ge(p_summed, n - 7)
                    nc.scalar.activation(P[0:kn[k], (p * KT + k) % 8].rearrange("k i q -> k (i q)"), psB[0:kn[k], (p * KT + k) % 2],
                                         ACT.Exp, scale=SCALE).then_inc(e_done, 1)

                def copy_out(b, G, p):
                    if due(G * KT):
                        act.wait_ge(pv_done, G * KT)
                    if not (isinstance(b, int) and b == 0 and p == 1):
                        act.wait_ge(free(("FG", (p - 1) % 8)), order.no(b if p else b - 1, ("FG", (p - 1) % 8)) + 1)
                    nc.scalar.activation(oT[:], psO[:, 0:S], ACT.Copy).then_inc(ot_ready, 1)

                def unit(b, u):
                    if u[0] == "X":
                        take(b, u)
                        nc.scalar.activation(xT[:], M(u)[:, 0:S], ACT.Copy).then_inc(free(u), 1)
                    elif u[0] == "FT":
                        take(b, u)
                        nc.scalar.activation(x1T[:], M(u)[:, 0:S], ACT.Copy).then_inc(free(u), 1)
                    elif u[0] == "C":
                        take(b, u)
                        a, z = kcuts[u[1]], kcuts[u[1] + 1]
                        nc.scalar.activation(cT[:, a:z], M(u)[:, 0:z - a], ACT.Copy).then_inc(free(u), 1)
                    elif u[0] == "K":
                        take(b, u)
                        a, z = kcuts[u[2]], kcuts[u[2] + 1]
                        for i in range(HB):
                            r = slice(i * DQ, (i + 1) * DQ)
                            last = nc.scalar.activation(K1[r, u[1] % 4, i, a:z], M(u)[r, 0:z - a], ACT.Copy)
                        act.drain().then_inc(hi_ready, 1)
                    elif u[0] == "V":
                        take(b, u)
                        k = u[2]
                        nc.scalar.activation(V[0:kn[k], k, u[1] * 512:u[1] * 512 + 512], M(u)[0:kn[k], :], ACT.Copy).then_inc(free(u), 1)

                for u in prologue:
                    unit(-1, u)

                def body(b, first, last):
                    for p in range(NP):
                        us = units(p, first, last)
                        for k in range(KT):
                            exps(b * 8 + p, p, k)
                            if k == LAG - 1 and not (first and p == 0):
                                copy_out(b, b * 8 + p, p)
                            for u in share(us, k):
                                unit(b, u)

                over(act, body)
                copy_out(NB, NB * 8, 0)
                for u in post:
                    unit(NB, u)

            @block.gpsimd
            def _(pool):
                def sums(b, G, p, k):
                    pool.wait_ge(e_done, G * KT + k + 1)
                    out, r = acc[:, p % 2, :], p * KT + k

                    def tile(r):
                        return P[:, r % 8].rearrange("k i q -> k (i q)")
                    if k == 1:
                        if not (isinstance(b, int) and b == 0 and p < 2):
                            use = ("FG", (p - 1) % 8)
                            pool.wait_ge(full(use), order.no(b if p >= 1 else b - 1, use) + 1)
                        nc.gpsimd.tensor_tensor(out, tile(r - 1), tile(r), ALU.add).then_inc(p_summed, 2)
                    else:
                        pool.wait_ge(p_summed, G * KT + k)
                        nc.gpsimd.tensor_tensor(out[0:kn[k]], out[0:kn[k]], tile(r)[0:kn[k]], ALU.add).then_inc(p_summed, 1)

                def root(n):
                    if due(n):
                        pool.wait_ge(ve_ready, n)
                    nc.gpsimd.tensor_tensor(rstd[:], ve[:], minus_half[:, 0:QT], ALU.pow).then_inc(rstd_ready, 1)

                def body(b, first, last):
                    for p in range(NP):
                        if not first and p == 2:
                            root(b * 2 - 1)
                        if not first and p == 6:
                            root(b * 2)
                        for k in range(1, KT):
                            sums(b, b * 8 + p, p, k)

                over(pool, body)
                root(NB * 2 - 1)
                root(NB * 2)

            @block.vector
            def _(dve):
                def take(b, u):
                    dve.wait_ge(full(u), order.no(b, u) + 1)

                def hi_no(bs, u):
                    return bs * 32 + u[1] * 4 + u[2] + 1

                def setup(b, bs, u):
                    if u[0] == "Q":
                        take(b, u)
                        p = u[1]
                        nc.vector.tensor_copy(qh[:], M(u)[:, 0:S])
                        dve.drain()
                        for i in range(HB):
                            r, o = slice(i * DQ, (i + 1) * DQ), slice((1 - i) * DQ, (2 - i) * DQ)
                            nc.vector.tensor_tensor(Q2[r, p % 4, i, :], M(u)[r, 0:S], qh[r, :], ALU.subtract)
                            nc.vector.tensor_copy(Q1[r, p % 4, i, :], qh[r, :])
                            nc.vector.tensor_copy(Q1[o, p % 4, i, :], qh[r, :])
                        dve.drain().then_inc(free(u), 1)
                    elif u[0] == "K":
                        take(b, u)
                        if due(hi_no(bs, u)):
                            dve.wait_ge(hi_ready, hi_no(bs, u))
                        a, z = kcuts[u[2]], kcuts[u[2] + 1]
                        for i in range(HB):
                            r, o = slice(i * DQ, (i + 1) * DQ), slice((1 - i) * DQ, (2 - i) * DQ)
                            nc.vector.tensor_tensor(K1[o, u[1] % 4, i, a:z], M(u)[r, 0:z - a], K1[r, u[1] % 4, i, a:z], ALU.subtract)
                        dve.drain().then_inc(free(u), 1)

                def copy_high(G, p):
                    if due((G - 1) * KT):
                        dve.wait_ge(t_full, (G - 1) * KT)
                    for i in range(HB):
                        r = slice(i * DQ, (i + 1) * DQ)
                        nc.vector.tensor_copy(K2[r, p % 2, i, :], K1[r, p % 4, i, :])
                    dve.drain().then_inc(k2_ready, 1)

                def maxima(G, ch):
                    n = G * CA + ch
                    if ch == 0:
                        if due(G):
                            dve.wait_ge(mx_ready, G)
                    dve.wait_ge(s_full, n + 1)
                    i, t, k = ch // 8, ch // 4 % 2, ch % 4
                    nc.vector.tensor_reduce(mpart[:, t, 1 - i, k:k + 1], psA[:, ch % AB, 0:cuts[k + 1] - cuts[k]],
                                            AX.X, ALU.max).then_inc(s_free, 1)
                    if ch == CA - 1:
                        dve.drain()
                        nc.vector.tensor_reduce(mfull[:], mpart[:], AX.X, ALU.max)
                        cols = MX[:].rearrange("p t (i s) -> p t i s", s=DQ)
                        dve.drain()
                        nc.vector.tensor_scalar(cols[:, :, :, 0], mfull[:], -1.0, None, ALU.mult)
                        dve.drain()
                        nc.vector.scalar_tensor_tensor(out=cols[:, :, :, 1], in0=mfull[:], scalar=-1.0, in1=cols[:, :, :, 0],
                                                       op0=ALU.mult, op1=ALU.subtract).then_inc(mx_ready, 1)

                def add_max(b, p, u):
                    take(b, u)
                    for i in range(HB):
                        o = slice((1 - i) * DQ, (2 - i) * DQ)
                        nc.vector.tensor_copy(Q2[o, p % 4, i, :], M(u)[o, 0:S // 2].bitcast(F16))
                    dve.drain().then_inc(free(u), 1)

                def end(b, be, G, gp, u):
                    if u[0] == "FG":
                        dve.wait_ge(ot_ready, G + 1)
                        take(b, u)
                        nc.vector.reciprocal(rsum[:], M(u)[:, 0:S])
                        dve.drain()
                        nc.vector.tensor_tensor(ON[:, gp, :], oT[:], rsum[:], ALU.mult)
                        dve.drain().then_inc(free(u), 1)
                    elif u[0] == "EW":
                        dve.wait_ge(xr_ld, be * 16 + 16)
                        take(b, u)
                        nc.vector.tensor_tensor(y[:], M(u)[:, 0:S].rearrange("p (t d) -> p t d", t=QT), bo[:], ALU.add)
                        dve.drain().then_inc(free(u), 1)
                        nc.vector.tensor_tensor(y[:], y[:], x_res[:], ALU.add)
                        dve.drain().then_inc(xr_used, 1)
                        layer_norm_stats(nc, dve, y, stats, mv, ve).then_inc(ve_ready, 1)
                    elif u[0] == "FW":
                        take(b, u)
                        nc.vector.tensor_tensor(y[:], M(u)[:, 0:S].rearrange("p (t d) -> p t d", t=QT), x1[:], ALU.add)
                        dve.drain().then_inc(free(u), 1)
                        layer_norm_stats(nc, dve, y, stats, mv, ve).then_inc(ve_ready, 1)
                    elif u[0] in ("EN", "FN"):
                        out = x1 if u[0] == "EN" else x_out
                        dve.wait_ge(rstd_ready, be * 2 + (1 if u[0] == "EN" else 2))
                        if u[0] == "FN":
                            if due(be * 16):
                                dve.wait_ge(st_done, be * 16)
                        for t in range(QT):
                            nc.vector.tensor_scalar(out[:, t, :], y[:, t, :], mv[:, t, 0:1], rstd[:, t:t + 1],
                                                    ALU.subtract, ALU.mult)
                        dve.drain().then_inc(x1_ready if u[0] == "EN" else y_ready, 1)

                for u in prologue:
                    setup(-1, 0, u)
                for ch in range(CA):
                    maxima(0, ch)
                add_max(-1, 0, ("MT", 7))
                copy_high(0, 0)
                for ch in range(CA):
                    maxima(1, ch)

                def body(b, first, last):
                    for p in range(NP):
                        for u in delayed(units(p, first, last)):
                            if u[0] == "A":
                                maxima(b * 8 + p + 2, u[2])
                            elif u[0] == "MT":
                                add_max(b, (p + 1) % 8, u)
                            elif u[0] == "C2":
                                copy_high(b * 8 + p + 1, (p + 1) % 8)
                            elif u[0] in ("FG", "EW", "EN", "FW", "FN"):
                                end(b, b - 1, b * 8 + p - 1, (p - 1) % 8, u)
                            else:
                                setup(b, b + 1 if p >= 5 else b, u)

                over(dve, body)
                for u in post:
                    end(NB, NB - 1, NB * 8 - 1, 7, u)


def experts(nc, x_src, x_dst, w, ident, minus_half):
    E, F = 8, 512
    FT, TQ = F // 128, 4
    NQ = NB * S // (TQ * 128)
    TT = TQ * 128
    xs = x_src.rearrange("b s d -> (b s) d").rearrange("(q t p) d -> q p t d", t=TQ, p=128)
    xd = x_dst.rearrange("b s d -> (b s) d").rearrange("(q t p) d -> q p t d", t=TQ, p=128)

    def quad(x, q):
        return x[bass.ds(q, 1)].rearrange("o p t d -> p (o t) d")

    with ExitStack() as cx:
        def sb(name, shape, dt=F32):
            return cx.enter_context(nc.sbuf_tensor(f"moe_{name}", shape, dt))

        def psum(name, shape):
            return cx.enter_context(nc.psum_tensor(f"moe_{name}", [128] + shape, F32))

        psA, psB = psum("outs", [2, BANK]), psum("hidden", [2, 2 * BANK])
        psO, psM = psum("gate_rows", [BANK]), psum("shared", [BANK])

        def sem(name):
            return cx.enter_context(nc.semaphore(f"moe_{name}"))

        def loaded(name, src):
            t = sb(name, list(src.shape))
            loads.append((t, src))
            return t

        loads = []
        sw, sbias, rank, pick, w1, b1, w2, b2 = (loaded(n, w[n]) for n in ("sw", "sb", "rank", "pick", "w1", "b1", "w2", "b2"))
        x_in = sb("x_in", [128, 2, TQ, 128])
        x_out = sb("x_out", [128, 2, TQ, 128])
        xT = sb("xT", [128, 2, TT])
        NT = NQ * TQ
        lg = sb("logits", [128, NT, E])
        ex = sb("exps", [128, NT, E])
        sel = sb("selected", [128, NT, E])
        gates = sb("gates", [128, NT, E])
        top = sb("top", [128, NT])
        den = sb("den", [128, NT])
        gq = sb("gq", [128, TQ, E])
        gT = sb("gT", [E, TT])
        gB = sb("gB", [128, 2, TT])
        hT = sb("hT", [128, 2, FT, TT])
        tmp = sb("tmp", [128, TT])
        accT = sb("accT", [128, TT])
        accS = sb("accS", [128, TT])
        y = sb("y", [128, TQ, 128])
        stats = sb("stats", [128, TQ, 6])
        mv = sb("mv", [128, TQ, 2])
        ve = sb("ve", [128, TQ])
        rstd = sb("rstd", [128, TQ])

        w_ld, r_ld = sem("weights_loaded"), sem("router_x_loaded")
        x_ld = [sem(f"x_loaded{i}") for i in range(2)]
        st_done = [sem(f"stored{i}") for i in range(2)]
        r_full, r_T, r_lg, r_free = sem("router_T_full"), sem("router_T_copied"), sem("router_logits_full"), sem("router_logits_read")
        d_ready, ex_ready = sem("shifted_ready"), sem("exps_ready")
        m_full, m_free, gq_ready = sem("bank_full"), sem("bank_free"), sem("gates_ready")
        h_full, h_done, y_full, y_used = sem("hidden_full"), sem("hidden_done"), sem("y_full"), sem("y_used")
        g_full, g_done, acc_ready = sem("gate_rows_full"), sem("gate_rows_done"), sem("sum_ready")
        x_used, ve_ready, rstd_ready, out_ready = sem("x_used"), sem("var_ready"), sem("rstd_ready"), sem("out_ready")

        with nc.Block() as block:
            @block.sync
            def _(sp):
                for t, src in loads:
                    sp.dma_start(t[:], src).then_inc(w_ld, 16)
                sp.wait_ge(w_ld, 16 * len(loads))

        with nc.Block() as block:
            @block.sync
            def _(sp):
                def load(q):
                    sp.dma_start(x_in[:, 0], quad(xs, q)).then_inc(r_ld, 16)
                load(0)
                with sp.Fori(1, NQ) as q:
                    if due(q):
                        sp.wait_ge(r_full, q)
                    load(q)

            @block.tensor
            def _(pe):
                def body(q):
                    pe.wait_ge(r_ld, q * 16 + 16)
                    if due(q):
                        pe.wait_ge(r_T, q)
                    for t in range(TQ):
                        last = nc.tensor.transpose(psM[:, t * 128:t * 128 + 128], x_in[:, 0, t, :], ident[:])
                    last.then_inc(r_full, 1)
                    pe.wait_ge(r_T, q + 1)
                    if due(q):
                        pe.wait_ge(r_free, q)
                    for t in range(TQ):
                        last = nc.tensor.matmul(psO[:, t * E:t * E + E], xT[:, 0, t * 128:t * 128 + 128], sw[:],
                                                start=True, stop=True, skip_group_check=True)
                    last.then_inc(r_lg, 1)
                body(0)
                with pe.Fori(1, NQ) as q:
                    body(q)

            @block.scalar
            def _(act):
                def body(q):
                    act.wait_ge(r_full, q + 1)
                    if due(q):
                        act.wait_ge(r_lg, q)
                    nc.scalar.activation(xT[:, 0], psM[:], ACT.Copy).then_inc(r_T, 1)
                body(0)
                with act.Fori(1, NQ) as q:
                    body(q)
                act.wait_ge(d_ready, 1)
                nc.scalar.activation(ex[:], ex[:], ACT.Exp).then_inc(ex_ready, 1)

            @block.vector
            def _(dve):
                def body(q):
                    dve.wait_ge(r_lg, q + 1)
                    nc.vector.tensor_tensor(lg[:, bass.ds(q * TQ, TQ), :], psO[:, 0:TQ * E].rearrange("p (t e) -> p t e", e=E),
                                            sbias[:], ALU.add).then_inc(r_free, 1)
                body(0)
                with dve.Fori(1, NQ) as q:
                    body(q)

                def wide(v):
                    return v[:].unsqueeze(2).to_broadcast([128, NT, E])
                dve.wait_ge(r_free, NQ)
                nc.vector.tensor_reduce(top[:], lg[:], AX.X, ALU.max)
                dve.drain()
                nc.vector.tensor_tensor(ex[:], lg[:], wide(top), ALU.subtract)
                nc.vector.tensor_tensor(sel[:], lg[:], wide(top), ALU.is_ge)
                dve.drain().then_inc(d_ready, 1)
                nc.vector.tensor_tensor(sel[:], sel[:], rank[:], ALU.mult)
                dve.drain()
                nc.vector.tensor_reduce(top[:], sel[:], AX.X, ALU.max)
                dve.drain()
                nc.vector.tensor_tensor(sel[:], sel[:], wide(top), ALU.is_equal)
                dve.wait_ge(ex_ready, 1)
                nc.vector.tensor_reduce(den[:], ex[:], AX.X, ALU.add)
                dve.drain()
                nc.vector.reciprocal(den[:], den[:])
                dve.drain()
                nc.vector.tensor_tensor(gates[:], sel[:], wide(den), ALU.mult)

        prologue = ["X", "GT"]
        body_uses = ["EO", "X", "GT"]

        def no(q, use):
            if isinstance(q, int):
                if q == -1:
                    return prologue.index(use)
                if q == 0:
                    return 2 + ["X", "GT"].index(use)
                if q == NQ - 1 or q == NQ:
                    return 4 + 3 * (NQ - 2) + (q - NQ + 1)
            return q * 3 + (1 + body_uses.index(use))

        def over(eng, body):
            body(0, 0, 0, True, False)
            body(1, 0, 1, False, False)
            with eng.Fori(1, NQ // 2 - 1) as i:
                for par in range(2):
                    body(i * 2 + par, i, par, False, False)
            body(NQ - 2, NQ // 2 - 1, 0, False, False)
            body(NQ - 1, NQ // 2 - 1, 1, False, True)

        with nc.Block() as block:
            @block.sync
            def _(sp):
                def load(q, par):
                    sp.dma_start(x_in[:, par], quad(xs, q)).then_inc(x_ld[par], 16)

                def store(q, par):
                    sp.wait_ge(out_ready, q + 1)
                    sp.dma_start(quad(xd, q), x_out[:, par]).then_inc(st_done[par], 16)
                load(0, 0)
                load(1, 1)

                def body(q, i, par, first, last):
                    if not first:
                        if not last:
                            if due(q):
                                sp.wait_ge(x_used, q)
                            load(q + 1, 1 - par)
                        store(q - 1, 1 - par)
                over(sp, body)
                store(NQ - 1, 1)
                sp.wait_ge(st_done[0], 16 * NQ // 2)
                sp.wait_ge(st_done[1], 16 * NQ // 2)

            @block.tensor
            def _(pe):
                def turn_x(q, par, its):
                    pe.wait_ge(x_ld[par], its * 16 + 16)
                    if due(no(q, "X")):
                        pe.wait_ge(m_free, no(q, "X"))
                    for t in range(TQ):
                        last = nc.tensor.transpose(psM[:, t * 128:t * 128 + 128], x_in[:, par, t, :], ident[:])
                    last.then_inc(m_full, 1)

                def turn_gates(q):
                    pe.wait_ge(gq_ready, q + 2)
                    if due(no(q, "GT")):
                        pe.wait_ge(m_free, no(q, "GT"))
                    for t in range(TQ):
                        last = nc.tensor.transpose(psM[0:E, t * 128:t * 128 + 128], gq[:, t, :], ident[:])
                    last.then_inc(m_full, 1)

                def turn_back(q):
                    if due(q):
                        pe.wait_ge(acc_ready, q)
                    if due(no(q, "EO")):
                        pe.wait_ge(m_free, no(q, "EO"))
                    for t in range(TQ):
                        last = nc.tensor.transpose(psM[:, t * 128:t * 128 + 128], accS[:, t * 128:t * 128 + 128], ident[:])
                    last.then_inc(m_full, 1)

                def hidden(q, par, e):
                    n = q * E + e
                    if e == 0:
                        pe.wait_ge(m_free, no(q - 1, "GT") + 1)
                    for f in range(FT):
                        if due(n * FT + f - 3):
                            pe.wait_ge(h_done, n * FT + f - 3)
                        nc.tensor.matmul(psB[:, f // 2, f % 2 * BANK:(f % 2 + 1) * BANK], w1[:, e, f * 128:f * 128 + 128], xT[:, par],
                                         start=True, stop=True, skip_group_check=True).then_inc(h_full, 1)
                    if due(n):
                        pe.wait_ge(g_done, n)
                    nc.tensor.matmul(psO[:], pick[:, e, :], gT[:], start=True, stop=True, skip_group_check=True).then_inc(g_full, 1)

                def out(n, e):
                    if due(n - 1):
                        pe.wait_ge(y_used, n - 1)
                    pe.wait_ge(h_done, n * FT + FT)
                    for f in range(FT):
                        last = nc.tensor.matmul(psA[:, e % 2], w2[:, e, f, :], hT[:, e % 2, f, :], start=(f == 0), stop=(f == FT - 1),
                                                skip_group_check=True)
                    last.then_inc(y_full, 1)

                turn_x(-1, 0, 0)
                turn_gates(-1)

                def body(q, i, par, first, last):
                    for e in range(E):
                        hidden(q, par, e)
                        if not (first and e == 0):
                            out(q * E + e - 1, (e - 1) % E)
                        if e == 2 and not first:
                            turn_back(q)
                        if e == 5 and not last:
                            turn_x(q, 1 - par, i + par)
                        if e == 7 and not last:
                            turn_gates(q)
                over(pe, body)
                out(NQ * E - 1, E - 1)
                turn_back(NQ)

            @block.scalar
            def _(act):
                def copy_x(q, par):
                    act.wait_ge(m_full, no(q, "X") + 1)
                    nc.scalar.activation(xT[:, par], psM[:], ACT.Copy).then_inc(m_free, 1)

                def copy_gates(q):
                    act.wait_ge(m_full, no(q, "GT") + 1)
                    if due((q + 1) * E):
                        act.wait_ge(g_full, (q + 1) * E)
                    nc.scalar.activation(gT[:], psM[0:E, :], ACT.Copy).then_inc(m_free, 1)

                copy_x(-1, 0)
                copy_gates(-1)

                def body(q, i, par, first, last):
                    for e in range(E):
                        n = q * E + e
                        for f in range(FT):
                            act.wait_ge(h_full, n * FT + f + 1)
                            if f == 0:
                                if due(n - 1):
                                    act.wait_ge(y_full, n - 1)
                            nc.scalar.activation(hT[:, e % 2, f, :], psB[:, f // 2, f % 2 * BANK:(f % 2 + 1) * BANK],
                                                 ACT.Gelu_apprx_tanh, bias=b1[:, e, f:f + 1]).then_inc(h_done, 1)
                        act.wait_ge(g_full, n + 1)
                        if due(n - 1):
                            act.wait_ge(y_used, n - 1)
                        nc.scalar.activation(gB[:, e % 2], psO[:], ACT.Copy).then_inc(g_done, 1)
                        if e == 5 and not last:
                            copy_x(q, 1 - par)
                        if e == 7 and not last:
                            copy_gates(q)
                over(act, body)

            @block.gpsimd
            def _(pool):
                def body(q, i, par, first, last):
                    pool.wait_ge(ve_ready, q + 1)
                    nc.gpsimd.tensor_tensor(rstd[:], ve[:], minus_half[:, 0:TQ], ALU.pow).then_inc(rstd_ready, 1)
                over(pool, body)

            @block.vector
            def _(dve):
                def take_gates(q):
                    if due(q + 1):
                        dve.wait_ge(m_full, no(q - 1, "GT") + 1)
                    nc.vector.tensor_copy(gq[:], gates[:, bass.ds((q + 1) * TQ, TQ), :]).then_inc(gq_ready, 1)

                def gate(n, e):
                    dve.wait_ge(g_done, n + 1)
                    dve.wait_ge(y_full, n + 1)
                    if e == 0:
                        nc.vector.scalar_tensor_tensor(out=accT[:], in0=psA[:, e % 2], scalar=b2[:, e:e + 1], in1=gB[:, e % 2],
                                                       op0=ALU.add, op1=ALU.mult)
                        dve.drain().then_inc(y_used, 1)
                    else:
                        nc.vector.scalar_tensor_tensor(out=tmp[:], in0=psA[:, e % 2], scalar=b2[:, e:e + 1], in1=gB[:, e % 2],
                                                       op0=ALU.add, op1=ALU.mult)
                        dve.drain().then_inc(y_used, 1)
                        nc.vector.tensor_tensor(accS[:] if e == E - 1 else accT[:], accT[:], tmp[:], ALU.add)
                        dve.drain()

                def finish(q, qe, par, its):
                    dve.wait_ge(m_full, no(q, "EO") + 1)
                    nc.vector.tensor_tensor(y[:], psM[:].rearrange("p (t d) -> p t d", t=TQ), x_in[:, par], ALU.add)
                    dve.drain().then_inc(m_free, 1)
                    for t in range(TQ):
                        nc.vector.bn_stats(stats[:, t, :], y[:, t, :])
                    dve.drain().then_inc(x_used, 1)
                    for t in range(TQ):
                        nc.vector.bn_aggr(mv[:, t, :], stats[:, t, :])
                    dve.drain()
                    nc.vector.tensor_scalar(ve[:], mv[:, :, 1], EPS, None, ALU.add).then_inc(ve_ready, 1)

                def normalise(qe, par, its):
                    dve.wait_ge(rstd_ready, qe + 1)
                    if due(its * 16):
                        dve.wait_ge(st_done[par], its * 16)
                    for t in range(TQ):
                        nc.vector.tensor_scalar(x_out[:, par, t, :], y[:, t, :], mv[:, t, 0:1], rstd[:, t:t + 1],
                                                ALU.subtract, ALU.mult)
                    dve.drain().then_inc(out_ready, 1)

                take_gates(-1)

                def body(q, i, par, first, last):
                    for e in range(E):
                        if not (first and e == 0):
                            gate(q * E + e - 1, (e - 1) % E)
                        if e == 0 and not first:
                            dve.drain().then_inc(acc_ready, 1)
                        if e == 2 and not first:
                            finish(q, q - 1, 1 - par, i - 1 + par)
                        if e == 4 and not first:
                            normalise(q - 1, 1 - par, i - 1 + par)
                        if e == 6 and not last:
                            take_gates(q)
                over(dve, body)
                gate(NQ * E - 1, E - 1)
                dve.drain().then_inc(acc_ready, 1)
                finish(NQ, NQ - 1, 1, NQ // 2 - 1)
                normalise(NQ - 1, 1, NQ // 2 - 1)


def decoder(nc, ins, out):
    with ExitStack() as c:
        ident = c.enter_context(nc.sbuf_tensor("identity", [128, 128], F32))
        ident16 = c.enter_context(nc.sbuf_tensor("identity16", [128, 128], F16))
        minus_half = c.enter_context(nc.sbuf_tensor("minus_half", [128, 4], F32))
        const_ld = c.enter_context(nc.semaphore("constants_loaded"))
        between = [nc.dram_tensor(f"x_after_{n}", (NB, S, D), F32, kind="Internal").ap() for n in ("rope", "wide", "chunked", "cross")]

        def of(part):
            return {k[len(part) + 1:]: v for k, v in ins.items() if k.startswith(part + "_")}

        with nc.Block() as block:
            @block.sync
            def _(sp):
                sp.dma_start(ident[:], ins["ident"]).then_inc(const_ld, 16)
                sp.dma_start(ident16[:], ins["ident16"]).then_inc(const_ld, 16)
                sp.wait_ge(const_ld, 32)

            @block.gpsimd
            def _(pool):
                nc.gpsimd.memset(minus_half[:], -0.5)

        attention8(nc, "rope", ins["x"], between[0], of("rope"), ident, ident16, minus_half)
        cross64(nc, between[0], between[1], of("wide"), ident, ident16, minus_half, ins["ctx"])
        attention8(nc, "chunked", between[1], between[2], of("chunked"), ident, ident16, minus_half)
        attention8(nc, "cross", between[2], between[3], of("cross"), ident, ident16, minus_half, ctx=ins["ctx"])
        experts(nc, between[3], out, of("moe"), ident, minus_half)


def head_columns(w, swap=False):
    w = np.asarray(w).reshape(D, H, DH)
    if swap:
        w = w.reshape(D, H, DH // 2, 2)[..., ::-1].reshape(D, H, DH)
    out = np.zeros((D, H, SLOT), np.float32)
    for s in range(3):
        out[:, :, DH * s:DH * s + DH] = w
    return out.reshape(D, H * SLOT)


def head_bias(b, shift_rows, swap=False):
    b = np.asarray(b).reshape(H, DH)
    if swap:
        b = b.reshape(H, DH // 2, 2)[..., ::-1].reshape(H, DH)
    out = np.zeros((H, SLOT), np.float32)
    for s in range(3):
        out[:, DH * s:DH * s + DH] = b
    out[:, M_ROW:M_ROW + 2] = shift_rows
    return np.ascontiguousarray(out.reshape(NG, HG * SLOT).T)


def low_rows():
    out = np.zeros((HG, SLOT, 2), np.float32)
    out[:, DH:2 * DH, 0] = 1
    out[:, 2 * DH:3 * DH, 1] = 1
    return out.reshape(128, 2)


def rope_tables():
    inv = (np.float32(1.0) / np.float32(10000.0) ** (np.arange(0, DH, 2, dtype=np.float32) / np.float32(DH))).astype(np.float32)
    freqs = np.arange(S, dtype=np.float32)[:, None] * inv[None, :]
    angle = np.concatenate([freqs, freqs], -1)[:, ::2]
    cos, sin = np.zeros((HG, SLOT, S), np.float32), np.zeros((HG, SLOT, S), np.float32)
    for s in range(3):
        for d in range(DH):
            cos[:, DH * s + d] = np.cos(angle[:, d // 2])
            sin[:, DH * s + d] = np.sin(angle[:, d // 2]) * (-1 if d % 2 == 0 else 1)
    cos[:, M_ROW:M_ROW + 2] = 1
    return cos.reshape(128, S), sin.reshape(128, S)


def chunk_columns(w, part):
    w = np.asarray(w).reshape(16, 3, DH, D)[:, part].transpose(2, 0, 1)
    out = np.zeros((D, 16, SLOT), np.float32)
    for s in range(3 if part < 2 else 1):
        out[:, :, DH * s:DH * s + DH] = w
    return out.reshape(D, 16 * SLOT)


def chunk_bias(b, part):
    b = np.asarray(b).reshape(16, 3, DH)[:, part].T
    out = np.zeros((HG, SLOT, 16), np.float32)
    for s in range(3 if part < 2 else 1):
        out[:, DH * s:DH * s + DH, :] = b
    if part == 1:
        out[:, M_ROW:M_ROW + 2] = 1
    if part == 2:
        out[:, DH] = 1
    return out.reshape(128, 16)


def on_rows(b, n):
    b = np.asarray(b).reshape(1, 1, -1)
    return np.ascontiguousarray(np.broadcast_to(b, (128, n, b.size)))


def flat_rows(b, n):
    return on_rows(b, n).reshape(128, -1)


def turned(w):
    return np.ascontiguousarray(np.asarray(w).T)


def laid_out(i):
    out = {"x": np.asarray(i["x"]), "ctx": np.asarray(i["ctx_1024"]),
           "ident": np.eye(128, dtype=np.float32), "ident16": np.eye(128, dtype=np.float16)}
    cos, sin = rope_tables()
    a = "L0_attn_"
    out |= {"rope_wq": head_columns(i[a + "Wq"]), "rope_wqs": head_columns(i[a + "Wq"], True),
            "rope_wk": head_columns(i[a + "Wk"]), "rope_wks": head_columns(i[a + "Wk"], True),
            "rope_bq": head_bias(i[a + "bq"], 0), "rope_bqs": head_bias(i[a + "bq"], 0, True),
            "rope_bk": head_bias(i[a + "bk"], 1), "rope_bks": head_bias(i[a + "bk"], 0, True),
            "rope_cos": cos, "rope_sin": sin, "rope_wv": np.asarray(i[a + "Wv"]), "rope_bv": flat_rows(i[a + "bv"], QT),
            "rope_lo": low_rows(), "rope_wo": np.asarray(i[a + "Wo"]), "rope_bo": on_rows(i[a + "bo"], QT)}
    a = "L0_xattn_"
    dd = np.asarray(i["L0_ffn_disha"])
    out |= {"wide_wq": np.asarray(i[a + "Wq"]), "wide_wk": np.asarray(i[a + "Wk"]), "wide_wv": np.asarray(i[a + "Wv"]),
            "wide_wo": np.ascontiguousarray(np.asarray(i[a + "Wo"]).reshape(8, 128, D).transpose(1, 0, 2)),
            "wide_bo": on_rows(i[a + "bo"], QT), "wide_wf": turned(i["L0_ffn_weight"]), "wide_dd": np.concatenate([dd, dd])}
    a = "L1_attn_"
    for n, name in enumerate("qkv"):
        out |= {f"chunked_w{name}": chunk_columns(i[a + "W_qkv"], n), f"chunked_b{name}": chunk_bias(i[a + "b_qkv"], n)}
    out |= {"chunked_lo": low_rows(), "chunked_wo": turned(i[a + "W_out"]), "chunked_bo": on_rows(i[a + "b_out"], QT)}
    a = "L1_xattn_"
    out |= {"cross_wq": head_columns(turned(i[a + "Wq"])), "cross_wk": head_columns(turned(i[a + "Wk"])),
            "cross_bq": head_bias(i[a + "bq"], 0), "cross_bk": head_bias(i[a + "bk"], 1),
            "cross_wv": turned(i[a + "Wv"]), "cross_bv": flat_rows(i[a + "bv"], 4), "cross_lo": low_rows()}
    a = "L1_ffn_"
    pick = np.zeros((8, 8, 128), np.float32)
    for e in range(8):
        pick[e, e] = 1
    out |= {"moe_sw": np.asarray(i[a + "switch_w"]), "moe_sb": on_rows(i[a + "switch_b"], 4),
            "moe_rank": on_rows(np.arange(8, 0, -1).astype(np.float32), NB * QT), "moe_pick": pick,
            "moe_w1": np.ascontiguousarray(np.asarray(i[a + "w1"]).transpose(1, 0, 2)),
            "moe_b1": np.ascontiguousarray(np.asarray(i[a + "b1"]).reshape(8, 4, 128).transpose(2, 0, 1)),
            "moe_w2": np.ascontiguousarray(np.asarray(i[a + "w2"]).reshape(8, 4, 128, D).transpose(2, 0, 1, 3)),
            "moe_b2": turned(i[a + "b2"])}
    return out


def kernel(**inputs):
    import concourse.bacc as bacc
    from concourse.bass_utils import run_bass_kernel_spmd

    nc = bacc.Bacc("TRN2", target_bir_lowering=False, num_devices=1)
    arrays = laid_out(inputs)
    ins = {k: nc.dram_tensor(f"in_{k}", v.shape, mybir.dt.from_np(v.dtype), kind="ExternalInput").ap() for k, v in arrays.items()}
    out = nc.dram_tensor("out", (NB, S, D), F32, kind="ExternalOutput").ap()
    decoder(nc, ins, out)
    r = run_bass_kernel_spmd(nc, [{f"in_{k}": v for k, v in arrays.items()}], core_ids=[0])
    return r.results[0]["out"]
```

```python
from contextlib import ExitStack

import numpy as np

import concourse.bass as bass
from concourse import mybir

F32 = mybir.dt.float32
F16 = mybir.dt.float16
ALU = mybir.AluOpType
ACT = mybir.ActivationFunctionType
AX = mybir.AxisListType

NB, S, D, NKC = 16, 256, 128, 1601
QT = S // 128
H, DH, NG, HG = 16, 8, 4, 4
SLOT = 32
M_ROW = 24
EPS = 1e-5
BANK = 512


def due(value):
    return not isinstance(value, int) or value > 0


class UseOrder:

    def __init__(self, banks, prologue, first, body, last, post):
        self.lists = prologue, first, body, last, post
        self.banks = {use: i % banks for i, use in enumerate(body)}

    def bank(self, use):
        return self.banks[use]

    def no(self, b, use):
        bank = self.banks[use]
        prologue, first, body, last, post = ([u for u in us if self.banks[u] == bank] for us in self.lists)
        if isinstance(b, int):
            if b == -1:
                return prologue.index(use)
            if b == 0:
                return len(prologue) + first.index(use)
            if b == NB - 1:
                return len(prologue) + len(first) + (NB - 2) * len(body) + last.index(use)
            if b == NB:
                return len(prologue) + len(first) + (NB - 2) * len(body) + len(last) + post.index(use)
        return b * len(body) + (len(prologue) + len(first) - len(body) + body.index(use))


def over_batches(eng, body):
    body(0, 0, 0, True, False)
    body(1, 0, 1, False, False)
    with eng.Fori(1, NB // 2 - 1) as i:
        for par in range(2):
            body(i * 2 + par, i, par, False, False)
    body(NB - 2, NB // 2 - 1, 0, False, False)
    body(NB - 1, NB // 2 - 1, 1, False, True)


def spread(others, chunks, before=False):
    out, n, m = [], len(others), len(chunks)
    for i in range(max(n, 1)):
        some = chunks[i * m // max(n, 1):(i + 1) * m // max(n, 1)]
        out += some + others[i:i + 1] if before else others[i:i + 1] + some
    return out


def mixed(a, b):
    at = [((i + (0 if us is b else 0.5)) / len(us), u) for us in (a, b) for i, u in enumerate(us)]
    return [u for _, u in sorted(at, key=lambda x: x[0])]


def delayed(us):
    us = list(us)
    for i in range(len(us) - 1, 0, -1):
        if us[i][0] == "A" and us[i - 1][0] != "A":
            us[i - 1:i + 1] = us[i], us[i - 1]
    return us


def tokens(x, b):
    return x[bass.ds(b, 1)].rearrange("o (t p) d -> p (o t) d", p=128)


def layer_norm_stats(nc, dve, y, stats, mv, ve):
    for t in range(QT):
        nc.vector.bn_stats(stats[:, t, :], y[:, t, :])
    dve.drain()
    for t in range(QT):
        nc.vector.bn_aggr(mv[:, t, :], stats[:, t, :])
    dve.drain()
    return nc.vector.tensor_scalar(ve[:], mv[:, :, 1], EPS, None, ALU.add)


def attention8(nc, kind, x_src, x_dst, w, ident, ident16, minus_half, ctx=None):
    cross, rope, chunked = kind == "cross", kind == "rope", kind == "chunked"
    NK = NKC if cross else S
    KT = -(-NK // 128)
    kn = [min(128, NK - 128 * k) for k in range(KT)]
    STEPS = 2 * KT
    LAG = 3 if cross else 2
    SCALE = float(DH) ** -0.5
    cuts = [NK * c // 4 for c in range(5)]
    CA = HG * QT * 4 if cross else HG
    kcuts = list(range(0, NK, BANK)) + [NK]
    PARTS = ((0, 0), (0, 1), (1, 0))
    AB, MB = (3, 2) if cross else (2, 3)
    back = [AB if i >= AB else CA - max(j for j in range(CA) if j % AB == i) + i for i in range(CA)]

    if cross:
        set_x, set_g = [("X",)] + [("C", i) for i in range(4)], [[("Q", g)] + [("K", g, c) for c in range(4)] for g in range(NG)]
        v_uses = [("V", i) for i in range(4)]
        setups = [set_x + set_g[0], set_g[1], v_uses[:2] + set_g[2], v_uses[2:] + set_g[3]]
    elif rope:
        setups = [[("X",), ("Q", 0), ("K", 0)], [("Q", 1), ("K", 1)], [("V",), ("Q", 2), ("K", 2)], [("Q", 3), ("K", 3)]]
    else:
        setups = [[("X",), ("Q", 0), ("Q", 1), ("K", 0), ("K", 1)], [("V", 0), ("V", 1)], [("T", 0), ("T", 1)], []]
    ends = [[], [("EL",)], [], [("EN",)]] if cross else [[], [("EO",)], [("EW",)], [("EN",)]]
    NO_BANK = ("EL", "EN", "A")

    def units(g, first, last):
        late = rope and g == 3
        u = [] if first or late else list(ends[g])
        u += [] if last else setups[g]
        u += ends[g] if late and not first else []
        if not (last and g == 3):
            u.insert(1 if cross else 0, ("MT", g))
        if not (first and g == 0):
            u.insert(max((len(u) + 1) // 2, len(u) if last else 0), ("FG", g))
        return spread(u, [] if last and g >= 2 else [("A", g, c) for c in range(CA)], True)

    def bank_uses(us):
        return [u for u in us if u[0] not in NO_BANK]

    def of_body(first, last):
        return bank_uses([u for g in range(NG) for u in units(g, first, last)])

    prologue = [u for s in setups for u in s]
    post = [("FG", 0)] + [u for e in ends for u in e]
    order = UseOrder(MB, prologue + [("MT", 3)], of_body(True, False), of_body(False, False), of_body(False, True), bank_uses(post))
    v_use = ("V", 3) if cross else ("V",) if rope else ("T", 1)

    def share(us, s):
        n = len(us)
        return us[n * s // STEPS:n * (s + 1) // STEPS]

    with ExitStack() as c:
        def sb(name, shape, dt=F32):
            return c.enter_context(nc.sbuf_tensor(f"{kind}_{name}", shape, dt))

        def psum(name, shape):
            return c.enter_context(nc.psum_tensor(f"{kind}_{name}", [128] + shape, F32))

        def sem(name):
            return c.enter_context(nc.semaphore(f"{kind}_{name}"))

        def loaded(name, src):
            t = sb(name, list(src.shape))
            loads.append((t, src))
            return t

        loads = []
        if rope:
            wq, wk, wqs, wks = (loaded(n, w[n]) for n in ("wq", "wk", "wqs", "wks"))
            bq, bk, bqs, bks = (loaded(n, w[n]) for n in ("bq", "bk", "bqs", "bks"))
            cos, sin = loaded("cos", w["cos"]), loaded("sin", w["sin"])
        else:
            wq, wk, bq, bk = (loaded(n, w[n]) for n in ("wq", "wk", "bq", "bk"))
        wv, bv = loaded("wv", w["wv"]), loaded("bv", w["bv"])
        lo = loaded("lo", w["lo"])
        if not cross:
            wo, bo = loaded("wo", w["wo"]), loaded("bo", w["bo"])

        psA, psB = psum("scores", [AB, BANK]), psum("scoresT", [2, BANK])
        psO, psM = psum("weighed", [BANK]), psum("shared", [MB, BANK])
        x_in = sb("x_in", [128, 2, QT, 128])
        x_res = sb("x_res", [128, 2, QT, 128])
        x_out = sb("x_out", [128, 2, QT, 128])
        xT = sb("xT", [128, S])
        KO = sb("KO", [128, 2, NG, NK], F16)
        QC = sb("QC", [128, NG, S], F16)
        QZ = sb("QZ", [128, 2, H, S], F16)
        VA = sb("VA", [128, 2, KT, H, SLOT])
        P = sb("P", [128, 8, 2, S])
        MX = sb("MX", [128, QT, 128], F16)
        mfull = sb("mfull", [128, QT, HG])
        mpart = sb("mpart", [128, QT, HG, 4])
        hi = sb("hi", [128, 2, BANK], F16)
        oT = sb("oT", [128, S])
        O = sb("O", [128, QT, 128])
        rsum = sb("rsum", [128, QT, HG])
        y = sb("y", [128, QT, 128])
        stats = sb("stats", [128, QT, 6])
        mv = sb("mv", [128, QT, 2])
        ve = sb("ve", [128, QT])
        rstd = sb("rstd", [128, QT])
        if not cross:
            OT = sb("OT", [128, S])
        if rope:
            rot = sb("rot", [128, 2, 3, S])
        if cross:
            ctx_in = sb("ctx_in", [128, 2, KT, 128])
            cT = sb("cT", [128, 2, NK], F16)
            wkp, wvp = sb("wk_parts", [128, 2, H * SLOT], F16), sb("wv_parts", [128, 2, 128], F16)
            lob = sb("lob", [128, NG])
            raw = sb("raw", [128, 2, BANK])
        if chunked:
            xs = sb("xs", [128, 2, BANK])
            VT = sb("VT", [128, NG, S])

        w_ld, init = sem("weights_loaded"), sem("initialised")
        x_ld = [sem(f"x_loaded{i}") for i in range(2)]
        xr_ld = [sem(f"residual_loaded{i}") for i in range(2)]
        c_ld = [sem(f"context_loaded{i}") for i in range(2)] if cross else None
        st_done = [sem(f"stored{i}") for i in range(2)]
        m_full, m_free = [sem(f"bank_full{i}") for i in range(MB)], [sem(f"bank_free{i}") for i in range(MB)]
        s_full, s_free = sem("scores_full"), sem("scores_maxed")
        t_full, e_done, pv_done = sem("scoresT_full"), sem("exp_done"), sem("pv_done")
        op_ready = sem("operand_ready")
        if cross:
            ch_ready = sem("context_high_ready")
        else:
            raw_ready = sem("raw_ready")
        if chunked:
            vt_ready = sem("values_ready")
        qc_ready = sem("queries_ready")
        q_ld = [sem(f"queries_spread{g}") for g in range(1 if chunked else NG)]
        mx_ready, ot_ready = sem("max_ready"), sem("oT_ready")
        xr_used, ve_ready, rstd_ready, y_ready = sem("residual_used"), sem("var_ready"), sem("rstd_ready"), sem("out_ready")

        def M(use):
            return psM[:, order.bank(use)]

        def full(use):
            return m_full[order.bank(use)]

        def free(use):
            return m_free[order.bank(use)]

        def raw_no(b, u):
            if cross:
                return (b + 1) * 16 + 4 * u[1] + u[2]
            if rope:
                return (b + 1) * 8 + 2 * u[1] + (u[0] == "K")
            return (b + 1) * 4 + 2 * (u[0] == "K") + u[1]

        def load(sp, b, par):
            sp.dma_start(x_in[:, par], tokens(x_src, b)).then_inc(x_ld[par], 16)

        def load_ctx(sp, b, par):
            src = ctx[bass.ds(b, 1)]
            full_rows = (KT - 1) * 128
            sp.dma_start(ctx_in[:, par, 0:KT - 1, :],
                         src[:, 0:full_rows].rearrange("o (k p) d -> p (o k) d", p=128)).then_inc(c_ld[par], 16)
            sp.dma_start(ctx_in[0:kn[-1], par, KT - 1, :],
                         src[:, full_rows:NK].rearrange("o p d -> p (o d)")).then_inc(c_ld[par], 16)

        def load_res(sp, b, par):
            sp.dma_start(x_res[:, par], tokens(x_src, b)).then_inc(xr_ld[par], 16)

        with nc.Block() as block:
            @block.sync
            def _(sp):
                for t, src in loads:
                    sp.dma_start(t[:], src).then_inc(w_ld, 16)
                for b in range(2):
                    load(sp, b, b)
                    if cross:
                        load_ctx(sp, b, b)
                    load_res(sp, b, b)
                sp.wait_ge(w_ld, 16 * len(loads))

            @block.gpsimd
            def _(pool):
                nc.gpsimd.memset(QZ[:], 0.0)

            @block.vector
            def _(dve):
                nc.vector.memset(MX[:], 0.0)
                nc.vector.memset(VA[:], 0.0)
                dve.drain()
                nc.vector.memset(VA[:, :, :, :, DH:DH + 1], 1.0)
                if cross:
                    dve.wait_ge(w_ld, 16 * len(loads))
                    nc.vector.tensor_scalar(lob[:], bk[:], lo[:, 0:1], None, ALU.mult)
                    for m, parts in ((wk, wkp), (wv, wvp)):
                        nc.vector.tensor_copy(parts[:, 0], m[:])
                    dve.drain()
                    for m, parts in ((wk, wkp), (wv, wvp)):
                        nc.vector.tensor_tensor(parts[:, 1], m[:], parts[:, 0], ALU.subtract)

        with nc.Block() as block:
            @block.sync
            def _(sp):
                def spread_queries(n, par, g):
                    sp.wait_ge(qc_ready, (n + 1) * 2 if chunked else n * NG + g + 1)
                    for j in range(HG):
                        r = slice(j * SLOT, (j + 1) * SLOT)
                        if chunked:
                            to, src = QZ[r, par].rearrange("r (g j) q -> r g j q", j=HG)[:, :, j], QC[r]
                        else:
                            to, src = QZ[r, par, 4 * g + j], QC[r, g]
                        sp.dma_start(to, src).then_inc(q_ld[g], 16)

                for g in range(len(q_ld)):
                    spread_queries(0, 0, g)

                def store(b, par):
                    sp.wait_ge(y_ready, b + 1)
                    sp.dma_start(tokens(x_dst, b), x_out[:, par]).then_inc(st_done[par], 16)

                def body(b, it, par, first, last):
                    if not (isinstance(b, int) and b >= NB - 2):
                        setup_b = b - 1
                        sp.wait_ge(free(("C", 3) if cross else ("X",)), order.no(setup_b, ("C", 3) if cross else ("X",)) + 1)
                        load(sp, b + 2, par)
                        if cross:
                            load_ctx(sp, b + 2, par)
                    if not last:
                        for g in range(len(q_ld)):
                            spread_queries(b + 1, 1 - par, g)
                    if not first:
                        store(b - 1, 1 - par)
                        if not last:
                            if due(b):
                                sp.wait_ge(xr_used, b)
                            load_res(sp, b + 1, 1 - par)

                over_batches(sp, body)
                store(NB - 1, 1)
                sp.wait_ge(st_done[0], 16 * NB // 2)
                sp.wait_ge(st_done[1], 16 * NB // 2)

            @block.tensor
            def _(pe):
                def begin(b, u):
                    if due(order.no(b, u)):
                        pe.wait_ge(free(u), order.no(b, u))

                def setup(b, bs, its, par, u):
                    begin(b, u)
                    if u[0] in "QKV" and (u[0] == "Q" or not cross):
                        pe.wait_ge(free(("X",)), order.no(b, ("X",)) + 1)
                    if cross and u[0] in "KV":
                        pe.wait_ge(free(("C", u[-1])), order.no(b, ("C", u[-1])) + 1)
                    if u[0] == "X":
                        pe.wait_ge(x_ld[par], its * 16 + 16)
                        for t in range(QT):
                            last = nc.tensor.transpose(M(u)[:, t * 128:t * 128 + 128], x_in[:, par, t, :], ident[:])
                    elif u[0] == "C":
                        if u[1] == 0:
                            pe.wait_ge(c_ld[par], its * 32 + 32)
                        for i, k in enumerate(range(4 * u[1], min(4 * u[1] + 4, KT))):
                            last = nc.tensor.transpose(M(u)[:, i * 128:i * 128 + kn[k]], ctx_in[0:kn[k], par, k, :],
                                                       ident[0:kn[k], 0:kn[k]])
                    elif rope and u[0] in "QK":
                        for i, m in enumerate((wq, wqs) if u[0] == "Q" else (wk, wks)):
                            last = nc.tensor.matmul(M(u)[:, i * S:i * S + S], m[:, u[1] * 128:u[1] * 128 + 128], xT[:],
                                                    start=True, stop=True, skip_group_check=True)
                    elif rope and u[0] == "V":
                        for t in range(QT):
                            last = nc.tensor.matmul(M(u)[:, t * 128:t * 128 + 128], xT[:, t * 128:t * 128 + 128], wv[:],
                                                    start=True, stop=True, skip_group_check=True)
                    elif chunked and u[0] in "QKV":
                        m = {"Q": wq, "K": wk, "V": wv}[u[0]]
                        for i in range(8):
                            for j in range(HG):
                                last = nc.tensor.matmul(M(u)[j * SLOT:(j + 1) * SLOT, i * 64:i * 64 + 64],
                                                        m[:, (8 * u[1] + i) * SLOT:(8 * u[1] + i + 1) * SLOT],
                                                        xT[:, j * 64:j * 64 + 64], start=True, stop=True, skip_group_check=True)
                    elif u[0] == "T":
                        pe.wait_ge(vt_ready, bs * 2 + 2)
                        for g in range(NG):
                            last = nc.tensor.transpose(M(u)[:, g * 128:g * 128 + 128], VT[:, g, u[1] * 128:u[1] * 128 + 128], ident[:])
                    elif u[0] == "Q":
                        last = nc.tensor.matmul(M(u)[:, 0:S], wq[:, u[1] * 128:u[1] * 128 + 128], xT[:],
                                                start=True, stop=True, skip_group_check=True)
                    elif u[0] == "K":
                        a, z = kcuts[u[2]], kcuts[u[2] + 1]
                        for wp, cp in PARTS:
                            last = nc.tensor.matmul(M(u)[:, 0:z - a], wkp[:, wp, u[1] * 128:u[1] * 128 + 128], cT[:, cp, a:z],
                                                    start=(wp == cp), stop=(wp == 1), skip_group_check=True)
                    elif u[0] == "V":
                        for i, k in enumerate(range(4 * u[1], min(4 * u[1] + 4, KT))):
                            for wp, cp in PARTS:
                                last = nc.tensor.matmul(M(u)[0:kn[k], i * 128:i * 128 + 128], cT[:, cp, k * 128:k * 128 + kn[k]],
                                                        wvp[:, wp], start=(wp == cp), stop=(wp == 1), skip_group_check=True)
                    last.then_inc(full(u), 1)

                def scores(G, g, par, ch, setup_at):
                    n = G * CA + ch
                    if ch == 0:
                        pe.wait_ge(q_ld[0 if chunked else g], (setup_at + 2) * 64)
                    if ch == 0 and chunked:
                        pe.wait_ge(op_ready, (setup_at + 2) * 4)
                    elif ch == 0 and rope:
                        pe.wait_ge(op_ready, (setup_at + 1) * 8 + 2 * g + 2)
                    elif ch == 0:
                        pe.wait_ge(op_ready, (setup_at + 1) * 16 + 4 * g + 4)
                    if due(n + 1 - back[ch]):
                        pe.wait_ge(s_free, n + 1 - back[ch])
                    out = psA[:, ch % AB]
                    if cross:
                        j, t, k = ch // 8, ch // 4 % 2, ch % 4
                        a, z = cuts[k], cuts[k + 1]
                        last = nc.tensor.matmul(out[:, 0:z - a], QZ[:, par, 4 * g + j, t * 128:t * 128 + 128], KO[:, par, g, a:z],
                                                start=True, stop=True, skip_group_check=True)
                    else:
                        for t in range(QT):
                            last = nc.tensor.matmul(out[:, t * S:t * S + S], QZ[:, par, 4 * g + ch, t * 128:t * 128 + 128],
                                                    KO[:, par, g, :], start=True, stop=True, skip_group_check=True)
                    last.then_inc(s_full, 1)

                def max_rows(b, G, u):
                    pe.wait_ge(mx_ready, G + 1)
                    begin(b, u)
                    for t in range(QT):
                        last = nc.tensor.transpose(M(u)[:, t * 64:t * 64 + 64].bitcast(F16), MX[:, t, :], ident16[:])
                    last.then_inc(full(u), 1)

                def scoresT(b, G, g, par, s):
                    n, kt, i = G * STEPS + s, s // 2, s % 2
                    if s == 0:
                        before = ("MT", (g - 1) % 4)
                        pe.wait_ge(free(before), order.no(b if g else b - 1, before) + 1)
                    if due(n - 1):
                        pe.wait_ge(e_done, n - 1)
                    nc.tensor.matmul(psB[0:kn[kt], i], KO[:, par, g, kt * 128:kt * 128 + kn[kt]],
                                     QZ[:, par, 4 * g + 2 * i:4 * g + 2 * i + 2, :],
                                     start=True, stop=True, skip_group_check=True).then_inc(t_full, 1)

                def weigh(b, G, g, par, s):
                    n, kt, i = G * STEPS + s, s // 2, s % 2
                    if s == 0:
                        if due(G):
                            pe.wait_ge(ot_ready, G)
                        if g == 0:
                            pe.wait_ge(free(v_use), order.no(b - 1, v_use) + 1)
                    pe.wait_ge(e_done, n + 1)
                    for j in (2 * i, 2 * i + 1):
                        last = nc.tensor.matmul(psO[j * SLOT:(j + 1) * SLOT, 0:S],
                                                VA[0:kn[kt], par, kt, 4 * g + j, :], P[0:kn[kt], (g * STEPS + s) % 8, j % 2, :],
                                                start=(kt == 0), stop=(kt == KT - 1), skip_group_check=True)
                    last.then_inc(pv_done, 1)

                def end(b, be, G, u):
                    if u[0] == "FG":
                        pe.wait_ge(ot_ready, G + 1)
                        begin(b, u)
                        for t in range(QT):
                            last = nc.tensor.transpose(M(u)[:, t * 128:t * 128 + 128], oT[:, t * 128:t * 128 + 128], ident[:])
                        last.then_inc(full(u), 1)
                    elif u[0] == "EO":
                        pe.wait_ge(free(("FG", 0)), order.no(b, ("FG", 0)) + 1)
                        begin(b, u)
                        for t in range(QT):
                            last = nc.tensor.transpose(M(u)[:, t * 128:t * 128 + 128], O[:, t, :], ident[:])
                        last.then_inc(full(u), 1)
                    elif u[0] == "EW":
                        pe.wait_ge(free(("EO",)), order.no(b, ("EO",)) + 1)
                        begin(b, u)
                        for t in range(QT):
                            last = nc.tensor.matmul(M(u)[:, t * 128:t * 128 + 128], OT[:, t * 128:t * 128 + 128], wo[:],
                                                    start=True, stop=True, skip_group_check=True)
                        last.then_inc(full(u), 1)

                def unit(b, it, par, u, g):
                    if u[0] == "A":
                        far = g >= 2
                        scores(b * 4 + g + 2, (g + 2) % 4, 1 - par if far else par, u[2], b if far else b - 1)
                    elif u[0] == "MT":
                        max_rows(b, b * 4 + g + 1, u)
                    elif u[0] in ("FG", "EO", "EW"):
                        end(b, b - 1, b * 4 + g - 1, u)
                    elif u[0] not in NO_BANK:
                        setup(b, b + 1, it + par, 1 - par, u)

                for u in prologue:
                    setup(-1, 0, 0, 0, u)
                for ch in range(CA):
                    scores(0, 0, 0, ch, -1)
                max_rows(-1, 0, ("MT", 3))
                for ch in range(CA):
                    scores(1, 1, 0, ch, -1)

                def body(b, it, par, first, last):
                    for g in range(NG):
                        us = units(g, first, last)
                        for s in range(STEPS):
                            scoresT(b, b * 4 + g, g, par, s)
                            if s >= LAG:
                                weigh(b, b * 4 + g, g, par, s - LAG)
                            elif g:
                                weigh(b, b * 4 + g - 1, g - 1, par, STEPS - LAG + s)
                            elif not first:
                                weigh(b - 1, b * 4 - 1, 3, 1 - par, STEPS - LAG + s)
                            for u in share(us, s):
                                unit(b, it, par, u, g)

                over_batches(pe, body)
                for s in range(STEPS - LAG, STEPS):
                    weigh(NB - 1, NB * 4 - 1, 3, 1, s)
                for u in post:
                    end(NB, NB - 1, NB * 4 - 1, u)

            @block.scalar
            def _(act):
                def take(b, u):
                    act.wait_ge(full(u), order.no(b, u) + 1)

                def exps(G, g, s):
                    n, kt = G * STEPS + s, s // 2
                    act.wait_ge(t_full, n + 1)
                    if due(n - 7):
                        act.wait_ge(pv_done, n - 7)
                    nc.scalar.activation(P[0:kn[kt], (g * STEPS + s) % 8].rearrange("p j q -> p (j q)"), psB[0:kn[kt], s % 2],
                                         ACT.Exp, scale=SCALE).then_inc(e_done, 1)

                def copy_out(b, G, g):
                    if due(G * STEPS):
                        act.wait_ge(pv_done, G * STEPS)
                    if not (isinstance(b, int) and b == 0 and g == 1):
                        act.wait_ge(full(("FG", (g - 1) % 4)), order.no(b if g else b - 1, ("FG", (g - 1) % 4)) + 1)
                    nc.scalar.activation(oT[:], psO[:, 0:S], ACT.Copy).then_inc(ot_ready, 1)

                def unit(b, be, G, u):
                    if u[0] == "X":
                        take(b, u)
                        if chunked:
                            nc.scalar.activation(xT[:].rearrange("d (j g t) -> d g j t", j=HG, g=NG),
                                                 M(u)[:, 0:S].rearrange("d (g j t) -> d g j t", j=HG, g=NG),
                                                 ACT.Copy).then_inc(free(u), 1)
                        else:
                            nc.scalar.activation(xT[:], M(u)[:, 0:S], ACT.Copy).then_inc(free(u), 1)
                    elif u[0] == "C":
                        take(b, u)
                        a, z = kcuts[u[1]], kcuts[u[1] + 1]
                        nc.scalar.activation(cT[:, 0, a:z], M(u)[:, 0:z - a], ACT.Copy).then_inc(ch_ready, 1)
                    elif u[0] == "K" and cross:
                        take(b, u)
                        a, z = kcuts[u[2]], kcuts[u[2] + 1]
                        n = raw_no(b, u)
                        if due(n - 1):
                            act.wait_ge(op_ready, n - 1)
                        nc.scalar.activation(raw[:, u[2] % 2, 0:z - a], M(u)[:, 0:z - a], ACT.Identity, bias=bk[:, u[1]:u[1] + 1])
                        nc.scalar.activation(hi[:, u[2] % 2, 0:z - a], M(u)[:, 0:z - a], ACT.Identity, scale=lo[:, 0:1],
                                             bias=lob[:, u[1]:u[1] + 1]).then_inc(free(u), 1)
                    elif u[0] == "T":
                        take(b, u)
                        nc.scalar.activation(VA[:, parity[0], u[1]].rearrange("k h s -> k (h s)"), M(u),
                                             ACT.Copy).then_inc(free(u), 1)
                    elif u[0] == "EO":
                        take(b, u)
                        nc.scalar.activation(OT[:], M(u)[:, 0:S], ACT.Copy).then_inc(free(u), 1)

                parity = [0]
                for u in prologue:
                    unit(-1, 0, 0, u)

                def body(b, it, par, first, last):
                    parity[0] = 1 - par
                    for g in range(NG):
                        us = units(g, first, last)
                        for s in range(STEPS):
                            exps(b * 4 + g, g, s)
                            if s == LAG - 1 and not (first and g == 0):
                                copy_out(b, b * 4 + g, g)
                            for u in share(us, s):
                                unit(b, b - 1, b * 4 + g - 1, u)

                over_batches(act, body)
                copy_out(NB, NB * 4, 0)
                for u in post:
                    unit(NB, NB - 1, NB * 4 - 1, u)

            @block.gpsimd
            def _(pool):
                def split(b, par, u):
                    if cross:
                        pool.wait_ge(free(u), order.no(b, u) + 1)
                        a, z = kcuts[u[2]], kcuts[u[2] + 1]
                        nc.gpsimd.tensor_tensor(KO[:, par, u[1], a:z], raw[:, u[2] % 2, 0:z - a], hi[:, u[2] % 2, 0:z - a],
                                                ALU.subtract).then_inc(op_ready, 1)
                        return
                    pool.wait_ge(raw_ready, raw_no(b, u) + 1)
                    isk = u[0] == "K"
                    slot = (2 * u[1] + isk) % 2 if rope else u[1] % 2
                    if rope:
                        x, hi_ = rot[:, slot, 2], hi[:, 0, 0:S]
                        nc.gpsimd.tensor_tensor(x, rot[:, slot, 0], rot[:, slot, 1], ALU.add)
                        pool.drain()
                        low = lo[:, 0:1] if isk else lo[:, 1:2]
                        nc.gpsimd.tensor_tensor(hi_, x, low.to_broadcast(list(x.shape)), ALU.mult)
                        pool.drain()
                    else:
                        x, hi_ = xs[:, slot], hi[:, slot]
                    if rope and isk:
                        nc.gpsimd.tensor_tensor(KO[:, par, u[1], :], x, hi_, ALU.subtract)
                    elif rope:
                        if not (isinstance(b, int) and b == -1):
                            pool.wait_ge(q_ld[u[1]], (b + 1) * 64)
                        nc.gpsimd.tensor_tensor(QC[:, u[1], :], x, hi_, ALU.subtract)
                        pool.drain().then_inc(qc_ready, 1)
                    else:
                        cs, cgt = slice(8 * u[1], 8 * u[1] + 8), "r (c g t) -> r c g t"
                        x_, h_ = x.rearrange(cgt, c=8, g=NG), hi_.rearrange(cgt, c=8, g=NG)
                        if isk:
                            nc.gpsimd.tensor_tensor(KO[:, par].rearrange("r g (t c) -> r c g t", c=16)[:, cs], x_, h_, ALU.subtract)
                        else:
                            if not (isinstance(b, int) and b == -1) and u[1] == 0:
                                pool.wait_ge(q_ld[0], (b + 1) * 64)
                            nc.gpsimd.tensor_tensor(QC[:].rearrange("r g (t c) -> r c g t", c=16)[:, cs], x_, h_, ALU.subtract)
                            pool.drain().then_inc(qc_ready, 1)
                    pool.drain().then_inc(op_ready, 1)

                def root(n):
                    pool.wait_ge(ve_ready, n)
                    nc.gpsimd.tensor_tensor(rstd[:], ve[:], minus_half[:, 0:QT], ALU.pow).then_inc(rstd_ready, 1)

                def splits(b, par, g):
                    for u in setups[g]:
                        if u[0] == "K" or u[0] == "Q" and not cross:
                            split(b, par, u)

                for g in range(NG):
                    splits(-1, 0, g)

                def body(b, it, par, first, last):
                    for g in range(NG):
                        if g == 3 and not first:
                            root(b)
                        if not last:
                            splits(b, 1 - par, g)
                over_batches(pool, body)
                root(NB)

            @block.vector
            def _(dve):
                def take(b, u):
                    dve.wait_ge(full(u), order.no(b, u) + 1)

                def setup(b, par, u):
                    if u[0] == "Q" and not chunked or u[0] == "K" and rope:
                        take(b, u)
                        g, isk = u[1], u[0] == "K"
                        if rope:
                            bias, biass = (bk, bks) if isk else (bq, bqs)
                            n, slot = raw_no(b, u), int(isk)
                            if due(n - 1):
                                dve.wait_ge(op_ready, n - 1)
                            nc.vector.scalar_tensor_tensor(out=rot[:, slot, 0], in0=M(u)[:, 0:S], scalar=bias[:, g:g + 1], in1=cos[:],
                                                           op0=ALU.add, op1=ALU.mult)
                            nc.vector.scalar_tensor_tensor(out=rot[:, slot, 1], in0=M(u)[:, S:2 * S], scalar=biass[:, g:g + 1],
                                                           in1=sin[:], op0=ALU.add, op1=ALU.mult).then_inc(free(u), 1)
                            dve.drain().then_inc(raw_ready, 1)
                        else:
                            nc.vector.tensor_scalar(hi2[:, 0:S], M(u)[:, 0:S], bq[:, g:g + 1], lo[:, 1:2], ALU.add, ALU.mult)
                            dve.drain()
                            if not (isinstance(b, int) and b == -1):
                                dve.wait_ge(q_ld[g], (b + 1) * 64)
                            nc.vector.scalar_tensor_tensor(out=QC[:, g, :], in0=M(u)[:, 0:S], scalar=bq[:, g:g + 1],
                                                           in1=hi2[:, 0:S], op0=ALU.add, op1=ALU.subtract).then_inc(free(u), 1)
                            dve.drain().then_inc(qc_ready, 1)
                    elif u[0] == "C":
                        take(b, u)
                        dve.wait_ge(ch_ready, (b + 1) * 4 + u[1] + 1)
                        a, z = kcuts[u[1]], kcuts[u[1] + 1]
                        nc.vector.tensor_tensor(cT[:, 1, a:z], M(u)[:, 0:z - a], cT[:, 0, a:z], ALU.subtract).then_inc(free(u), 1)
                    elif u[0] in "QKV" and chunked:
                        take(b, u)
                        bias = {"Q": bq, "K": bk, "V": bv}[u[0]]
                        cs = slice(8 * u[1], 8 * u[1] + 8)
                        b_ = bias[:, cs].unsqueeze(2).to_broadcast([128, 8, 64])
                        if u[0] == "V":
                            nc.vector.tensor_tensor(VT[:].rearrange("r g (t c) -> r c g t", c=16)[:, cs],
                                                    M(u).rearrange("r (c g t) -> r c g t", c=8, g=NG),
                                                    bias[:, cs].unsqueeze(2).unsqueeze(3).to_broadcast([128, 8, NG, 16]),
                                                    ALU.add).then_inc(free(u), 1)
                            dve.drain().then_inc(vt_ready, 1)
                        else:
                            n = raw_no(b, u)
                            if due(n - 1):
                                dve.wait_ge(op_ready, n - 1)
                            nc.vector.tensor_tensor(xs[:, u[1]].rearrange("r (c q) -> r c q", c=8),
                                                    M(u).rearrange("r (c q) -> r c q", c=8), b_, ALU.add).then_inc(free(u), 1)
                            dve.drain()
                            col = 0 if u[0] == "K" else 1
                            nc.vector.tensor_scalar(hi[:, u[1]], xs[:, u[1]], lo[:, col:col + 1], None, ALU.mult)
                            dve.drain().then_inc(raw_ready, 1)
                    elif u[0] == "V" and not chunked:
                        take(b, u)
                        if rope:
                            nc.vector.tensor_tensor(VA[:, par].rearrange("k t h s -> k (t h) s")[:, :, 0:DH],
                                                    M(u)[:, 0:QT * 128].rearrange("k (a s) -> k a s", s=DH),
                                                    bv[:].rearrange("k (a s) -> k a s", s=DH), ALU.add).then_inc(free(u), 1)
                        else:
                            ks = range(4 * u[1], min(4 * u[1] + 4, KT))
                            n, r = len(ks), kn[ks[-1]]
                            nc.vector.tensor_tensor(
                                VA[0:r, par, ks[0]:ks[-1] + 1].rearrange("k t h s -> k (t h) s")[:, :, 0:DH],
                                M(u)[0:r, 0:n * 128].rearrange("k (a s) -> k a s", s=DH),
                                bv[0:r, 0:n * 128].rearrange("k (a s) -> k a s", s=DH), ALU.add).then_inc(free(u), 1)

                def maxima(G, ch):
                    n = G * CA + ch
                    if ch == 0:
                        if due(G):
                            dve.wait_ge(mx_ready, G)
                    dve.wait_ge(s_full, n + 1)
                    if cross:
                        j, t, k = ch // 8, ch // 4 % 2, ch % 4
                        nc.vector.tensor_reduce(mpart[:, t, j, k:k + 1], psA[:, ch % AB, 0:cuts[k + 1] - cuts[k]],
                                                AX.X, ALU.max).then_inc(s_free, 1)
                    else:
                        nc.vector.tensor_reduce(mfull[:, :, ch], psA[:, ch % AB].rearrange("p (t k) -> p t k", t=QT),
                                                AX.X, ALU.max).then_inc(s_free, 1)
                    if ch == CA - 1:
                        if cross:
                            dve.drain()
                            nc.vector.tensor_reduce(mfull[:], mpart[:], AX.X, ALU.max)
                        cols = MX[:].rearrange("p t (j s) -> p t j s", s=SLOT)
                        dve.drain()
                        nc.vector.tensor_scalar(cols[:, :, :, M_ROW], mfull[:], -1.0, None, ALU.mult)
                        dve.drain()
                        nc.vector.scalar_tensor_tensor(out=cols[:, :, :, M_ROW + 1], in0=mfull[:], scalar=-1.0,
                                                       in1=cols[:, :, :, M_ROW], op0=ALU.mult,
                                                       op1=ALU.subtract).then_inc(mx_ready, 1)

                def add_max(b, g, par, u):
                    take(b, u)
                    for j in range(HG):
                        r = slice(j * SLOT, (j + 1) * SLOT)
                        nc.vector.tensor_tensor(QZ[r, par, 4 * g + j, :], M(u)[r, 0:S // 2].bitcast(F16),
                                                QZ[r, par, 4 * g + j, :], ALU.add)
                    dve.drain().then_inc(free(u), 1)

                def end(b, be, G, gg, it, par, u):
                    if u[0] == "FG":
                        take(b, u)
                        rows = M(u)[:, 0:S].rearrange("p (t j s) -> p t j s", t=QT, j=HG)
                        nc.vector.reciprocal(rsum[:], rows[:, :, :, DH])
                        dve.drain()
                        for t in range(QT):
                            last = nc.vector.tensor_tensor(
                                O[:, t, gg * 32:gg * 32 + 32].rearrange("p (j d) -> p j d", j=HG), rows[:, t, :, 0:DH],
                                rsum[:, t, :].unsqueeze(2).to_broadcast([128, HG, DH]), ALU.mult)
                        dve.drain().then_inc(free(u), 1)
                    elif u[0] in ("EW", "EL"):
                        dve.wait_ge(xr_ld[par], it * 16 + 16)
                        if u[0] == "EW":
                            take(b, u)
                            nc.vector.tensor_tensor(y[:], M(u)[:, 0:S].rearrange("p (t d) -> p t d", t=QT), bo[:], ALU.add)
                            dve.drain().then_inc(free(u), 1)
                            nc.vector.tensor_tensor(y[:], y[:], x_res[:, par], ALU.add)
                        else:
                            nc.vector.tensor_tensor(y[:], O[:], x_res[:, par], ALU.add)
                        dve.drain().then_inc(xr_used, 1)
                        layer_norm_stats(nc, dve, y, stats, mv, ve).then_inc(ve_ready, 1)
                    elif u[0] == "EN":
                        dve.wait_ge(rstd_ready, be + 1)
                        if due(it * 16):
                            dve.wait_ge(st_done[par], it * 16)
                        for t in range(QT):
                            nc.vector.tensor_scalar(x_out[:, par, t, :], y[:, t, :], mv[:, t, 0:1], rstd[:, t:t + 1],
                                                    ALU.subtract, ALU.mult)
                        dve.drain().then_inc(y_ready, 1)

                hi2 = sb("hi2", [128, S], F16) if cross else None
                for u in prologue:
                    setup(-1, 0, u)
                for ch in range(CA):
                    maxima(0, ch)
                add_max(-1, 0, 0, ("MT", 3))
                for ch in range(CA):
                    maxima(1, ch)

                def body(b, it, par, first, last):
                    for g in range(NG):
                        for u in delayed(units(g, first, last)):
                            if u[0] == "A":
                                maxima(b * 4 + g + 2, u[2])
                            elif u[0] == "MT":
                                add_max(b, (g + 1) % 4, 1 - par if g == 3 else par, u)
                            elif u[0] in ("FG", "EW", "EL", "EN"):
                                end(b, b - 1, b * 4 + g - 1, (g - 1) % 4, it - 1 + par, 1 - par, u)
                            elif u[0] != "EO":
                                setup(b, 1 - par, u)

                over_batches(dve, body)
                for u in post:
                    end(NB, NB - 1, NB * 4 - 1, 3, NB // 2 - 1, 1, u)


def cross64(nc, x_src, x_dst, w, ident, ident16, minus_half, ctx):
    NK, DQ, NP, HB = NKC, 64, 8, 2
    KT = -(-NK // 128)
    kn = [min(128, NK - 128 * k) for k in range(KT)]
    LAG = 2
    SCALE = float(DQ) ** -0.5
    cuts = [NK * c // 4 for c in range(5)]
    CA = HB * QT * 4
    kcuts = list(range(0, NK, BANK)) + [NK]
    PARTS = ((0, 0), (0, 1), (1, 0))
    AB, MB = 2, 3
    back = [AB if i >= AB else CA - max(j for j in range(CA) if j % AB == i) + i for i in range(CA)]
    VS = [[0, 4, 7, 10, 13], [0, 5, 9, 13]]

    xc = [("X",)] + [("C", i) for i in range(4)]
    kq = [[("Q", p)] + [("K", p, c) for c in range(4)] for p in range(NP)]
    v1 = [[("V", 1, k) for k in range(VS[0][i], VS[0][i + 1])] for i in range(4)]
    v0 = [[("V", 0, k) for k in range(VS[1][i], VS[1][i + 1])] for i in range(3)]
    ends = [[], [("EW",)], [], [("EN",)], [("FT",)], [("FW",)], [], [("FN",)]]
    NO_BANK = ("EN", "FN", "A", "C2")

    def units(p, first, last):
        u = [] if first else list(ends[p])
        u += xc if p == 5 and not last else []
        values = v1[p] if p < 4 else v0[p - 5] if p >= 5 and not last else []
        u += mixed(values, [] if last and p >= 5 else kq[(p + 3) % 8])
        if not (first and p == 0):
            u.insert(len(u) // 2, ("FG", p))
        if not (last and p == 7):
            u[2:2] = [("MT", p)]
            for i in range(4):
                u[3 + 3 * i:3 + 3 * i] = [("C2", p, i)]
        return spread(u, [] if last and p >= 6 else [("A", p, c) for c in range(CA)])

    def bank_uses(us):
        return [u for u in us if u[0] not in NO_BANK]

    def of_body(first, last):
        return bank_uses([u for p in range(NP) for u in units(p, first, last)])

    prologue = xc + kq[0] + kq[1] + kq[2] + v0[0] + v0[1] + v0[2]
    post = [("FG", 0)] + [u for e in ends for u in e]
    order = UseOrder(MB, prologue + [("MT", 7)], of_body(True, False), of_body(False, False), of_body(False, True), bank_uses(post))

    def over(eng, body):
        body(0, True, False)
        with eng.Fori(1, NB - 1) as b:
            body(b, False, False)
        body(NB - 1, False, True)

    def share(us, k):
        n = len(us)
        return us[n * k // KT:n * (k + 1) // KT]

    with ExitStack() as cx:
        def sb(name, shape, dt=F32):
            return cx.enter_context(nc.sbuf_tensor(f"wide_{name}", shape, dt))

        def psum(name, shape):
            return cx.enter_context(nc.psum_tensor(f"wide_{name}", [128] + shape, F32))

        def sem(name):
            return cx.enter_context(nc.semaphore(f"wide_{name}"))

        def loaded(name, src):
            t = sb(name, list(src.shape))
            loads.append((t, src))
            return t

        loads = []
        wq, wk, wv, wo, bo, wf, dd = (loaded(n, w[n]) for n in ("wq", "wk", "wv", "wo", "bo", "wf", "dd"))
        psA, psB = psum("scores", [AB, BANK]), psum("scoresT", [2, BANK])
        psO, psM = psum("weighed", [BANK]), psum("shared", [MB, BANK])
        x_in = sb("x_in", [128, QT, 128])
        x_res = sb("x_res", [128, QT, 128])
        x_out = sb("x_out", [128, QT, 128])
        x1 = sb("x1", [128, QT, 128])
        x1T = sb("x1T", [128, S])
        xT = sb("xT", [128, S])
        ctx_in = sb("ctx_in", [128, KT, 128])
        cT = sb("cT", [128, 2, NK], F16)
        wkp, wvp = sb("wk_parts", [128, 2, H * DQ], F16), sb("wv_parts", [128, 2, H * DQ], F16)
        V = sb("V", [128, KT, H * DQ])
        K1 = sb("K1", [128, 4, HB, NK], F16)
        K2 = sb("K2", [128, 2, HB, NK], F16)
        Q1 = sb("Q1", [128, 4, HB, S], F16)
        Q2 = sb("Q2", [128, 4, HB, S], F16)
        qh = sb("qh", [128, S], F16)
        P = sb("P", [128, 8, HB, S])
        acc = sb("acc", [128, 2, HB * S])
        MX = sb("MX", [128, QT, 128], F16)
        mpart = sb("mpart", [128, QT, HB, 4])
        mfull = sb("mfull", [128, QT, HB])
        ones = sb("ones", [128, DQ])
        oT = sb("oT", [128, S])
        rsum = sb("rsum", [128, S])
        ON = sb("ON", [128, NP, S])
        y = sb("y", [128, QT, 128])
        stats = sb("stats", [128, QT, 6])
        mv = sb("mv", [128, QT, 2])
        ve = sb("ve", [128, QT])
        rstd = sb("rstd", [128, QT])

        w_ld, started = sem("weights_loaded"), sem("started")
        x_ld, xr_ld, c_ld, st_done = sem("x_loaded"), sem("residual_loaded"), sem("context_loaded"), sem("stored")
        m_full, m_free = [sem(f"bank_full{i}") for i in range(MB)], [sem(f"bank_free{i}") for i in range(MB)]
        s_full, s_free = sem("scores_full"), sem("scores_maxed")
        t_full, e_done, pv_done = sem("scoresT_full"), sem("exp_done"), sem("pv_done")
        p_summed = sem("p_summed")
        ch_ready = sem("context_high_ready")
        mx_ready, hi_ready, ot_ready, k2_ready = sem("max_ready"), sem("high_ready"), sem("oT_ready"), sem("k2_ready")
        x1_ready = sem("x1_ready")
        xr_used, ve_ready, rstd_ready, y_ready = sem("residual_used"), sem("var_ready"), sem("rstd_ready"), sem("out_ready")

        def M(use):
            return psM[:, order.bank(use)]

        def full(use):
            return m_full[order.bank(use)]

        def free(use):
            return m_free[order.bank(use)]

        def load(sp, b):
            sp.dma_start(x_in[:], tokens(x_src, b)).then_inc(x_ld, 16)
            src = ctx[bass.ds(b, 1)]
            full_rows = (KT - 1) * 128
            sp.dma_start(ctx_in[:, 0:KT - 1, :], src[:, 0:full_rows].rearrange("o (k p) d -> p (o k) d", p=128)).then_inc(c_ld, 16)
            sp.dma_start(ctx_in[0:kn[-1], KT - 1, :], src[:, full_rows:NK].rearrange("o p d -> p (o d)")).then_inc(c_ld, 16)

        def load_res(sp, b):
            sp.dma_start(x_res[:], tokens(x_src, b)).then_inc(xr_ld, 16)

        with nc.Block() as block:
            @block.sync
            def _(sp):
                for t, src in loads:
                    sp.dma_start(t[:], src).then_inc(w_ld, 16)
                load(sp, 0)
                load_res(sp, 0)
                sp.wait_ge(w_ld, 16 * len(loads))

            @block.gpsimd
            def _(pool):
                nc.gpsimd.memset(Q2[:], 0.0)
                nc.gpsimd.memset(K2[:], 0.0)
                pool.drain()
                nc.gpsimd.memset(K2[DQ:DQ + 2, :, 0, :], 1.0)
                nc.gpsimd.memset(K2[0:2, :, 1, :], 1.0)

            @block.vector
            def _(dve):
                nc.vector.memset(MX[:], 0.0)
                nc.vector.memset(ones[:], 1.0)
                dve.wait_ge(w_ld, 16 * len(loads))
                for m, parts in ((wk, wkp), (wv, wvp)):
                    nc.vector.tensor_copy(parts[:, 0], m[:])
                dve.drain()
                for m, parts in ((wk, wkp), (wv, wvp)):
                    nc.vector.tensor_tensor(parts[:, 1], m[:], parts[:, 0], ALU.subtract)
                dve.drain().then_inc(started, 1)

        with nc.Block() as block:
            @block.sync
            def _(sp):
                def store(b):
                    sp.wait_ge(y_ready, b + 1)
                    sp.dma_start(tokens(x_dst, b), x_out[:]).then_inc(st_done, 16)

                def body(b, first, last):
                    if not last:
                        sp.wait_ge(free(("C", 3)), order.no(b - 1, ("C", 3)) + 1)
                        load(sp, b + 1)
                    if not first:
                        if due(b):
                            sp.wait_ge(xr_used, b)
                        load_res(sp, b)
                        store(b - 1)

                over(sp, body)
                store(NB - 1)
                sp.wait_ge(st_done, 16 * NB)

            @block.tensor
            def _(pe):
                def begin(b, u):
                    if due(order.no(b, u)):
                        pe.wait_ge(free(u), order.no(b, u))

                def setup(b, bs, u):
                    begin(b, u)
                    if u[0] == "X":
                        pe.wait_ge(x_ld, bs * 16 + 16)
                        for t in range(QT):
                            last = nc.tensor.transpose(M(u)[:, t * 128:t * 128 + 128], x_in[:, t, :], ident[:])
                    elif u[0] == "C":
                        if u[1] == 0:
                            pe.wait_ge(c_ld, bs * 32 + 32)
                        for i, k in enumerate(range(4 * u[1], min(4 * u[1] + 4, KT))):
                            last = nc.tensor.transpose(M(u)[:, i * 128:i * 128 + kn[k]], ctx_in[0:kn[k], k, :],
                                                       ident[0:kn[k], 0:kn[k]])
                    elif u[0] == "Q":
                        if u[1] == 0:
                            pe.wait_ge(free(("X",)), order.no(b, ("X",)) + 1)
                        last = nc.tensor.matmul(M(u)[:, 0:S], wq[:, u[1] * 128:u[1] * 128 + 128], xT[:],
                                                start=True, stop=True, skip_group_check=True)
                    elif u[0] == "K":
                        a, z = kcuts[u[2]], kcuts[u[2] + 1]
                        if u[1] == 0:
                            pe.wait_ge(free(("C", u[2])), order.no(b, ("C", u[2])) + 1)
                        for wp, cp in PARTS:
                            last = nc.tensor.matmul(M(u)[:, 0:z - a], wkp[:, wp, u[1] * 128:u[1] * 128 + 128], cT[:, cp, a:z],
                                                    start=(wp == cp), stop=(wp == 1), skip_group_check=True)
                    elif u[0] == "V":
                        k = u[2]
                        if u[1] == 0:
                            pe.wait_ge(free(("C", k // 4)), order.no(b, ("C", k // 4)) + 1)
                        for wp, cp in PARTS:
                            last = nc.tensor.matmul(M(u)[0:kn[k], :], cT[:, cp, k * 128:k * 128 + kn[k]],
                                                    wvp[:, wp, u[1] * 512:u[1] * 512 + 512],
                                                    start=(wp == cp), stop=(wp == 1), skip_group_check=True)
                    last.then_inc(full(u), 1)

                def scores(G, p, ch, at, use):
                    n = G * CA + ch
                    if ch == 0:
                        pe.wait_ge(free(use), order.no(at, use) + 1)
                    if due(n + 1 - back[ch]):
                        pe.wait_ge(s_free, n + 1 - back[ch])
                    i, t, k = ch // 8, ch // 4 % 2, ch % 4
                    a, z = cuts[k], cuts[k + 1]
                    nc.tensor.matmul(psA[:, ch % AB, 0:z - a], Q1[:, p % 4, i, t * 128:t * 128 + 128], K1[:, p % 4, i, a:z],
                                     start=True, stop=True, skip_group_check=True).then_inc(s_full, 1)

                def max_rows(b, G, u):
                    pe.wait_ge(mx_ready, G + 1)
                    begin(b, u)
                    for t in range(QT):
                        last = nc.tensor.transpose(M(u)[:, t * 64:t * 64 + 64].bitcast(F16), MX[:, t, :], ident16[:])
                    last.then_inc(full(u), 1)

                def scoresT(b, G, p, k):
                    n = G * KT + k
                    if k == 0:
                        pe.wait_ge(free(("MT", (p - 1) % 8)), order.no(b if p else b - 1, ("MT", (p - 1) % 8)) + 1)
                        pe.wait_ge(k2_ready, G * 4 + 4)
                    if due(n - 1):
                        pe.wait_ge(e_done, n - 1)
                    ks = slice(k * 128, k * 128 + kn[k])
                    for i in range(HB):
                        out = psB[0:kn[k], (p * KT + k) % 2, i * S:i * S + S]
                        nc.tensor.matmul(out, K1[:, p % 4, i, ks], Q1[:, p % 4, i, :], start=True, stop=False, skip_group_check=True)
                        last = nc.tensor.matmul(out, K2[:, p % 2, i, ks], Q2[:, p % 4, i, :], start=False, stop=True,
                                                skip_group_check=True)
                    last.then_inc(t_full, 1)

                def weigh(b, G, p, k):
                    if k == 0:
                        if due(G):
                            pe.wait_ge(ot_ready, G)
                        if p in (0, 4):
                            v_use = ("V", p // 4, KT - 1)
                            pe.wait_ge(free(v_use), order.no(b if p else b - 1, v_use) + 1)
                    pe.wait_ge(e_done, G * KT + k + 1)
                    pe.wait_ge(started, 1)
                    for i in range(HB):
                        last = nc.tensor.matmul(psO[i * DQ:(i + 1) * DQ, 0:S], V[0:kn[k], k, (2 * p + i) * DQ:(2 * p + i + 1) * DQ],
                                                P[0:kn[k], (p * KT + k) % 8, i, :], start=(k == 0), stop=(k == KT - 1),
                                                skip_group_check=True)
                    last.then_inc(pv_done, 1)

                def end(b, G, u):
                    if u[0] == "FG":
                        pe.wait_ge(p_summed, G * KT + KT)
                        begin(b, u)
                        pe.wait_ge(started, 1)
                        for i in range(HB):
                            last = nc.tensor.matmul(M(u)[i * DQ:(i + 1) * DQ, 0:S], ones[:], acc[:, (u[1] - 1) % 2, i * S:i * S + S],
                                                    start=True, stop=True, skip_group_check=True)
                        last.then_inc(full(u), 1)
                    elif u[0] == "EW":
                        pe.wait_ge(free(("FG", 0)), order.no(b, ("FG", 0)) + 1)
                        begin(b, u)
                        for t in range(QT):
                            for p in range(NP):
                                last = nc.tensor.matmul(M(u)[:, t * 128:t * 128 + 128], ON[:, p, t * 128:t * 128 + 128], wo[:, p, :],
                                                        start=(p == 0), stop=(p == NP - 1), skip_group_check=True)
                        last.then_inc(full(u), 1)
                    elif u[0] == "FT":
                        if due(b):
                            pe.wait_ge(x1_ready, b)
                        begin(b, u)
                        for t in range(QT):
                            last = nc.tensor.transpose(M(u)[:, t * 128:t * 128 + 128], x1[:, t, :], ident[:])
                        last.then_inc(full(u), 1)
                    elif u[0] == "FW":
                        pe.wait_ge(free(("FT",)), order.no(b, ("FT",)) + 1)
                        begin(b, u)
                        for t in range(QT):
                            for m in (wf, dd):
                                last = nc.tensor.matmul(M(u)[:, t * 128:t * 128 + 128], x1T[:, t * 128:t * 128 + 128], m[:],
                                                        start=(m is wf), stop=(m is dd), skip_group_check=True)
                        last.then_inc(full(u), 1)

                def unit(b, p, u):
                    if u[0] == "A":
                        q = (p + 2) % 8
                        at = b if p else b - 1
                        scores(b * 8 + p + 2, q, u[2], at, ("K", q, 3))
                    elif u[0] == "MT":
                        max_rows(b, b * 8 + p + 1, u)
                    elif u[0] in ("FG", "EW", "FT", "FW"):
                        end(b, b * 8 + p - 1, u)
                    elif u[0] not in NO_BANK:
                        setup(b, b + 1 if u[0] in "XC" else 0, u)

                for u in prologue:
                    setup(-1, 0, u)
                for ch in range(CA):
                    scores(0, 0, ch, -1, ("K", 0, 3))
                max_rows(-1, 0, ("MT", 7))
                for ch in range(CA):
                    scores(1, 1, ch, -1, ("K", 1, 3))

                def body(b, first, last):
                    for p in range(NP):
                        us = units(p, first, last)
                        for k in range(KT):
                            scoresT(b, b * 8 + p, p, k)
                            if k >= LAG:
                                weigh(b, b * 8 + p, p, k - LAG)
                            elif not (first and p == 0):
                                weigh(b if p else b - 1, b * 8 + p - 1, (p - 1) % 8, KT - LAG + k)
                            for u in share(us, k):
                                unit(b, p, u)

                over(pe, body)
                for k in range(KT - LAG, KT):
                    weigh(NB - 1, NB * 8 - 1, 7, k)
                for u in post:
                    end(NB, NB * 8 - 1, u)

            @block.scalar
            def _(act):
                def take(b, u):
                    act.wait_ge(full(u), order.no(b, u) + 1)

                def exps(G, p, k):
                    n = G * KT + k
                    act.wait_ge(t_full, n + 1)
                    if due(n - 7):
                        act.wait_ge(pv_done, n - 7)
                    if due(n - 7):
                        act.wait_ge(p_summed, n - 7)
                    nc.scalar.activation(P[0:kn[k], (p * KT + k) % 8].rearrange("k i q -> k (i q)"), psB[0:kn[k], (p * KT + k) % 2],
                                         ACT.Exp, scale=SCALE).then_inc(e_done, 1)

                def copy_out(b, G, p):
                    if due(G * KT):
                        act.wait_ge(pv_done, G * KT)
                    if not (isinstance(b, int) and b == 0 and p == 1):
                        act.wait_ge(free(("FG", (p - 1) % 8)), order.no(b if p else b - 1, ("FG", (p - 1) % 8)) + 1)
                    nc.scalar.activation(oT[:], psO[:, 0:S], ACT.Copy).then_inc(ot_ready, 1)

                def copy_high(G, p, c):
                    if due((G - 1) * KT):
                        act.wait_ge(t_full, (G - 1) * KT)
                    a, z = kcuts[c], kcuts[c + 1]
                    for i in range(HB):
                        r = slice(i * DQ, (i + 1) * DQ)
                        last = nc.scalar.activation(K2[r, p % 2, i, a:z], K1[r, p % 4, i, a:z], ACT.Copy)
                    last.then_inc(k2_ready, 1)

                def unit(b, u):
                    if u[0] == "X":
                        take(b, u)
                        nc.scalar.activation(xT[:], M(u)[:, 0:S], ACT.Copy).then_inc(free(u), 1)
                    elif u[0] == "FT":
                        take(b, u)
                        nc.scalar.activation(x1T[:], M(u)[:, 0:S], ACT.Copy).then_inc(free(u), 1)
                    elif u[0] == "C":
                        take(b, u)
                        a, z = kcuts[u[1]], kcuts[u[1] + 1]
                        nc.scalar.activation(cT[:, 0, a:z], M(u)[:, 0:z - a], ACT.Copy).then_inc(ch_ready, 1)
                    elif u[0] == "K":
                        take(b, u)
                        a, z = kcuts[u[2]], kcuts[u[2] + 1]
                        for i in range(HB):
                            r = slice(i * DQ, (i + 1) * DQ)
                            last = nc.scalar.activation(K1[r, u[1] % 4, i, a:z], M(u)[r, 0:z - a], ACT.Copy)
                        act.drain().then_inc(hi_ready, 1)
                    elif u[0] == "V":
                        take(b, u)
                        k = u[2]
                        nc.scalar.activation(V[0:kn[k], k, u[1] * 512:u[1] * 512 + 512], M(u)[0:kn[k], :], ACT.Copy).then_inc(free(u), 1)

                for u in prologue:
                    unit(-1, u)
                for c in range(4):
                    copy_high(0, 0, c)

                def body(b, first, last):
                    for p in range(NP):
                        us = units(p, first, last)
                        for k in range(KT):
                            exps(b * 8 + p, p, k)
                            if k == LAG - 1 and not (first and p == 0):
                                copy_out(b, b * 8 + p, p)
                            for u in share(us, k):
                                if u[0] == "C2":
                                    copy_high(b * 8 + p + 1, (p + 1) % 8, u[2])
                                else:
                                    unit(b, u)

                over(act, body)
                copy_out(NB, NB * 8, 0)
                for u in post:
                    unit(NB, u)

            @block.gpsimd
            def _(pool):
                def sums(b, G, p, k):
                    pool.wait_ge(e_done, G * KT + k + 1)
                    out, r = acc[:, p % 2, :], p * KT + k

                    def tile(r):
                        return P[:, r % 8].rearrange("k i q -> k (i q)")
                    if k == 1:
                        if not (isinstance(b, int) and b == 0 and p < 2):
                            use = ("FG", (p - 1) % 8)
                            pool.wait_ge(full(use), order.no(b if p >= 1 else b - 1, use) + 1)
                        nc.gpsimd.tensor_tensor(out, tile(r - 1), tile(r), ALU.add).then_inc(p_summed, 2)
                    else:
                        pool.wait_ge(p_summed, G * KT + k)
                        nc.gpsimd.tensor_tensor(out[0:kn[k]], out[0:kn[k]], tile(r)[0:kn[k]], ALU.add).then_inc(p_summed, 1)

                def root(n):
                    if due(n):
                        pool.wait_ge(ve_ready, n)
                    nc.gpsimd.tensor_tensor(rstd[:], ve[:], minus_half[:, 0:QT], ALU.pow).then_inc(rstd_ready, 1)

                def body(b, first, last):
                    for p in range(NP):
                        if not first and p == 2:
                            root(b * 2 - 1)
                        if not first and p == 6:
                            root(b * 2)
                        for k in range(1, KT):
                            sums(b, b * 8 + p, p, k)

                over(pool, body)
                root(NB * 2 - 1)
                root(NB * 2)

            @block.vector
            def _(dve):
                def take(b, u):
                    dve.wait_ge(full(u), order.no(b, u) + 1)

                def hi_no(bs, u):
                    return bs * 32 + u[1] * 4 + u[2] + 1

                def setup(b, bs, u):
                    if u[0] == "Q":
                        take(b, u)
                        p = u[1]
                        nc.vector.tensor_copy(qh[:], M(u)[:, 0:S])
                        dve.drain()
                        for i in range(HB):
                            r, o = slice(i * DQ, (i + 1) * DQ), slice((1 - i) * DQ, (2 - i) * DQ)
                            nc.vector.tensor_tensor(Q2[r, p % 4, i, :], M(u)[r, 0:S], qh[r, :], ALU.subtract)
                            nc.vector.tensor_copy(Q1[r, p % 4, i, :], qh[r, :])
                            nc.vector.tensor_copy(Q1[o, p % 4, i, :], qh[r, :])
                        dve.drain().then_inc(free(u), 1)
                    elif u[0] == "C":
                        take(b, u)
                        a, z = kcuts[u[1]], kcuts[u[1] + 1]
                        dve.wait_ge(ch_ready, bs * 4 + u[1] + 1)
                        nc.vector.tensor_tensor(cT[:, 1, a:z], M(u)[:, 0:z - a], cT[:, 0, a:z], ALU.subtract).then_inc(free(u), 1)
                    elif u[0] == "K":
                        take(b, u)
                        if due(hi_no(bs, u)):
                            dve.wait_ge(hi_ready, hi_no(bs, u))
                        a, z = kcuts[u[2]], kcuts[u[2] + 1]
                        for i in range(HB):
                            r, o = slice(i * DQ, (i + 1) * DQ), slice((1 - i) * DQ, (2 - i) * DQ)
                            nc.vector.tensor_tensor(K1[o, u[1] % 4, i, a:z], M(u)[r, 0:z - a], K1[r, u[1] % 4, i, a:z], ALU.subtract)
                        dve.drain().then_inc(free(u), 1)

                def maxima(G, ch):
                    n = G * CA + ch
                    if ch == 0:
                        if due(G):
                            dve.wait_ge(mx_ready, G)
                    dve.wait_ge(s_full, n + 1)
                    i, t, k = ch // 8, ch // 4 % 2, ch % 4
                    nc.vector.tensor_reduce(mpart[:, t, 1 - i, k:k + 1], psA[:, ch % AB, 0:cuts[k + 1] - cuts[k]],
                                            AX.X, ALU.max).then_inc(s_free, 1)
                    if ch == CA - 1:
                        dve.drain()
                        nc.vector.tensor_reduce(mfull[:], mpart[:], AX.X, ALU.max)
                        cols = MX[:].rearrange("p t (i s) -> p t i s", s=DQ)
                        dve.drain()
                        nc.vector.tensor_scalar(cols[:, :, :, 0], mfull[:], -1.0, None, ALU.mult)
                        dve.drain()
                        nc.vector.scalar_tensor_tensor(out=cols[:, :, :, 1], in0=mfull[:], scalar=-1.0, in1=cols[:, :, :, 0],
                                                       op0=ALU.mult, op1=ALU.subtract).then_inc(mx_ready, 1)

                def add_max(b, p, u):
                    take(b, u)
                    for i in range(HB):
                        o = slice((1 - i) * DQ, (2 - i) * DQ)
                        nc.vector.tensor_copy(Q2[o, p % 4, i, :], M(u)[o, 0:S // 2].bitcast(F16))
                    dve.drain().then_inc(free(u), 1)

                def end(b, be, G, gp, u):
                    if u[0] == "FG":
                        dve.wait_ge(ot_ready, G + 1)
                        take(b, u)
                        nc.vector.reciprocal(rsum[:], M(u)[:, 0:S])
                        dve.drain()
                        nc.vector.tensor_tensor(ON[:, gp, :], oT[:], rsum[:], ALU.mult)
                        dve.drain().then_inc(free(u), 1)
                    elif u[0] == "EW":
                        dve.wait_ge(xr_ld, be * 16 + 16)
                        take(b, u)
                        nc.vector.tensor_tensor(y[:], M(u)[:, 0:S].rearrange("p (t d) -> p t d", t=QT), bo[:], ALU.add)
                        dve.drain().then_inc(free(u), 1)
                        nc.vector.tensor_tensor(y[:], y[:], x_res[:], ALU.add)
                        dve.drain().then_inc(xr_used, 1)
                        layer_norm_stats(nc, dve, y, stats, mv, ve).then_inc(ve_ready, 1)
                    elif u[0] == "FW":
                        take(b, u)
                        nc.vector.tensor_tensor(y[:], M(u)[:, 0:S].rearrange("p (t d) -> p t d", t=QT), x1[:], ALU.add)
                        dve.drain().then_inc(free(u), 1)
                        layer_norm_stats(nc, dve, y, stats, mv, ve).then_inc(ve_ready, 1)
                    elif u[0] in ("EN", "FN"):
                        out = x1 if u[0] == "EN" else x_out
                        dve.wait_ge(rstd_ready, be * 2 + (1 if u[0] == "EN" else 2))
                        if u[0] == "FN":
                            if due(be * 16):
                                dve.wait_ge(st_done, be * 16)
                        for t in range(QT):
                            nc.vector.tensor_scalar(out[:, t, :], y[:, t, :], mv[:, t, 0:1], rstd[:, t:t + 1],
                                                    ALU.subtract, ALU.mult)
                        dve.drain().then_inc(x1_ready if u[0] == "EN" else y_ready, 1)

                for u in prologue:
                    setup(-1, 0, u)
                for ch in range(CA):
                    maxima(0, ch)
                add_max(-1, 0, ("MT", 7))
                for ch in range(CA):
                    maxima(1, ch)

                def body(b, first, last):
                    for p in range(NP):
                        for u in delayed(units(p, first, last)):
                            if u[0] == "A":
                                maxima(b * 8 + p + 2, u[2])
                            elif u[0] == "MT":
                                add_max(b, (p + 1) % 8, u)
                            elif u[0] in ("FG", "EW", "EN", "FW", "FN"):
                                end(b, b - 1, b * 8 + p - 1, (p - 1) % 8, u)
                            elif u[0] != "C2":
                                setup(b, b + 1 if p >= 5 else b, u)

                over(dve, body)
                for u in post:
                    end(NB, NB - 1, NB * 8 - 1, 7, u)


def experts(nc, x_src, x_dst, w, ident, minus_half):
    E, F = 8, 512
    FT, TQ = F // 128, 4
    LO = 32
    PARTS = ((0, 0), (1, 0), (0, 1))
    NQ = NB * S // (TQ * 128)
    TT = TQ * 128
    xs = x_src.rearrange("b s d -> (b s) d").rearrange("(q t p) d -> q p t d", t=TQ, p=128)
    xd = x_dst.rearrange("b s d -> (b s) d").rearrange("(q t p) d -> q p t d", t=TQ, p=128)

    def quad(x, q):
        return x[bass.ds(q, 1)].rearrange("o p t d -> p (o t) d")

    with ExitStack() as cx:
        def sb(name, shape, dt=F32):
            return cx.enter_context(nc.sbuf_tensor(f"moe_{name}", shape, dt))

        def psum(name, shape):
            return cx.enter_context(nc.psum_tensor(f"moe_{name}", [128] + shape, F32))

        psA, psB = psum("outs", [2, BANK]), psum("hidden", [2, 2 * BANK])
        psO, psM = psum("gate_rows", [BANK]), psum("shared", [BANK])

        def sem(name):
            return cx.enter_context(nc.semaphore(f"moe_{name}"))

        def loaded(name, src):
            t = sb(name, list(src.shape))
            loads.append((t, src))
            return t

        loads = []
        sw, sbias, rank, w1, b1, w2, b2 = (loaded(n, w[n]) for n in ("sw", "sb", "rank", "w1", "b1", "w2", "b2"))
        pick = sb("pick", [LO + E, E, 128], F16)
        loads.append((pick, w["pick"]))
        x_in = sb("x_in", [128, 2, TQ, 128])
        x_out = sb("x_out", [128, 2, TQ, 128])
        xT = sb("xT", [128, TT])
        w1p, w2p = sb("w1_parts", [128, 2, E, F], F16), sb("w2_parts", [128, 2, E, FT, 128], F16)
        xp = sb("x_parts", [128, 2, 2, TT], F16)
        hp = sb("hidden_parts", [128, 2, 2, FT, TT], F16)
        NT = NQ * TQ
        lg = sb("logits", [128, NT, E])
        ex = sb("exps", [128, NT, E])
        sel = sb("selected", [128, NT, E])
        gates = sb("gates", [128, NT, E])
        top = sb("top", [128, NT])
        den = sb("den", [128, NT])
        gq = sb("gq", [128, TQ, E])
        gT = sb("gT", [LO + E, TT], F16)
        gB = sb("gB", [128, 2, TT])
        hT = sb("hT", [128, 2, FT, TT])
        tmp = sb("tmp", [128, TT])
        accT = sb("accT", [128, TT])
        accS = sb("accS", [128, TT])
        y = sb("y", [128, TQ, 128])
        stats = sb("stats", [128, TQ, 6])
        mv = sb("mv", [128, TQ, 2])
        ve = sb("ve", [128, TQ])
        rstd = sb("rstd", [128, TQ])

        w_ld, r_ld = sem("weights_loaded"), sem("router_x_loaded")
        x_ld = [sem(f"x_loaded{i}") for i in range(2)]
        st_done = [sem(f"stored{i}") for i in range(2)]
        r_full, r_T, r_lg, r_free = sem("router_T_full"), sem("router_T_copied"), sem("router_logits_full"), sem("router_logits_read")
        d_ready, ex_ready = sem("shifted_ready"), sem("exps_ready")
        m_full, m_free, gq_ready = sem("bank_full"), sem("bank_free"), sem("gates_ready")
        xh_ready, gh_ready, hh_done = sem("x_high_ready"), sem("gates_high_ready"), sem("hidden_high_done")
        hl_pool, hl_dve = sem("hidden_low_by_pool"), sem("hidden_low_by_dve")
        h_full, h_done, y_full, y_used = sem("hidden_full"), sem("hidden_done"), sem("y_full"), sem("y_used")
        g_full, g_done, acc_ready = sem("gate_rows_full"), sem("gate_rows_done"), sem("sum_ready")
        x_used, ve_ready, rstd_ready, out_ready = sem("x_used"), sem("var_ready"), sem("rstd_ready"), sem("out_ready")

        with nc.Block() as block:
            @block.sync
            def _(sp):
                for t, src in loads:
                    sp.dma_start(t[:], src).then_inc(w_ld, 16)
                sp.wait_ge(w_ld, 16 * len(loads))

            @block.scalar
            def _(act):
                act.wait_ge(w_ld, 16 * len(loads))
                nc.scalar.activation(w1p[:, 0], w1[:], ACT.Copy)
                nc.scalar.activation(w2p[:, 0], w2[:], ACT.Copy)

            @block.vector
            def _(dve):
                nc.vector.memset(gT[:], 0.0)

        with nc.Block() as block:
            @block.sync
            def _(sp):
                def load(q):
                    sp.dma_start(x_in[:, 0], quad(xs, q)).then_inc(r_ld, 16)
                load(0)
                with sp.Fori(1, NQ) as q:
                    if due(q):
                        sp.wait_ge(r_full, q)
                    load(q)

            @block.tensor
            def _(pe):
                def body(q):
                    pe.wait_ge(r_ld, q * 16 + 16)
                    if due(q):
                        pe.wait_ge(r_T, q)
                    for t in range(TQ):
                        last = nc.tensor.transpose(psM[:, t * 128:t * 128 + 128], x_in[:, 0, t, :], ident[:])
                    last.then_inc(r_full, 1)
                    pe.wait_ge(r_T, q + 1)
                    if due(q):
                        pe.wait_ge(r_free, q)
                    for t in range(TQ):
                        last = nc.tensor.matmul(psO[:, t * E:t * E + E], xT[:, t * 128:t * 128 + 128], sw[:],
                                                start=True, stop=True, skip_group_check=True)
                    last.then_inc(r_lg, 1)
                body(0)
                with pe.Fori(1, NQ) as q:
                    body(q)

            @block.scalar
            def _(act):
                def body(q):
                    act.wait_ge(r_full, q + 1)
                    if due(q):
                        act.wait_ge(r_lg, q)
                    nc.scalar.activation(xT[:], psM[:], ACT.Copy).then_inc(r_T, 1)
                body(0)
                with act.Fori(1, NQ) as q:
                    body(q)
                act.wait_ge(d_ready, 1)
                nc.scalar.activation(ex[:], ex[:], ACT.Exp).then_inc(ex_ready, 1)

            @block.gpsimd
            def _(pool):
                nc.gpsimd.tensor_tensor(w2p[:, 1], w2[:], w2p[:, 0], ALU.subtract)

            @block.vector
            def _(dve):
                nc.vector.tensor_tensor(w1p[:, 1], w1[:], w1p[:, 0], ALU.subtract)

                def body(q):
                    dve.wait_ge(r_lg, q + 1)
                    nc.vector.tensor_tensor(lg[:, bass.ds(q * TQ, TQ), :], psO[:, 0:TQ * E].rearrange("p (t e) -> p t e", e=E),
                                            sbias[:], ALU.add).then_inc(r_free, 1)
                body(0)
                with dve.Fori(1, NQ) as q:
                    body(q)

                def wide(v):
                    return v[:].unsqueeze(2).to_broadcast([128, NT, E])
                dve.wait_ge(r_free, NQ)
                nc.vector.tensor_reduce(top[:], lg[:], AX.X, ALU.max)
                dve.drain()
                nc.vector.tensor_tensor(ex[:], lg[:], wide(top), ALU.subtract)
                nc.vector.tensor_tensor(sel[:], lg[:], wide(top), ALU.is_ge)
                dve.drain().then_inc(d_ready, 1)
                nc.vector.tensor_tensor(sel[:], sel[:], rank[:], ALU.mult)
                dve.drain()
                nc.vector.tensor_reduce(top[:], sel[:], AX.X, ALU.max)
                dve.drain()
                nc.vector.tensor_tensor(sel[:], sel[:], wide(top), ALU.is_equal)
                dve.wait_ge(ex_ready, 1)
                nc.vector.tensor_reduce(den[:], ex[:], AX.X, ALU.add)
                dve.drain()
                nc.vector.reciprocal(den[:], den[:])
                dve.drain()
                nc.vector.tensor_tensor(gates[:], sel[:], wide(den), ALU.mult)

        prologue = ["X", "GT"]
        body_uses = ["EO", "X", "GT"]

        def no(q, use):
            if isinstance(q, int):
                if q == -1:
                    return prologue.index(use)
                if q == 0:
                    return 2 + ["X", "GT"].index(use)
                if q == NQ - 1 or q == NQ:
                    return 4 + 3 * (NQ - 2) + (q - NQ + 1)
            return q * 3 + (1 + body_uses.index(use))

        def over(eng, body):
            body(0, 0, 0, True, False)
            body(1, 0, 1, False, False)
            with eng.Fori(1, NQ // 2 - 1) as i:
                for par in range(2):
                    body(i * 2 + par, i, par, False, False)
            body(NQ - 2, NQ // 2 - 1, 0, False, False)
            body(NQ - 1, NQ // 2 - 1, 1, False, True)

        with nc.Block() as block:
            @block.sync
            def _(sp):
                def load(q, par):
                    sp.dma_start(x_in[:, par], quad(xs, q)).then_inc(x_ld[par], 16)

                def store(q, par):
                    sp.wait_ge(out_ready, q + 1)
                    sp.dma_start(quad(xd, q), x_out[:, par]).then_inc(st_done[par], 16)
                load(0, 0)
                load(1, 1)

                def body(q, i, par, first, last):
                    if not first:
                        if not last:
                            if due(q):
                                sp.wait_ge(x_used, q)
                            load(q + 1, 1 - par)
                        store(q - 1, 1 - par)
                over(sp, body)
                store(NQ - 1, 1)
                sp.wait_ge(st_done[0], 16 * NQ // 2)
                sp.wait_ge(st_done[1], 16 * NQ // 2)

            @block.tensor
            def _(pe):
                def turn_x(q, par, its):
                    pe.wait_ge(x_ld[par], its * 16 + 16)
                    if due(no(q, "X")):
                        pe.wait_ge(m_free, no(q, "X"))
                    for t in range(TQ):
                        last = nc.tensor.transpose(psM[:, t * 128:t * 128 + 128], x_in[:, par, t, :], ident[:])
                    last.then_inc(m_full, 1)

                def turn_gates(q):
                    pe.wait_ge(gq_ready, q + 2)
                    if due(no(q, "GT")):
                        pe.wait_ge(m_free, no(q, "GT"))
                    for t in range(TQ):
                        last = nc.tensor.transpose(psM[0:E, t * 128:t * 128 + 128], gq[:, t, :], ident[:])
                    last.then_inc(m_full, 1)

                def turn_back(q):
                    if due(q):
                        pe.wait_ge(acc_ready, q)
                    if due(no(q, "EO")):
                        pe.wait_ge(m_free, no(q, "EO"))
                    for t in range(TQ):
                        last = nc.tensor.transpose(psM[:, t * 128:t * 128 + 128], accS[:, t * 128:t * 128 + 128], ident[:])
                    last.then_inc(m_full, 1)

                def hidden(q, par, e):
                    n = q * E + e
                    if e == 0:
                        pe.wait_ge(m_free, no(q - 1, "GT") + 1)
                    for f in range(FT):
                        if due(n * FT + f - 3):
                            pe.wait_ge(h_done, n * FT + f - 3)
                        for wp, other in PARTS:
                            last = nc.tensor.matmul(psB[:, f // 2, f % 2 * BANK:(f % 2 + 1) * BANK],
                                                    w1p[:, wp, e, f * 128:f * 128 + 128], xp[:, par, other],
                                                    start=(wp == other), stop=(other == 1), skip_group_check=True)
                        last.then_inc(h_full, 1)
                    if due(n):
                        pe.wait_ge(g_done, n)
                    nc.tensor.matmul(psO[:], pick[:, e, :], gT[:], start=True, stop=True, skip_group_check=True).then_inc(g_full, 1)

                def out(n, e):
                    if due(n - 1):
                        pe.wait_ge(y_used, n - 1)
                    pe.wait_ge(hh_done, n * FT + FT)
                    for wp, other in PARTS:
                        for f in range(FT):
                            if other == 1 and f < FT - 1:
                                pe.wait_ge(hl_pool, n * (FT - 1) + f + 1)
                            elif other == 1:
                                pe.wait_ge(hl_dve, n + 1)
                            last = nc.tensor.matmul(psA[:, e % 2], w2p[:, wp, e, f, :], hp[:, e % 2, other, f, :],
                                                    start=(wp == other and f == 0), stop=(other == 1 and f == FT - 1),
                                                    skip_group_check=True)
                    last.then_inc(y_full, 1)

                turn_x(-1, 0, 0)
                turn_gates(-1)

                def body(q, i, par, first, last):
                    for e in range(E):
                        hidden(q, par, e)
                        if not (first and e == 0):
                            out(q * E + e - 1, (e - 1) % E)
                        if e == 2 and not first:
                            turn_back(q)
                        if e == 5 and not last:
                            turn_x(q, 1 - par, i + par)
                        if e == 7 and not last:
                            turn_gates(q)
                over(pe, body)
                out(NQ * E - 1, E - 1)
                turn_back(NQ)

            @block.scalar
            def _(act):
                def copy_x(q, par):
                    act.wait_ge(m_full, no(q, "X") + 1)
                    nc.scalar.activation(xp[:, par, 0], psM[:], ACT.Copy).then_inc(xh_ready, 1)

                def copy_gates(q):
                    act.wait_ge(m_full, no(q, "GT") + 1)
                    if due((q + 1) * E):
                        act.wait_ge(g_full, (q + 1) * E)
                    nc.scalar.activation(gT[0:E], psM[0:E, :], ACT.Copy).then_inc(gh_ready, 1)

                def high(n, e, f):
                    act.wait_ge(h_done, n * FT + f + 1)
                    nc.scalar.activation(hp[:, e % 2, 0, f, :], hT[:, e % 2, f, :], ACT.Copy).then_inc(hh_done, 1)

                copy_x(-1, 0)
                copy_gates(-1)

                def body(q, i, par, first, last):
                    for e in range(E):
                        n = q * E + e
                        for f in range(FT):
                            act.wait_ge(h_full, n * FT + f + 1)
                            if f == 0:
                                if due(n - 1):
                                    act.wait_ge(y_full, n - 1)
                            nc.scalar.activation(hT[:, e % 2, f, :], psB[:, f // 2, f % 2 * BANK:(f % 2 + 1) * BANK],
                                                 ACT.Gelu_apprx_tanh, bias=b1[:, e, f:f + 1]).then_inc(h_done, 1)
                            if f:
                                high(n, e, f - 1)
                        act.wait_ge(g_full, n + 1)
                        if due(n - 1):
                            act.wait_ge(y_used, n - 1)
                        nc.scalar.activation(gB[:, e % 2], psO[:], ACT.Copy).then_inc(g_done, 1)
                        high(n, e, FT - 1)
                        if e == 5 and not last:
                            copy_x(q, 1 - par)
                        if e == 7 and not last:
                            copy_gates(q)
                over(act, body)

            @block.gpsimd
            def _(pool):
                def root(q):
                    pool.wait_ge(ve_ready, q)
                    nc.gpsimd.tensor_tensor(rstd[:], ve[:], minus_half[:, 0:TQ], ALU.pow).then_inc(rstd_ready, 1)

                def body(q, i, par, first, last):
                    for e in range(E):
                        for f in range(FT - 1):
                            pool.wait_ge(hh_done, (q * E + e) * FT + f + 1)
                            nc.gpsimd.tensor_tensor(hp[:, e % 2, 1, f, :], hT[:, e % 2, f, :], hp[:, e % 2, 0, f, :],
                                                    ALU.subtract).then_inc(hl_pool, 1)
                        if e == 3 and not first:
                            root(q)
                over(pool, body)
                root(NQ)

            @block.vector
            def _(dve):
                def take_gates(q):
                    if due(q + 1):
                        dve.wait_ge(m_full, no(q - 1, "GT") + 1)
                    nc.vector.tensor_copy(gq[:], gates[:, bass.ds((q + 1) * TQ, TQ), :]).then_inc(gq_ready, 1)

                def gate(n, e):
                    dve.wait_ge(g_done, n + 1)
                    dve.wait_ge(y_full, n + 1)
                    if e == 0:
                        nc.vector.scalar_tensor_tensor(out=accT[:], in0=psA[:, e % 2], scalar=b2[:, e:e + 1], in1=gB[:, e % 2],
                                                       op0=ALU.add, op1=ALU.mult)
                        dve.drain().then_inc(y_used, 1)
                    else:
                        nc.vector.scalar_tensor_tensor(out=tmp[:], in0=psA[:, e % 2], scalar=b2[:, e:e + 1], in1=gB[:, e % 2],
                                                       op0=ALU.add, op1=ALU.mult)
                        dve.drain().then_inc(y_used, 1)
                        nc.vector.tensor_tensor(accS[:] if e == E - 1 else accT[:], accT[:], tmp[:], ALU.add)
                        dve.drain()

                def finish(q, qe, par, its):
                    dve.wait_ge(m_full, no(q, "EO") + 1)
                    nc.vector.tensor_tensor(y[:], psM[:].rearrange("p (t d) -> p t d", t=TQ), x_in[:, par], ALU.add)
                    dve.drain().then_inc(m_free, 1)
                    for t in range(TQ):
                        nc.vector.bn_stats(stats[:, t, :], y[:, t, :])
                    dve.drain().then_inc(x_used, 1)
                    for t in range(TQ):
                        nc.vector.bn_aggr(mv[:, t, :], stats[:, t, :])
                    dve.drain()
                    nc.vector.tensor_scalar(ve[:], mv[:, :, 1], EPS, None, ALU.add).then_inc(ve_ready, 1)

                def normalise(qe, par, its):
                    dve.wait_ge(rstd_ready, qe + 1)
                    if due(its * 16):
                        dve.wait_ge(st_done[par], its * 16)
                    for t in range(TQ):
                        nc.vector.tensor_scalar(x_out[:, par, t, :], y[:, t, :], mv[:, t, 0:1], rstd[:, t:t + 1],
                                                ALU.subtract, ALU.mult)
                    dve.drain().then_inc(out_ready, 1)

                def low(n, e):
                    dve.wait_ge(hh_done, n * FT + FT)
                    nc.vector.tensor_tensor(hp[:, e % 2, 1, FT - 1, :], hT[:, e % 2, FT - 1, :], hp[:, e % 2, 0, FT - 1, :],
                                            ALU.subtract).then_inc(hl_dve, 1)

                def low_x(q, par):
                    dve.wait_ge(xh_ready, q + 2)
                    nc.vector.tensor_tensor(xp[:, par, 1], psM[:], xp[:, par, 0], ALU.subtract).then_inc(m_free, 1)

                def low_gates(q):
                    dve.wait_ge(gh_ready, q + 2)
                    nc.vector.tensor_tensor(gT[LO:LO + E], psM[0:E, :], gT[0:E], ALU.subtract).then_inc(m_free, 1)

                take_gates(-1)
                low_x(-1, 0)
                low_gates(-1)

                def body(q, i, par, first, last):
                    for e in range(E):
                        if not (first and e == 0):
                            gate(q * E + e - 1, (e - 1) % E)
                        if e == 0 and not first:
                            dve.drain().then_inc(acc_ready, 1)
                        if e == 2 and not first:
                            finish(q, q - 1, 1 - par, i - 1 + par)
                        low(q * E + e, e)
                        if e == 5 and not last:
                            low_x(q, 1 - par)
                        if e == 7 and not last:
                            low_gates(q)
                        if e == 4 and not first:
                            normalise(q - 1, 1 - par, i - 1 + par)
                        if e == 6 and not last:
                            take_gates(q)
                over(dve, body)
                gate(NQ * E - 1, E - 1)
                dve.drain().then_inc(acc_ready, 1)
                finish(NQ, NQ - 1, 1, NQ // 2 - 1)
                normalise(NQ - 1, 1, NQ // 2 - 1)


def decoder(nc, ins, out):
    with ExitStack() as c:
        ident = c.enter_context(nc.sbuf_tensor("identity", [128, 128], F32))
        ident16 = c.enter_context(nc.sbuf_tensor("identity16", [128, 128], F16))
        minus_half = c.enter_context(nc.sbuf_tensor("minus_half", [128, 4], F32))
        const_ld = c.enter_context(nc.semaphore("constants_loaded"))
        between = [nc.dram_tensor(f"x_after_{n}", (NB, S, D), F32, kind="Internal").ap() for n in ("rope", "wide", "chunked", "cross")]

        def of(part):
            return {k[len(part) + 1:]: v for k, v in ins.items() if k.startswith(part + "_")}

        with nc.Block() as block:
            @block.sync
            def _(sp):
                sp.dma_start(ident[:], ins["ident"]).then_inc(const_ld, 16)
                sp.dma_start(ident16[:], ins["ident16"]).then_inc(const_ld, 16)
                sp.wait_ge(const_ld, 32)

            @block.gpsimd
            def _(pool):
                nc.gpsimd.memset(minus_half[:], -0.5)

        attention8(nc, "rope", ins["x"], between[0], of("rope"), ident, ident16, minus_half)
        cross64(nc, between[0], between[1], of("wide"), ident, ident16, minus_half, ins["ctx"])
        attention8(nc, "chunked", between[1], between[2], of("chunked"), ident, ident16, minus_half)
        attention8(nc, "cross", between[2], between[3], of("cross"), ident, ident16, minus_half, ctx=ins["ctx"])
        experts(nc, between[3], out, of("moe"), ident, minus_half)


def head_columns(w, swap=False):
    w = np.asarray(w).reshape(D, H, DH)
    if swap:
        w = w.reshape(D, H, DH // 2, 2)[..., ::-1].reshape(D, H, DH)
    out = np.zeros((D, H, SLOT), np.float32)
    for s in range(3):
        out[:, :, DH * s:DH * s + DH] = w
    return out.reshape(D, H * SLOT)


def head_bias(b, shift_rows, swap=False):
    b = np.asarray(b).reshape(H, DH)
    if swap:
        b = b.reshape(H, DH // 2, 2)[..., ::-1].reshape(H, DH)
    out = np.zeros((H, SLOT), np.float32)
    for s in range(3):
        out[:, DH * s:DH * s + DH] = b
    out[:, M_ROW:M_ROW + 2] = shift_rows
    return np.ascontiguousarray(out.reshape(NG, HG * SLOT).T)


def low_rows():
    out = np.zeros((HG, SLOT, 2), np.float32)
    out[:, DH:2 * DH, 0] = 1
    out[:, 2 * DH:3 * DH, 1] = 1
    return out.reshape(128, 2)


def rope_tables():
    inv = (np.float32(1.0) / np.float32(10000.0) ** (np.arange(0, DH, 2, dtype=np.float32) / np.float32(DH))).astype(np.float32)
    freqs = np.arange(S, dtype=np.float32)[:, None] * inv[None, :]
    angle = np.concatenate([freqs, freqs], -1)[:, ::2]
    cos, sin = np.zeros((HG, SLOT, S), np.float32), np.zeros((HG, SLOT, S), np.float32)
    for s in range(3):
        for d in range(DH):
            cos[:, DH * s + d] = np.cos(angle[:, d // 2])
            sin[:, DH * s + d] = np.sin(angle[:, d // 2]) * (-1 if d % 2 == 0 else 1)
    cos[:, M_ROW:M_ROW + 2] = 1
    return cos.reshape(128, S), sin.reshape(128, S)


def chunk_columns(w, part):
    w = np.asarray(w).reshape(16, 3, DH, D)[:, part].transpose(2, 0, 1)
    out = np.zeros((D, 16, SLOT), np.float32)
    for s in range(3 if part < 2 else 1):
        out[:, :, DH * s:DH * s + DH] = w
    return out.reshape(D, 16 * SLOT)


def chunk_bias(b, part):
    b = np.asarray(b).reshape(16, 3, DH)[:, part].T
    out = np.zeros((HG, SLOT, 16), np.float32)
    for s in range(3 if part < 2 else 1):
        out[:, DH * s:DH * s + DH, :] = b
    if part == 1:
        out[:, M_ROW:M_ROW + 2] = 1
    if part == 2:
        out[:, DH] = 1
    return out.reshape(128, 16)


def on_rows(b, n):
    b = np.asarray(b).reshape(1, 1, -1)
    return np.ascontiguousarray(np.broadcast_to(b, (128, n, b.size)))


def flat_rows(b, n):
    return on_rows(b, n).reshape(128, -1)


def turned(w):
    return np.ascontiguousarray(np.asarray(w).T)


def laid_out(i):
    out = {"x": np.asarray(i["x"]), "ctx": np.asarray(i["ctx_1024"]),
           "ident": np.eye(128, dtype=np.float32), "ident16": np.eye(128, dtype=np.float16)}
    cos, sin = rope_tables()
    a = "L0_attn_"
    out |= {"rope_wq": head_columns(i[a + "Wq"]), "rope_wqs": head_columns(i[a + "Wq"], True),
            "rope_wk": head_columns(i[a + "Wk"]), "rope_wks": head_columns(i[a + "Wk"], True),
            "rope_bq": head_bias(i[a + "bq"], 0), "rope_bqs": head_bias(i[a + "bq"], 0, True),
            "rope_bk": head_bias(i[a + "bk"], 1), "rope_bks": head_bias(i[a + "bk"], 0, True),
            "rope_cos": cos, "rope_sin": sin, "rope_wv": np.asarray(i[a + "Wv"]), "rope_bv": flat_rows(i[a + "bv"], QT),
            "rope_lo": low_rows(), "rope_wo": np.asarray(i[a + "Wo"]), "rope_bo": on_rows(i[a + "bo"], QT)}
    a = "L0_xattn_"
    dd = np.asarray(i["L0_ffn_disha"])
    out |= {"wide_wq": np.asarray(i[a + "Wq"]), "wide_wk": np.asarray(i[a + "Wk"]), "wide_wv": np.asarray(i[a + "Wv"]),
            "wide_wo": np.ascontiguousarray(np.asarray(i[a + "Wo"]).reshape(8, 128, D).transpose(1, 0, 2)),
            "wide_bo": on_rows(i[a + "bo"], QT), "wide_wf": turned(i["L0_ffn_weight"]), "wide_dd": np.concatenate([dd, dd])}
    a = "L1_attn_"
    for n, name in enumerate("qkv"):
        out |= {f"chunked_w{name}": chunk_columns(i[a + "W_qkv"], n), f"chunked_b{name}": chunk_bias(i[a + "b_qkv"], n)}
    out |= {"chunked_lo": low_rows(), "chunked_wo": turned(i[a + "W_out"]), "chunked_bo": on_rows(i[a + "b_out"], QT)}
    a = "L1_xattn_"
    out |= {"cross_wq": head_columns(turned(i[a + "Wq"])), "cross_wk": head_columns(turned(i[a + "Wk"])),
            "cross_bq": head_bias(i[a + "bq"], 0), "cross_bk": head_bias(i[a + "bk"], 1),
            "cross_wv": turned(i[a + "Wv"]), "cross_bv": flat_rows(i[a + "bv"], 4), "cross_lo": low_rows()}
    a = "L1_ffn_"
    pick = np.zeros((40, 8, 128), np.float16)
    for e in range(8):
        pick[e, e] = pick[32 + e, e] = 1
    out |= {"moe_sw": np.asarray(i[a + "switch_w"]), "moe_sb": on_rows(i[a + "switch_b"], 4),
            "moe_rank": on_rows(np.arange(8, 0, -1).astype(np.float32), NB * QT), "moe_pick": pick,
            "moe_w1": np.ascontiguousarray(np.asarray(i[a + "w1"]).transpose(1, 0, 2)),
            "moe_b1": np.ascontiguousarray(np.asarray(i[a + "b1"]).reshape(8, 4, 128).transpose(2, 0, 1)),
            "moe_w2": np.ascontiguousarray(np.asarray(i[a + "w2"]).reshape(8, 4, 128, D).transpose(2, 0, 1, 3)),
            "moe_b2": turned(i[a + "b2"])}
    return out


def kernel(**inputs):
    import concourse.bacc as bacc
    from concourse.bass_utils import run_bass_kernel_spmd

    nc = bacc.Bacc("TRN2", target_bir_lowering=False, num_devices=1)
    arrays = laid_out(inputs)
    ins = {k: nc.dram_tensor(f"in_{k}", v.shape, mybir.dt.from_np(v.dtype), kind="ExternalInput").ap() for k, v in arrays.items()}
    out = nc.dram_tensor("out", (NB, S, D), F32, kind="ExternalOutput").ap()
    decoder(nc, ins, out)
    r = run_bass_kernel_spmd(nc, [{f"in_{k}": v for k, v in arrays.items()}], core_ids=[0])
    return r.results[0]["out"]
```
